# Optimizing a Trainium2 kernel written in Bass

```python
import numpy as np
import jax
import jax.numpy as jnp

def _softmax(x, axis=-1):
    return jax.nn.softmax(x, axis=axis)

def _gelu(x):
    return jax.nn.gelu(x, approximate=True)

def _silu(x):
    return jax.nn.silu(x)

def _sigmoid(x):
    return jax.nn.sigmoid(x)

def _layernorm(x, axis=-1, eps=1e-05):
    m = jnp.mean(x, axis=axis, keepdims=True)
    v = jnp.var(x, axis=axis, keepdims=True)
    return (x - m) / jnp.sqrt(v + eps)

def _scatter_add(tgt, idx, src, axis=0):
    return tgt.at[idx].add(src)

def _segment_sum(src, seg, n):
    return jax.ops.segment_sum(src, seg, n)
kernel_name = 'mk_seq_postln_d1_jaxref_r4_443c07'

def setup_inputs(seed: int=0):
    np.random.seed(seed)
    _w = jnp.asarray

    def _L0_attn_setup():
        import jax, jax.numpy as jnp
        import numpy as np
        B, S, D, H = (2, 1024, 256, 16)
        HD = D // H
        KCONV = 4

        def _rmsnorm(x, scale, eps=1e-06):
            return x * jax.lax.rsqrt(jnp.mean(x * x, axis=-1, keepdims=True) + eps) * scale

        def _l2norm(x, eps=1e-06):
            return x * jax.lax.rsqrt(jnp.sum(x * x, axis=-1, keepdims=True) + eps)

        def _causal_dwconv_silu(x, w):
            k = w.shape[1]
            s = x.shape[1]
            xp = jnp.pad(x, ((0, 0), (k - 1, 0), (0, 0)))
            out = sum((xp[:, i:i + s, :] * w[:, i] for i in range(k)))
            return jax.nn.silu(out)

        def _p20_scan(x, decay_log, theta):
            b, s, d = x.shape
            xc = x.reshape(b, s, d // 2, 2)
            u = jax.lax.complex(xc[..., 0], xc[..., 1])
            a = jnp.exp(-jnp.exp(decay_log)) * jnp.exp(1j * theta)

            def step(carry, u_t):
                st = carry * a + u_t
                return (st, st)
            _, ys = jax.lax.scan(step, jnp.zeros((b, d // 2), u.dtype), jnp.swapaxes(u, 0, 1))
            ys = jnp.swapaxes(ys, 0, 1)
            return jnp.stack([ys.real, ys.imag], axis=-1).reshape(b, s, d)

        def _gated_delta_rule(q, k, v, g, beta):
            scale = q.shape[-1] ** (-0.5)
            q = _l2norm(q)
            k = _l2norm(k)
            qt, kt, vt = (jnp.moveaxis(t, 1, 0) for t in (q, k, v))
            gt, bt = (jnp.moveaxis(t, 1, 0) for t in (g, beta))
            s0 = jnp.zeros((q.shape[0], q.shape[2], q.shape[3], v.shape[3]), v.dtype)

            def step(state, inp):
                q_t, k_t, v_t, g_t, b_t = inp
                state = state * jnp.exp(g_t)[..., None, None]
                v_err = (v_t - jnp.einsum('bhkv,bhk->bhv', state, k_t)) * b_t[..., None]
                state = state + jnp.einsum('bhk,bhv->bhkv', k_t, v_err)
                o_t = jnp.einsum('bhkv,bhk->bhv', state, q_t) * scale
                return (state, o_t)
            _, o = jax.lax.scan(step, s0, (qt, kt, vt, gt, bt))
            return jnp.moveaxis(o, 0, 1)
        key = jax.random.key(seed)
        ks = jax.random.split(key, 16)
        w = lambda k, shp, s=0.02: jax.random.normal(k, shp, jnp.float32) * s
        ctrl_out = 3 * D + 2 * H + D
        ctrl_b = jnp.concatenate([jnp.zeros((3 * D,), jnp.float32), jnp.full((H,), 1.5, jnp.float32), jnp.full((H,), -2.0, jnp.float32), jnp.full((D,), -1.5, jnp.float32)])

        def conv_w(k):
            base = jnp.zeros((D, KCONV), jnp.float32).at[:, -1].set(1.0)
            return base + w(k, (D, KCONV), 0.02)
        return {'hidden': jax.random.normal(ks[0], (B, S, D), jnp.float32), 'p20_decay_log': w(ks[1], (D // 2,), 1.0), 'p20_theta': jax.random.uniform(ks[2], (D // 2,), jnp.float32, 0.0, 2.0 * np.pi), 'ctrl_W': w(ks[3], (D, ctrl_out)), 'ctrl_b': ctrl_b, 'p20c_W': w(ks[4], (D, 3 * D), 0.001), 'qconv_w': conv_w(ks[5]), 'kconv_w': conv_w(ks[6]), 'vconv_w': conv_w(ks[7]), 'mnorm_scale': jnp.ones((HD,), jnp.float32), 'vnorm_scale': jnp.ones((D,), jnp.float32), 'ramp_logit': jnp.full((D,), -4.595, jnp.float32), 'out_W': w(ks[8], (2 * D, D), 0.02), 'out_b': jnp.zeros((D,), jnp.float32)}
    _L0_attn_in = _L0_attn_setup()

    def _L0_ffn_setup():
        import math
        import jax, jax.numpy as jnp
        import numpy as np
        K = 2
        CAP_FACTOR = 1.0
        EPS = 1e-09
        key = jax.random.key(seed)
        ks = jax.random.split(key, 6)
        B, S, D, H, E = (4, 512, 256, 1024, 8)
        x = jax.random.normal(ks[0], (B, S, D), jnp.float32)
        wg = jax.random.normal(ks[1], (D, E), jnp.float32) * 0.02
        w1 = jax.random.normal(ks[2], (E, D, H), jnp.float32) * 0.02
        b1 = jnp.zeros((E, H), jnp.float32)
        w2 = jax.random.normal(ks[3], (E, H, D), jnp.float32) * 0.02
        b2 = jnp.zeros((E, D), jnp.float32)
        return {'x': x, 'wg': wg, 'w1': w1, 'b1': b1, 'w2': w2, 'b2': b2}
    _L0_ffn_in = _L0_ffn_setup()
    _d = {'L0_attn_hidden': _L0_attn_in['hidden'], 'L0_attn_p20_decay_log': _L0_attn_in['p20_decay_log'], 'L0_attn_p20_theta': _L0_attn_in['p20_theta'], 'L0_attn_ctrl_W': _L0_attn_in['ctrl_W'], 'L0_attn_ctrl_b': _L0_attn_in['ctrl_b'], 'L0_attn_p20c_W': _L0_attn_in['p20c_W'], 'L0_attn_qconv_w': _L0_attn_in['qconv_w'], 'L0_attn_kconv_w': _L0_attn_in['kconv_w'], 'L0_attn_vconv_w': _L0_attn_in['vconv_w'], 'L0_attn_mnorm_scale': _L0_attn_in['mnorm_scale'], 'L0_attn_vnorm_scale': _L0_attn_in['vnorm_scale'], 'L0_attn_ramp_logit': _L0_attn_in['ramp_logit'], 'L0_attn_out_W': _L0_attn_in['out_W'], 'L0_attn_out_b': _L0_attn_in['out_b'], 'L0_ffn_wg': _L0_ffn_in['wg'], 'L0_ffn_w1': _L0_ffn_in['w1'], 'L0_ffn_b1': _L0_ffn_in['b1'], 'L0_ffn_w2': _L0_ffn_in['w2'], 'L0_ffn_b2': _L0_ffn_in['b2']}
    _x0 = _d['L0_attn_hidden']
    _d['L0_attn_hidden'] = jax.random.normal(jax.random.fold_in(jax.random.key(seed), 1), (16, 1024, 256), dtype=_x0.dtype)
    del _x0
    return _d

def reference(L0_attn_hidden, L0_attn_p20_decay_log, L0_attn_p20_theta, L0_attn_ctrl_W, L0_attn_ctrl_b, L0_attn_p20c_W, L0_attn_qconv_w, L0_attn_kconv_w, L0_attn_vconv_w, L0_attn_mnorm_scale, L0_attn_vnorm_scale, L0_attn_ramp_logit, L0_attn_out_W, L0_attn_out_b, L0_ffn_wg, L0_ffn_w1, L0_ffn_b1, L0_ffn_w2, L0_ffn_b2):

    def _L0_attn_ref(hidden, p20_decay_log, p20_theta, ctrl_W, ctrl_b, p20c_W, qconv_w, kconv_w, vconv_w, mnorm_scale, vnorm_scale, ramp_logit, out_W, out_b):
        import jax, jax.numpy as jnp
        import numpy as np
        B, S, D, H = (2, 1024, 256, 16)
        HD = D // H
        KCONV = 4

        def _rmsnorm(x, scale, eps=1e-06):
            return x * jax.lax.rsqrt(jnp.mean(x * x, axis=-1, keepdims=True) + eps) * scale

        def _l2norm(x, eps=1e-06):
            return x * jax.lax.rsqrt(jnp.sum(x * x, axis=-1, keepdims=True) + eps)

        def _causal_dwconv_silu(x, w):
            k = w.shape[1]
            s = x.shape[1]
            xp = jnp.pad(x, ((0, 0), (k - 1, 0), (0, 0)))
            out = sum((xp[:, i:i + s, :] * w[:, i] for i in range(k)))
            return jax.nn.silu(out)

        def _p20_scan(x, decay_log, theta):
            b, s, d = x.shape
            xc = x.reshape(b, s, d // 2, 2)
            u = jax.lax.complex(xc[..., 0], xc[..., 1])
            a = jnp.exp(-jnp.exp(decay_log)) * jnp.exp(1j * theta)

            def step(carry, u_t):
                st = carry * a + u_t
                return (st, st)
            _, ys = jax.lax.scan(step, jnp.zeros((b, d // 2), u.dtype), jnp.swapaxes(u, 0, 1))
            ys = jnp.swapaxes(ys, 0, 1)
            return jnp.stack([ys.real, ys.imag], axis=-1).reshape(b, s, d)

        def _gated_delta_rule(q, k, v, g, beta):
            scale = q.shape[-1] ** (-0.5)
            q = _l2norm(q)
            k = _l2norm(k)
            qt, kt, vt = (jnp.moveaxis(t, 1, 0) for t in (q, k, v))
            gt, bt = (jnp.moveaxis(t, 1, 0) for t in (g, beta))
            s0 = jnp.zeros((q.shape[0], q.shape[2], q.shape[3], v.shape[3]), v.dtype)

            def step(state, inp):
                q_t, k_t, v_t, g_t, b_t = inp
                state = state * jnp.exp(g_t)[..., None, None]
                v_err = (v_t - jnp.einsum('bhkv,bhk->bhv', state, k_t)) * b_t[..., None]
                state = state + jnp.einsum('bhk,bhv->bhkv', k_t, v_err)
                o_t = jnp.einsum('bhkv,bhk->bhv', state, q_t) * scale
                return (state, o_t)
            _, o = jax.lax.scan(step, s0, (qt, kt, vt, gt, bt))
            return jnp.moveaxis(o, 0, 1)
        b, s, d = hidden.shape
        p20_read = _p20_scan(hidden, p20_decay_log, p20_theta)
        normed_p20 = _rmsnorm(p20_read, vnorm_scale)
        p20_q, p20_k, p20_v = jnp.split(normed_p20 @ p20c_W, 3, axis=-1)
        ramp = jax.nn.sigmoid(ramp_logit)
        ctrl = hidden @ ctrl_W + ctrl_b
        q_in, k_in, v_in, dec_in, beta_in, gate_in = jnp.split(ctrl, np.cumsum([d, d, d, H, H]).tolist(), axis=-1)
        q_in = _causal_dwconv_silu(q_in, qconv_w)
        k_in = _causal_dwconv_silu(k_in, kconv_w)
        v_in = _causal_dwconv_silu(v_in, vconv_w)
        queries = (q_in + ramp * p20_q).reshape(b, s, H, HD)
        keys = (k_in + ramp * p20_k).reshape(b, s, H, HD)
        values = (v_in + ramp * p20_v).reshape(b, s, H, HD)
        g = jax.nn.log_sigmoid(dec_in.astype(jnp.float32)).astype(hidden.dtype)
        beta = jax.nn.sigmoid(beta_in)
        reads = _gated_delta_rule(queries, keys, values, g, beta)
        normed_reads = _rmsnorm(reads, mnorm_scale).reshape(b, s, d)
        fused = jnp.concatenate([normed_reads, normed_p20], axis=-1)
        projected = fused @ out_W + out_b
        return jax.nn.sigmoid(gate_in) * projected

    def _L0_ffn_ref(x, wg, w1, b1, w2, b2):
        import math
        import jax, jax.numpy as jnp
        import numpy as np
        K = 2
        CAP_FACTOR = 1.0
        EPS = 1e-09
        B, S, D = x.shape
        E = wg.shape[1]
        xt = x.reshape(-1, D)
        N = xt.shape[0]
        cap = int(math.ceil(CAP_FACTOR * K * N / E))
        logits = xt.astype(jnp.float32) @ wg.astype(jnp.float32)
        scores = jax.nn.softmax(logits, axis=-1)
        gvals, gidx = jax.lax.top_k(scores, K)
        gvals = gvals / jnp.clip(gvals.sum(-1, keepdims=True), EPS)
        offset = jnp.zeros((E,), jnp.int32)
        pos_l, keep_l = ([], [])
        for kk in range(K):
            m = jax.nn.one_hot(gidx[:, kk], E, dtype=jnp.int32)
            loc = jnp.cumsum(m, axis=0) - 1 + offset[None, :]
            offset = offset + m.sum(axis=0)
            pos = jnp.take_along_axis(loc, gidx[:, kk:kk + 1], axis=1)[:, 0]
            keep = pos < cap
            pos_l.append(jnp.where(keep, pos, 0))
            keep_l.append(keep)
        pos = jnp.stack(pos_l, axis=1)
        keep = jnp.stack(keep_l, axis=1)
        gvals = gvals * keep
        e_flat = gidx.reshape(-1)
        p_flat = pos.reshape(-1)
        kmask = keep.reshape(-1).astype(x.dtype)
        x_rep = jnp.repeat(xt, K, axis=0)
        disp = jnp.zeros((E, cap, D), x.dtype).at[e_flat, p_flat].add(x_rep * kmask[:, None])
        h = jax.nn.gelu(jnp.einsum('ecd,edh->ech', disp, w1) + b1[:, None, :], approximate=False)
        y = jnp.einsum('ech,ehd->ecd', h, w2) + b2[:, None, :]
        yk = y[e_flat, p_flat]
        w = gvals.reshape(-1).astype(x.dtype)
        out = (yk * w[:, None]).reshape(N, K, D).sum(axis=1)
        return out.reshape(B, S, D)
    x = L0_attn_hidden
    x = _layernorm(x + _L0_attn_ref(x, L0_attn_p20_decay_log, L0_attn_p20_theta, L0_attn_ctrl_W, L0_attn_ctrl_b, L0_attn_p20c_W, L0_attn_qconv_w, L0_attn_kconv_w, L0_attn_vconv_w, L0_attn_mnorm_scale, L0_attn_vnorm_scale, L0_attn_ramp_logit, L0_attn_out_W, L0_attn_out_b), axis=-1)
    x = _layernorm(x + _L0_ffn_ref(x, L0_ffn_wg, L0_ffn_w1, L0_ffn_b1, L0_ffn_w2, L0_ffn_b2), axis=-1)
    return x

_drawn_inputs = setup_inputs


def setup_inputs(seed=0):
    import zlib

    import numpy as np

    out = dict(_drawn_inputs(seed))
    spreads = {'L0_attn_mnorm_scale': (1.0, 0.6),
     'L0_attn_vnorm_scale': (1.0, 0.6),
     'L0_attn_ramp_logit': (-4.59499979019165, 0.6),
     'L0_attn_out_b': (0.0, 0.344),
     'L0_ffn_b1': (0.0, 0.307),
     'L0_ffn_b2': (0.0, 0.1)}
    factors = {'L0_attn_p20c_W': 26.054}
    for name, (base, spread) in spreads.items():
        noise = np.random.default_rng([zlib.crc32(name.encode()), seed]).standard_normal(out[name].shape)
        drawn = base * np.exp(spread * noise) if base else spread * noise
        out[name] = jnp.asarray(drawn.astype(out[name].dtype))
    for name, factor in factors.items():
        out[name] = (out[name] * factor).astype(out[name].dtype)
    return out
```

```python
import numpy as np
import concourse.bass as bass
from concourse import mybir
from contextlib import ExitStack

F32 = mybir.dt.float32
I32 = mybir.dt.int32
U32 = mybir.dt.uint32
ALU = mybir.AluOpType
ACT = mybir.ActivationFunctionType
AX = mybir.AxisListType

P = 128
B, S, D, H = 16, 1024, 256, 16
HD = D // H
TAPS = 4
CHUNK = 16
HPT = P // HD
E, TOPK, HID = 8, 2, 1024
N = B * S
CAP = -(-TOPK * N // E)
BPU = 8
GROUPS = B // BPU
SLABS = S // P
COLS = BPU * P
NCH = P // CHUNK
SETS = 2 * BPU
G = SETS * NCH
TILES = N // P
BLKS = E * CAP // P
SPB = 4
EPS_RMS, EPS_LN, EPS_GATE = 1e-6, 1e-5, 1e-9
TWO_PI = 2.0 * np.pi


class Bank:

    def __init__(self, order, banks, filled, freed):
        self.order, self.banks, self.filled, self.freed = order, banks, filled, freed
        self.at = {key: i for i, (key, _) in enumerate(order)}
        assert len(self.at) == len(order) and len(order) % len(banks) == 0
        self.count = {w: sum(o == w for _, o in order) for w in freed}
        self.nth, seen = [], {w: 0 for w in freed}
        for _, w in order:
            seen[w] += 1
            self.nth.append(seen[w])
        self.pads = sum(key[0] == "pad" for key, _ in order)
        self.said = 0

    def __getitem__(self, key):
        return self.banks[self.at[key] % len(self.banks)]

    def full(self, u, key):
        return u * len(self.order) + self.at[key] + 1

    def take(self, pe, u, key):
        i = self.at[key]
        assert i == self.said % len(self.order), (key, self.order[self.said % len(self.order)])
        self.said += 1
        if self.said == len(self.order) - self.pads:
            self.said = 0
        j = i - len(self.banks)
        who = self.order[j][1]
        value = u * self.count[who] + self.nth[j] + (self.count[who] if j >= 0 else 0)
        pe.wait_ge(self.freed[who], value)
        return self[key]


class Steps:

    def __init__(self, eng, sem, per):
        self.eng, self.sem, self.per, self.k = eng, sem, per, 0

    def start(self, u):
        self.u, self.k = u, 0

    def then(self, ins):
        self.k += 1
        ins.then_inc(self.sem, 1)
        self.eng.wait_ge(self.sem, self.u * self.per + self.k)

    def end(self):
        assert self.k == self.per, (self.k, self.per)


def build(nc, hidden, decay_log, theta, ctrl_W, ctrl_b, p20c_W, qconv, kconv, vconv, mnorm, vnorm,
          ramp, out_W, out_b, wg, w1, b1, w2, b2, out, groups=GROUPS, slabs=SLABS, stage=9):
    ctx = ExitStack()
    with ctx:
        x1d = nc.dram_tensor("x1_rows", [N, D], F32, kind="Internal").ap()
        yd = nc.dram_tensor("expert_rows", [E * CAP, D], F32, kind="Internal").ap()
        keep = ctx.enter_context(nc.sbuf_tensor("router_scores", [P, B, SLABS, E], F32))
        ident = ctx.enter_context(nc.sbuf_tensor("ident", [P, P], F32))
        ones = ctx.enter_context(nc.sbuf_tensor("ones", [P, P], F32))
        banks = [ctx.enter_context(nc.psum_tensor(f"bank{i}", [P, 512], F32)) for i in range(8)]
        attention(nc, hidden, decay_log, theta, ctrl_W, ctrl_b, p20c_W, qconv, kconv, vconv, mnorm,
                  vnorm, ramp, out_W, out_b, wg, x1d, keep, ident, ones, banks, groups, slabs)
        if stage < 2:
            return
        idx = ctx.enter_context(nc.sbuf_tensor("slot_token", [P, BLKS], U32))
        slot = ctx.enter_context(nc.sbuf_tensor("token_slot", [P, TILES, TOPK], U32))
        wk = ctx.enter_context(nc.sbuf_tensor("token_weight", [P, TOPK, TILES], F32))
        route(nc, keep, ident, ones, banks, idx, slot, wk)
        if stage < 3:
            return
        experts(nc, x1d, yd, w1, b1, w2, b2, idx, ident, banks)
        combine(nc, x1d, yd, slot, wk, out.rearrange("b t d -> (b t) d"))


def attention(nc, hidden, decay_log, theta, ctrl_W, ctrl_b, p20c_W, qconv, kconv, vconv, mnorm,
              vnorm, ramp, out_W, out_b, wg, x1d, keep, ident, ones, banks, groups, slabs):
    ctx = ExitStack()
    with ctx:
        def sb(name, *shape, dt=F32):
            return ctx.enter_context(nc.sbuf_tensor(name, list(shape), dt))

        def sem(name):
            return ctx.enter_context(nc.semaphore(name))

        ctrlW = sb("ctrlW", P, 2, 3 * D + 2 * H + D)
        p20W = sb("p20W", P, 2, 3 * D)
        outW = sb("outW", P, 4, D)
        wgs = sb("wgs", P, 2, E)
        cb = sb("ctrl_bias", P, 6)
        gb = sb("gate_bias", H, 2)
        convw = sb("convw", P, 6, TAPS)
        mn = sb("mn", P, 1)
        vn = sb("vn", P, 2)
        outb = sb("outb_rows", P, D)
        gateb = sb("gateb_rows", P, D)
        blk = sb("head_blocks", P, P)
        hmask = sb("head_mask", P, HPT)
        diag = sb("diag16", P, CHUNK)
        upto = sb("upto16", P, CHUNK)
        below = sb("neg_below16", P, CHUNK)
        sel = sb("head_select", H, 2, P)
        eps = sb("eps", P, 4)
        cosT = sb("cosT", P, P)
        sinT = sb("sinT", P, P)
        pw = sb("powers", P, 4, 2)
        rdec = sb("rdec", P, 4)
        decay0 = sb("decay_pattern", P, COLS)
        restart = sb("restart_pattern", H, COLS)
        carry = sb("scan_carry", P, 2, BPU)
        csm = sb("carry_small", P, 4, BPU)
        hist = sb("conv_history", P, 6, BPU, TAPS - 1)
        state = sb("delta_state", P, SETS, HD)
        R = [sb(f"region{i}", P, 2 * COLS) for i in range(10)]
        r10 = sb("region10", P, 2 * BPU * (P + TAPS - 1))
        r11 = sb("region11", P, 2 * COLS)
        inv = sb("inverse", P, CHUNK, HPT, CHUNK)
        kqi = sb("kqi", P, G, 3, CHUNK)
        bdk = sb("bd_k", P, 2, SETS, P)
        bdt = sb("bd_t", P, SETS, P)
        bdc = sb("bd_kc", P, SETS, P)
        gj = sb("gj", P, 6, G)
        stats = sb("stats", P, BPU, 6)
        mv = sb("mv", P, BPU, 2)
        rstd = sb("rstd", P, BPU)

        def half(t, i):
            return t[:, i * COLS:(i + 1) * COLS]

        x = R[0][:, :].rearrange("p (b d) -> p b d", b=BPU)
        xT = R[1][:, :].rearrange("p (e n) -> p e n", e=2)
        prod_v, prod_p = R[2], R[3]
        zin, zout = R[4], R[5]
        npT = R[6][:, :].rearrange("p (e n) -> p e n", e=2)
        gate = R[7][:, :].rearrange("p (b d) -> p b d", b=BPU)
        vT = R[8]
        tmp = R[9]
        gi, bi, fdec = R[2], R[3], R[4]
        fP, fA, gq, aT = R[1], R[5], R[9], R[2]
        pT, kc = r10, r11
        bds = R[5][:, :].rearrange("p (s n) -> p s n", n=P)
        bde = R[8][:, :].rearrange("p (s n) -> p s n", n=P)
        ch = R[1][:, 0:4 * SETS * HD].rearrange("p (k s v) -> p k s v", k=4, s=SETS)
        aB, tT, vB, vbeta = R[3], R[4], R[1], R[2]
        oT = R[3][:, :].rearrange("p (e n) -> p e n", e=2)
        osq, orr, y1 = R[4], R[8], R[8][:, :].rearrange("p (b d) -> p b d", b=BPU)
        x1T = R[3]
        cin = r10[:, :].rearrange("p (a b t) -> p a b t", a=2, t=P + TAPS - 1)
        decx, logx = R[2][0:H, 0:COLS], R[2][0:H, COLS:]
        gcum, bet = R[5][0:H, 0:COLS], R[5][0:H, COLS:]
        g16 = lambda t: t[:, 0:G * CHUNK].rearrange("p (g i) -> p g i", i=CHUNK)
        by_chunk = lambda t: t[:, 0:G * CHUNK].rearrange("p (s c i) -> p s c i", s=SETS, c=NCH)
        GJ, BJ, EC, ECJ, NBG, GT = (gj[:, i, :] for i in range(6))

        passed = sem("wait_passed")
        s_load, s_const, s_x, s_x1 = sem("weights_loaded"), sem("constants"), sem("x_loaded"), sem("x1_stored")
        s_prep, s_ready = sem("prepared"), sem("setup_done")
        unit_done = sem("unit_done")
        zeroed = sem("state_zeroed")
        xT_ready, rot_p, scanned = sem("xT_ready"), sem("rotated_by_pool"), sem("scanned")
        y_v, y_p, sq_ready, rs_ready = sem("y_even"), sem("y_odd"), sem("p20_squares"), sem("p20_rs")
        np_v, np_p = sem("np_even"), sem("np_odd")
        gate_added, gate_ready = sem("gate_added"), sem("gate_ready")
        dec_log, bet_ready, gcum_ready = sem("dec_log"), sem("bet_ready"), sem("gcum_ready")
        gi_ready, bi_ready = sem("gi_ready"), sem("bi_ready")
        cin_ready, conv_done, silu_done, raw_ready = sem("cin_ready"), sem("conv_done"), sem("silu_done"), sem("raw_ready")
        msq_ready, mrs_ready, kq_ready = sem("msq_ready"), sem("mrs_ready"), sem("kq_ready")
        diag_mul, gj_ready, diff_ready = sem("diag_mul"), sem("gj_ready"), sem("diff_ready")
        f_ready, e_ready, fp_ready, sm_ready = sem("f_ready"), sem("e_ready"), sem("fp_ready"), sem("sm_ready")
        bd1_ready, bd1_used = sem("bd1_ready"), sem("bd1_used")
        a_ready, ab_ready, inv_ready, tT_ready = sem("a_ready"), sem("ab_ready"), sem("inv_ready"), sem("tT_ready")
        vb_ready, vbeta_ready = sem("vb_ready"), sem("vbeta_ready")
        bdk_r, bdt_r, bdc_r, bds_r, bde_r = sem("bdk_r"), sem("bdt_r"), sem("bdc_r"), sem("bds_r"), sem("bde_r")
        d_ready, ed_ready, st_ready = sem("d_ready"), sem("ed_ready"), sem("st_ready")
        e_plain = sem("e_plain")
        o_evac, osq_ready, ors_ready, on_ready = sem("o_evac"), sem("osq_ready"), sem("ors_ready"), sem("on_ready")
        var_ready, rstd_ready, x1_ready, x1T_ready = sem("var_ready"), sem("rstd_ready"), sem("x1_ready"), sem("x1T_ready")
        filled_f, filled_b = sem("front_filled"), sem("back_filled")
        freed = {(r, w): sem(f"{r}_freed_by_{w}") for r in "fb" for w in ("act", "dve")}
        dve_steps = sem("dve_steps")
        dve_chain, act_chain, pool_chain = sem("dve_chain"), sem("act_chain"), sem("pool_chain")

        MS = (2, 3, 0, 1, 4, 5)
        order = [(("xT", q, e), "act") for q in range(2) for e in range(2)]
        order += [(("gate", b), "dve") for b in range(BPU // 2)]
        order += [((n, q), "act") for n in ("dec", "bet") for q in range(2)]
        order += [(("pss", q), "act") for q in range(2)]
        order += [((n, hh, q), "act") for n in ("gi", "bi") for hh in range(2) for q in range(2)]
        for m in MS:
            order += [(("ctl", m, q), "act") for q in range(2)]
        for m in MS:
            order += [(("p20", m, q), "dve") for q in range(2)]
            if m < 4:
                order += [(("nrm", m, q), "act") for q in range(2)]
        order += [(("mm1", t), "dve") for t in range(G // 8)]
        order += [(("v1", t), "act") for t in range(4)]
        order += [(("aT", t), "act") for t in range(4)]
        order += [(("v2", t), "dve") for t in range(4)]
        order += [(("tT", t), "act") for t in range(4)]
        while len(order) % 4:
            order.append((("pad", len(order)), "act"))
        front = Bank(order, banks[0:4], filled_f, {w: freed["f", w] for w in ("act", "dve")})
        order = []
        for c in range(NCH):
            order += [(("X", c), "dve"), (("E", c), "dve"), (("dS", c), "dve"), (("O", c), "act")]
        order += [(("on", hh, q), "act") for hh in range(2) for q in range(2)]
        order += [(("proj", b), "dve") for b in range(BPU // 2)]
        order += [(("x1T", b), "act") for b in range(BPU // 2)]
        order += [(("lg", 0), "act")]
        while len(order) % 4:
            order.append((("pad", len(order)), "act"))
        back = Bank(order, banks[4:8], filled_b, {w: freed["b", w] for w in ("act", "dve")})

        def loop(eng, body, begin=None):
            with eng.Fori(0, groups) as grp:
                if begin is not None:
                    begin(grp)
                with eng.Fori(0, slabs) as s:
                    body(grp * slabs + s, grp, s)

        NLOAD = 16 + HPT
        with nc.Block() as block:
            def bd(eng, out_, in_):
                return eng.tensor_tensor(out_.rearrange("p s (h i) -> p s h i", h=HPT),
                                         in_.unsqueeze(2).broadcast_to([P, SETS, HPT, CHUNK]),
                                         hmask[:, :].unsqueeze(1).unsqueeze(3).broadcast_to([P, SETS, HPT, CHUNK]),
                                         ALU.mult)

            def convo(i):
                return [half(R[9], 0), half(R[9], 1), half(R[5], 0), half(R[5], 1), half(vT, 0), half(vT, 1)][i]

            @block.sync
            def _(sp):
                for dst, src in (
                    (ctrlW[:, :, :], ctrl_W.rearrange("(p e) n -> p e n", e=2)),
                    (p20W[:, :, :], p20c_W.rearrange("(p e) n -> p e n", e=2)),
                    (outW[:, 0:2, :], out_W[0:D, :].rearrange("(k p) n -> p k n", p=P)),
                    (outW[:, 2:4, :], out_W[D:2 * D, :].rearrange("(p e) n -> p e n", e=2)),
                    (wgs[:, :, :], wg.rearrange("(k p) n -> p k n", p=P)),
                    (cb[:, :], ctrl_b[0:3 * D].rearrange("(m p) -> p m", p=P)),
                    (gb[:, :], ctrl_b[3 * D:3 * D + 2 * H].rearrange("(k p) -> p k", p=H)),
                    (convw[:, 0:2, :], qconv.rearrange("(m p) t -> p m t", p=P)),
                    (convw[:, 2:4, :], kconv.rearrange("(m p) t -> p m t", p=P)),
                    (convw[:, 4:6, :], vconv.rearrange("(m p) t -> p m t", p=P)),
                    (vn[:, :], vnorm.rearrange("(p e) -> p e", e=2)),
                    (outb[:, :], out_b.partition_broadcast(P)),
                    (gateb[:, :], ctrl_b[3 * D + 2 * H:].partition_broadcast(P)),
                    (rdec[:, 0:1], decay_log.rearrange("(p o) -> p o", o=1)),
                    (rdec[:, 1:2], theta.rearrange("(p o) -> p o", o=1)),
                    (R[0][:, 0:D], ramp.partition_broadcast(P)),
                ):
                    sp.dma_start(dst, src, allow_slow_non_contiguous=True).then_inc(s_load, 16)
                for h in range(HPT):
                    sp.dma_start(mn[h * HD:(h + 1) * HD, :], mnorm.rearrange("(p o) -> p o", o=1)).then_inc(s_load, 16)

                def body(u, grp, s):
                    sp.wait_ge(unit_done, u + 1)
                    sp.dma_start(x, hidden[bass.ds(grp * BPU, BPU), bass.ds(s * P, P), :]
                                 .rearrange("b t d -> t b d")).then_inc(s_x, 16)
                    sp.wait_ge(x1_ready, u + 1)
                    sp.dma_start(x1d.rearrange("(b t) d -> t b d", b=B)[bass.ds(s * P, P), bass.ds(grp * BPU, BPU), :],
                                 y1).then_inc(s_x1, 16)
                sp.wait_ge(s_ready, 1)
                loop(sp, body)
                sp.wait_ge(s_x1, groups * slabs * 16 + 16)

            @block.gpsimd
            def _(pool):
                pc = Steps(pool, pool_chain, 8)
                pool.memset(ident[:, :], 0.0).then_inc(s_const, 1)
                pool.memset(hmask[:, :], 1.0).then_inc(s_const, 1)
                pool.memset(sel[:, :, :], 0.0).then_inc(s_const, 1)
                pool.memset(ones[:, :], 1.0).then_inc(s_const, 1)
                pool.wait_ge(s_const, 4)
                pool.affine_select(out=ident[:, :], in_=ident[:, :], compare_op=ALU.not_equal, fill=1.0, base=0,
                                   pattern=[[-1, P]], channel_multiplier=1).then_inc(s_const, 1)
                pool.affine_select(out=hmask[:, :], in_=hmask[:, :], compare_op=ALU.is_ge, fill=0.0, base=0,
                                   pattern=[[-HD, HPT]], channel_multiplier=1).then_inc(s_const, 1)
                pool.affine_select(out=sel[:, :, :].rearrange("k a (h j) -> k a h j", j=HD),
                                   in_=sel[:, :, :].rearrange("k a (h j) -> k a h j", j=HD),
                                   compare_op=ALU.not_equal, fill=1.0, base=0,
                                   pattern=[[-HPT, 2], [-1, HPT], [0, HD]], channel_multiplier=1).then_inc(s_const, 1)
                pool.wait_ge(s_const, 7)
                pool.affine_select(out=hmask[:, :], in_=hmask[:, :], compare_op=ALU.is_ge, fill=0.0, base=HD - 1,
                                   pattern=[[HD, HPT]], channel_multiplier=-1).then_inc(s_const, 1)
                pool.wait_ge(s_const, 8)
                pool.tensor_tensor(blk[:, :].rearrange("p (h j) -> p h j", j=HD),
                                   hmask[:, :].unsqueeze(2).broadcast_to([P, HPT, HD]),
                                   ones[:, :].rearrange("p (h j) -> p h j", j=HD), ALU.mult).then_inc(s_const, 1)
                pool.wait_ge(s_const, 9)
                pool.affine_select(out=bds[:, 0, :], in_=blk[:, :], compare_op=ALU.is_ge, fill=0.0, base=0,
                                   pattern=[[1, P]], channel_multiplier=-1).then_inc(s_const, 1)
                pool.wait_ge(s_ready, 1)
                tab = lambda t: t[:, :].unsqueeze(1).broadcast_to([P, BPU, P])
                v3 = lambda t, i: half(t, i).rearrange("p (b t) -> p b t", b=BPU)
                m16 = lambda t: t[:, :].unsqueeze(1).broadcast_to([P, G, CHUNK])

                def body(u, grp, s):
                    pc.start(u)
                    pool.wait_ge(unit_done, u + 1)
                    pool.wait_ge(xT_ready, u * 4 + 4)
                    pool.tensor_tensor(v3(prod_p, 0), xT[:, 1, :].rearrange("p (b t) -> p b t", b=BPU), tab(cosT), ALU.mult)
                    pc.then(pool.tensor_tensor(v3(prod_p, 1), xT[:, 0, :].rearrange("p (b t) -> p b t", b=BPU), tab(sinT), ALU.mult))
                    pool.tensor_tensor(half(zin, 1), half(prod_p, 0), half(prod_p, 1), ALU.subtract).then_inc(rot_p, 1)
                    pool.wait_ge(scanned, u * 2 + 2)
                    pool.wait_ge(rot_p, u + 1)
                    pool.tensor_tensor(v3(prod_p, 0), v3(zout, 1), tab(cosT), ALU.mult)
                    pc.then(pool.tensor_tensor(v3(prod_p, 1), v3(zout, 0), tab(sinT), ALU.mult))
                    pool.tensor_tensor(npT[:, 1, :], half(prod_p, 0), half(prod_p, 1), ALU.add).then_inc(y_p, 1)
                    pool.wait_ge(rs_ready, u * 2 + 2)
                    pool.wait_ge(y_p, u + 1)
                    pool.tensor_tensor(npT[:, 1, :], npT[:, 1, :], half(R[4], 0), ALU.mult).then_inc(np_p, 1)
                    pool.wait_ge(gi_ready, u * 4 + 4)
                    pool.wait_ge(np_v, u + 1)
                    pool.wait_ge(np_p, u + 1)
                    pool.tensor_tensor(g16(R[4]), g16(gi), m16(diag), ALU.mult).then_inc(diag_mul, 1)
                    pool.wait_ge(bi_ready, u * 4 + 4)
                    pool.wait_ge(gj_ready, u * 2 + 1)
                    pool.tensor_tensor(g16(R[4]), g16(bi), m16(diag), ALU.mult).then_inc(diag_mul, 1)
                    pool.wait_ge(f_ready, u + 1)
                    pc.then(pool.tensor_tensor(g16(fP), g16(fdec), m16(upto), ALU.mult))
                    pc.then(pool.tensor_tensor(g16(fdec), g16(fdec), m16(below), ALU.mult))
                    pool.tensor_tensor(g16(fA), g16(fdec), g16(bi), ALU.mult).then_inc(fp_ready, 1)
                    pool.wait_ge(e_ready, u + 1)
                    pool.wait_ge(kq_ready, u * 4 + 4)
                    pool.wait_ge(raw_ready, u * 12 + 12)
                    pool.tensor_tensor(g16(gq), kqi[:, :, 1, :], g16(r11), ALU.mult).then_inc(fp_ready, 1)
                    for t in range(NCH):
                        if t >= 2:
                            pool.wait_ge(bd1_used, u * NCH + t - 1)
                        pool.tensor_tensor(bdk[:, t % 2, :, :].rearrange("p s (h i) -> p s h i", h=HPT),
                                           kqi[:, t * SETS:(t + 1) * SETS, 0, :].unsqueeze(2).broadcast_to([P, SETS, HPT, CHUNK]),
                                           hmask[:, :].unsqueeze(1).unsqueeze(3).broadcast_to([P, SETS, HPT, CHUNK]),
                                           ALU.mult).then_inc(bd1_ready, 1)
                    for c in range(NCH):
                        if c < 2:
                            pool.wait_ge(bd1_used, u * NCH + NCH - 1 + c)
                        else:
                            pool.wait_ge(back.filled, back.full(u, ("X", c - 2)))
                        bd(pool, bdk[:, c % 2, :, :], kqi[:, :, 0, :].rearrange("p (s c) i -> p s c i", c=NCH)[:, :, c, :]).then_inc(bdk_r, 1)
                        if c == 0:
                            pool.wait_ge(a_ready, u * 16 + 16)
                        else:
                            pool.wait_ge(back.filled, back.full(u, ("dS", c - 1)))
                        bd(pool, bdc[:, :, :], by_chunk(kc)[:, :, c, :]).then_inc(bdc_r, 1)
                    pc.end()
                pc.per = 4
                loop(pool, body)

            @block.scalar
            def _(act):
                A = nc.scalar.activation
                act.wait_ge(s_load, NLOAD * 16)
                act.wait_ge(s_prep, 1)
                A(rdec[:, 0:1], rdec[:, 0:1], ACT.Exp).then_inc(s_prep, 1)
                act.wait_ge(s_prep, 2)
                A(rdec[:, 0:1], rdec[:, 0:1], ACT.Exp, scale=-1.0).then_inc(s_prep, 1)
                A(pw[:, 0, 1:2], rdec[:, 1:2], ACT.Sin).then_inc(s_prep, 1)
                A(pw[:, 0, 0:1], rdec[:, 2:3], ACT.Sin).then_inc(s_prep, 1)
                A(R[0][:, 0:D], R[0][:, 0:D], ACT.Sigmoid).then_inc(s_prep, 1)
                act.wait_ge(s_ready, 1)
                act.sem_inc(unit_done, 1)
                act.sem_inc(front.freed["act"], front.count["act"])
                act.sem_inc(back.freed["act"], back.count["act"])
                ac = Steps(act, act_chain, 0)

                def rs(bank, u, key, out_, scale, e):
                    act.wait_ge(bank.filled, bank.full(u, key))
                    ac.then(A(out_, bank[key][:, :], ACT.Ln, scale=scale, bias=eps[:, e:e + 1]))
                    return A(out_, out_, ACT.Exp, scale=-0.5)

                def body(u, grp, s):
                    ac.start(u)
                    act.wait_ge(unit_done, u + 1)
                    for q in range(2):
                        for e in range(2):
                            act.wait_ge(front.filled, front.full(u, ("xT", q, e)))
                            A(xT[:, e, q * 512:(q + 1) * 512], front["xT", q, e][:, :], ACT.Copy).then_inc(xT_ready, 1)
                            act.wait_ge(xT_ready, u * 4 + q * 2 + e + 1)
                            act.sem_inc(front.freed["act"], 1)
                    act.wait_ge(gate_added, u * 4 + 4)
                    A(R[7][:, :], R[7][:, :], ACT.Sigmoid).then_inc(gate_ready, 1)
                    act.wait_ge(scanned, u * 2 + 2)
                    act.wait_ge(y_v, u + 1)
                    act.wait_ge(y_p, u + 1)
                    for q in range(2):
                        act.wait_ge(front.filled, front.full(u, ("dec", q)))
                        ac.then(A(decx[:, q * 512:(q + 1) * 512], front["dec", q][0:H, :], ACT.Identity, bias=gb[:, 0:1]))
                        act.sem_inc(front.freed["act"], 1)
                    for q in range(2):
                        act.wait_ge(front.filled, front.full(u, ("bet", q)))
                        ac.then(A(bet[:, q * 512:(q + 1) * 512], front["bet", q][0:H, :], ACT.Sigmoid, bias=gb[:, 1:2]))
                        act.sem_inc(front.freed["act"], 1)
                    act.sem_inc(bet_ready, 1)
                    A(half(R[4], 0), npT[:, 0, :], ACT.Square).then_inc(sq_ready, 1)
                    A(half(R[4], 1), npT[:, 1, :], ACT.Square).then_inc(sq_ready, 1)
                    ac.then(A(logx, decx, ACT.Abs))
                    ac.then(A(logx, logx, ACT.Exp, scale=-1.0))
                    A(logx, logx, ACT.Ln, bias=1.0).then_inc(dec_log, 1)
                    act.wait_ge(front.filled, front.full(u, ("pss", 1)))
                    for q in range(2):
                        ins = rs(front, u, ("pss", q), R[4][:, q * 512:(q + 1) * 512], 1.0 / D, 0)
                        ins.then_inc(rs_ready, 1)
                        act.sem_inc(front.freed["act"], 1)
                    for n, dst, sg in (("gi", gi, gi_ready), ("bi", bi, bi_ready)):
                        for hh in range(2):
                            for q in range(2):
                                act.wait_ge(front.filled, front.full(u, (n, hh, q)))
                                ac.then(A(dst[:, hh * COLS + q * 512:hh * COLS + (q + 1) * 512], front[n, hh, q][:, :], ACT.Copy))
                                act.sem_inc(front.freed["act"], 1)
                                act.sem_inc(sg, 1)
                    for i, m in enumerate(MS):
                        if i >= 2:
                            act.wait_ge(conv_done, u * 6 + i - 1)
                        A(cin[:, i % 2, :, 0:TAPS - 1], hist[:, m, :, :], ACT.Copy)
                        for q in range(2):
                            act.wait_ge(front.filled, front.full(u, ("ctl", m, q)))
                            ac.then(A(cin[:, i % 2, 4 * q:4 * q + 4, TAPS - 1:], front["ctl", m, q][:, :].rearrange("p (b t) -> p b t", b=4),
                                      ACT.Identity, bias=cb[:, m:m + 1]))
                            act.sem_inc(front.freed["act"], 1)
                        act.sem_inc(cin_ready, 1)
                        A(hist[:, m, :, :], cin[:, i % 2, :, P:], ACT.Copy).then_inc(cin_ready, 1)
                    for i, m in enumerate(MS):
                        act.wait_ge(conv_done, u * 6 + i + 1)
                        A(convo(i), convo(i), ACT.Silu).then_inc(silu_done, 1)
                    for i, m in enumerate(MS[:4]):
                        act.wait_ge(raw_ready, u * 12 + 2 * i + 2)
                        if i:
                            act.wait_ge(kq_ready, u * 4 + i)
                            act.wait_ge(mrs_ready, u * 8 + 2 * i)
                        A(half(r11, 0), convo(i), ACT.Square).then_inc(msq_ready, 1)
                        for q in range(2):
                            ins = rs(front, u, ("nrm", m, q), r11[:, COLS + q * 512:COLS + (q + 1) * 512],
                                     float(HD) if m < 2 else 1.0, 1 if m < 2 else 0)
                            ins.then_inc(mrs_ready, 1)
                            act.sem_inc(front.freed["act"], 1)
                    act.wait_ge(kq_ready, u * 4 + 4)
                    act.wait_ge(diff_ready, u + 1)
                    A(g16(fdec), g16(fdec), ACT.Exp).then_inc(f_ready, 1)
                    A(r11[:, :], gi[:, :], ACT.Exp).then_inc(e_ready, 1)
                    A(EC, g16(gi)[:, :, CHUNK - 1], ACT.Exp)
                    A(ECJ, ECJ, ACT.Exp)
                    A(NBG, GJ, ACT.Exp).then_inc(sm_ready, 1)
                    act.wait_ge(a_ready, u * 16 + 16)
                    for t in range(4):
                        act.wait_ge(front.filled, front.full(u, ("v1", t)))
                        ac.then(A(vB[:, :].rearrange("p (v h j) -> p j h v", v=HD, h=HPT)[:, 4 * t:4 * t + 4, :, :],
                                  front["v1", t][:, :].rearrange("p (j h v) -> p j h v", j=4, h=HPT), ACT.Copy))
                        act.sem_inc(front.freed["act"], 1)
                    act.sem_inc(vb_ready, 1)
                    for t in range(4):
                        act.wait_ge(front.filled, front.full(u, ("aT", t)))
                        ac.then(A(aB[:, t * 512:(t + 1) * 512], front["aT", t][:, :], ACT.Copy))
                        act.sem_inc(front.freed["act"], 1)
                    act.sem_inc(ab_ready, 1)
                    for t in range(4):
                        act.wait_ge(front.filled, front.full(u, ("tT", t)))
                        ac.then(A(g16(tT).rearrange("p g i -> p i g")[:, 4 * t:4 * t + 4, :],
                                  front["tT", t][:, :].rearrange("p (i g) -> p i g", i=4), ACT.Copy))
                        act.sem_inc(front.freed["act"], 1)
                    act.sem_inc(tT_ready, 1)
                    if front.pads:
                        act.sem_inc(front.freed["act"], front.pads)
                    for c in range(NCH):
                        act.wait_ge(back.filled, back.full(u, ("O", c)))
                        ac.then(A(R[3][:, :].rearrange("p (s c i) -> p s c i", s=SETS, c=NCH)[:, :, c, :],
                                  back["O", c][:, 0:SETS * CHUNK].rearrange("p (s i) -> p s i", i=CHUNK), ACT.Copy))
                        act.sem_inc(back.freed["act"], 1)
                    A(osq[:, :], R[3][:, :], ACT.Square).then_inc(osq_ready, 1)
                    for hh in range(2):
                        for q in range(2):
                            ins = rs(back, u, ("on", hh, q), orr[:, hh * COLS + q * 512:hh * COLS + (q + 1) * 512], 1.0 / HD, 0)
                            ins.then_inc(ors_ready, 1)
                            act.sem_inc(back.freed["act"], 1)
                    act.wait_ge(var_ready, u + 1)
                    ac.then(A(rstd[:, :], mv[:, :, 1], ACT.Ln, bias=eps[:, 2:3]))
                    A(rstd[:, :], rstd[:, :], ACT.Exp, scale=-0.5).then_inc(rstd_ready, 1)
                    for b in range(BPU // 2):
                        act.wait_ge(back.filled, back.full(u, ("x1T", b)))
                        ac.then(A(x1T[:, b * 512:(b + 1) * 512], back["x1T", b][:, :], ACT.Copy))
                        act.sem_inc(back.freed["act"], 1)
                        act.sem_inc(x1T_ready, 1)
                    act.wait_ge(back.filled, back.full(u, ("lg", 0)))
                    ac.then(A(keep[:, bass.ds(grp * BPU, BPU), bass.ds(s, 1), :],
                              back["lg", 0][:, 0:BPU * E].rearrange("p (b o e) -> p b o e", o=1, e=E), ACT.Copy))
                    act.sem_inc(back.freed["act"], 1 + back.pads)
                    act.sem_inc(unit_done, 1)
                    ac.end()

                ac.per = 66
                loop(act, body, lambda grp: act.wait_ge(zeroed, grp + 1))

            @block.vector
            def _(dve):
                V = nc.vector
                setup = [0]

                def link(ins):
                    setup[0] += 1
                    ins.then_inc(dve_chain, 1)
                    dve.wait_ge(dve_chain, setup[0])
                dve.wait_ge(s_load, NLOAD * 16)
                dve.wait_ge(s_const, 10)
                link(V.tensor_scalar(rdec[:, 2:3], rdec[:, 1:2], 1.0 / TWO_PI, 12582912.0, ALU.mult, ALU.add))
                link(V.tensor_scalar(rdec[:, 2:3], rdec[:, 2:3], -12582912.0, None, ALU.add))
                link(V.scalar_tensor_tensor(rdec[:, 1:2], rdec[:, 2:3], -6.28125, rdec[:, 1:2], ALU.mult, ALU.add))
                link(V.scalar_tensor_tensor(rdec[:, 1:2], rdec[:, 2:3], -(TWO_PI - 6.28125), rdec[:, 1:2], ALU.mult, ALU.add))
                link(V.tensor_scalar(rdec[:, 1:2], rdec[:, 1:2], float(np.float32(3.1415925)), float(np.float32(-3.1415925)), ALU.min, ALU.max))
                link(V.tensor_scalar(rdec[:, 2:3], rdec[:, 1:2], -1.0, None, ALU.mult))
                link(V.tensor_tensor(rdec[:, 2:3], rdec[:, 1:2], rdec[:, 2:3], ALU.max))
                link(V.tensor_scalar(rdec[:, 2:3], rdec[:, 2:3], -1.0, float(np.pi / 2), ALU.mult, ALU.add))
                V.memset(eps[:, 0:1], EPS_RMS)
                V.memset(eps[:, 1:2], HD * EPS_RMS)
                link(V.memset(eps[:, 2:3], EPS_LN))
                dve.sem_inc(s_prep, 1)
                link(V.tensor_reduce(diag[:, :], ident[:, :].rearrange("p (h i) -> p i h", h=HPT), AX.X, ALU.add))
                link(V.tensor_reduce(upto[:, :], bds[:, 0, :].rearrange("p (h i) -> p i h", h=HPT), AX.X, ALU.add))
                link(V.tensor_tensor(below[:, :], diag[:, :], upto[:, :], ALU.subtract))
                V.tensor_copy(kqi[:, :, 2, :], diag[:, :].unsqueeze(1).broadcast_to([P, G, CHUNK]))
                V.memset(inv[:, :, :, :], 0.0)
                V.memset(restart[:, :], 1.0)
                V.memset(cosT[:, 0:1], 1.0)
                link(V.memset(sinT[:, 0:1], 0.0))
                for i in range(CHUNK):
                    V.memset(inv[:, i, :, i:i + 1], 1.0)
                link(V.memset(restart[:, :].rearrange("p (g i) -> p g i", i=CHUNK)[:, :, 0:1], 0.0))
                for e in range(2):
                    V.tensor_scalar(p20W[:, e, :], p20W[:, e, :], vn[:, e:e + 1], None, ALU.mult)
                    V.tensor_scalar(outW[:, 2 + e, :], outW[:, 2 + e, :], vn[:, e:e + 1], None, ALU.mult)
                    link(V.tensor_scalar(outW[:, e, :], outW[:, e, :], mn[:, 0:1], None, ALU.mult))
                dve.wait_ge(s_prep, 6)
                for e in range(2):
                    link(V.tensor_tensor(p20W[:, e, :].rearrange("p (k n) -> p k n", k=3), p20W[:, e, :].rearrange("p (k n) -> p k n", k=3),
                                         R[0][:, 0:D].unsqueeze(1).broadcast_to([P, 3, D]), ALU.mult))
                link(V.memset(decay0[:, :], 1.0))
                link(V.tensor_scalar(decay0[:, :], decay0[:, :], rdec[:, 0:1], None, ALU.mult))
                link(V.memset(decay0[:, :].rearrange("p (b t) -> p b t", b=BPU)[:, :, 0:1], 0.0))
                n = 1
                while n < P:
                    link(V.tensor_scalar(pw[:, 2, :], pw[:, 0, :], pw[:, 0, 1:2], None, ALU.mult))
                    c0, s0 = pw[:, 0, 0:1], pw[:, 0, 1:2]
                    link(V.tensor_scalar(cosT[:, n:2 * n], sinT[:, 0:n], s0, -1.0, ALU.mult, ALU.mult))
                    link(V.scalar_tensor_tensor(cosT[:, n:2 * n], cosT[:, 0:n], c0, cosT[:, n:2 * n], ALU.mult, ALU.add))
                    link(V.tensor_scalar(sinT[:, n:2 * n], cosT[:, 0:n], s0, None, ALU.mult))
                    link(V.scalar_tensor_tensor(sinT[:, n:2 * n], sinT[:, 0:n], c0, sinT[:, n:2 * n], ALU.mult, ALU.add))
                    link(V.scalar_tensor_tensor(pw[:, 1, 0:1], c0, c0, pw[:, 2, 1:2], ALU.mult, ALU.subtract))
                    link(V.tensor_scalar(pw[:, 1, 1:2], pw[:, 2, 0:1], 2.0, None, ALU.mult))
                    link(V.tensor_copy(pw[:, 0, :], pw[:, 1, :]))
                    n *= 2
                dve.sem_inc(front.freed["dve"], front.count["dve"])
                dve.sem_inc(back.freed["dve"], back.count["dve"])
                dve.sem_inc(s_x1, 16)
                dve.sem_inc(s_ready, 1)
                dc = Steps(dve, dve_steps, 0)
                tab = lambda t: t[:, :].unsqueeze(1).broadcast_to([P, BPU, P])
                v3 = lambda t, i: half(t, i).rearrange("p (b t) -> p b t", b=BPU)
                xb = lambda e: xT[:, e, :].rearrange("p (b t) -> p b t", b=BPU)

                def freed_(bank, n=1):
                    dve.sem_inc(bank.freed["dve"], n)

                def body(u, grp, s):
                    dc.start(u)
                    dve.wait_ge(zeroed, grp + 1)
                    dve.wait_ge(unit_done, u + 1)
                    dve.wait_ge(s_x1, u * 16 + 16)
                    for b in range(BPU // 2):
                        dve.wait_ge(front.filled, front.full(u, ("gate", b)))
                        V.tensor_tensor(gate[:, 2 * b:2 * b + 2, :], front["gate", b][:, :].rearrange("p (b d) -> p b d", b=2),
                                        gateb[:, :].unsqueeze(1).broadcast_to([P, 2, D]), ALU.add).then_inc(gate_added, 1)
                        dve.wait_ge(gate_added, u * 4 + b + 1)
                        freed_(front)
                    dve.wait_ge(xT_ready, u * 4 + 4)
                    V.tensor_tensor(v3(prod_v, 0), xb(0), tab(cosT), ALU.mult)
                    dc.then(V.tensor_tensor(v3(prod_v, 1), xb(1), tab(sinT), ALU.mult))
                    dc.then(V.tensor_tensor(half(zin, 0), half(prod_v, 0), half(prod_v, 1), ALU.add))
                    dve.wait_ge(rot_p, u + 1)
                    for e in range(2):
                        dc.then(V.scalar_tensor_tensor(v3(zin, e)[:, :, 0], carry[:, e, :], rdec[:, 0:1], v3(zin, e)[:, :, 0], ALU.mult, ALU.add))
                    for e in range(2):
                        V.tensor_tensor_scan(half(zout, e), decay0[:, :], half(zin, e), 0.0, ALU.mult, ALU.add).then_inc(scanned, 1)
                    dve.wait_ge(scanned, u * 2 + 2)
                    zr, zi = v3(zout, 0)[:, :, P - 1], v3(zout, 1)[:, :, P - 1]
                    V.tensor_scalar(csm[:, 0, :], zi, pw[:, 0, 1:2], None, ALU.mult)
                    dc.then(V.tensor_scalar(csm[:, 1, :], zr, pw[:, 0, 1:2], None, ALU.mult))
                    V.scalar_tensor_tensor(carry[:, 0, :], zr, pw[:, 0, 0:1], csm[:, 0, :], ALU.mult, ALU.subtract)
                    V.scalar_tensor_tensor(carry[:, 1, :], zi, pw[:, 0, 0:1], csm[:, 1, :], ALU.mult, ALU.add)
                    V.tensor_tensor(v3(prod_v, 0), v3(zout, 0), tab(cosT), ALU.mult)
                    dc.then(V.tensor_tensor(v3(prod_v, 1), v3(zout, 1), tab(sinT), ALU.mult))
                    V.tensor_tensor(npT[:, 0, :], half(prod_v, 0), half(prod_v, 1), ALU.subtract).then_inc(y_v, 1)
                    dve.wait_ge(dec_log, u + 1)
                    dc.then(V.scalar_tensor_tensor(logx, decx, 0.0, logx, ALU.min, ALU.subtract))
                    V.tensor_tensor_scan(gcum, restart[:, :], logx, 0.0, ALU.mult, ALU.add).then_inc(gcum_ready, 1)
                    dve.wait_ge(rs_ready, u * 2 + 2)
                    dve.wait_ge(y_v, u + 1)
                    V.tensor_tensor(npT[:, 0, :], npT[:, 0, :], half(R[4], 0), ALU.mult).then_inc(np_v, 1)
                    dve.wait_ge(diag_mul, u * 2 + 1)
                    V.tensor_reduce(GJ, g16(R[4]), AX.X, ALU.add).then_inc(gj_ready, 1)
                    dve.wait_ge(diag_mul, u * 2 + 2)
                    V.tensor_reduce(BJ, g16(R[4]), AX.X, ALU.add).then_inc(gj_ready, 1)
                    dve.wait_ge(gj_ready, u * 2 + 2)
                    dc.then(V.tensor_tensor(g16(fdec), g16(gi), GJ.unsqueeze(2).broadcast_to([P, G, CHUNK]), ALU.subtract))
                    V.tensor_scalar(g16(fdec), g16(fdec), 0.0, None, ALU.min)
                    V.tensor_tensor(ECJ, g16(gi)[:, :, CHUNK - 1], GJ, ALU.subtract).then_inc(diff_ready, 1)
                    for i, m in enumerate(MS):
                        dve.wait_ge(cin_ready, u * 12 + 2 * i + 1)
                        o = convo(i).rearrange("p (b t) -> p b t", b=BPU)
                        if i == 2:
                            dve.wait_ge(bi_ready, u * 4 + 4)
                        for k in range(TAPS):
                            src = cin[:, i % 2, :, TAPS - 1 - k:TAPS - 1 - k + P]
                            w = convw[:, m, TAPS - 1 - k:TAPS - k]
                            if k == 0:
                                dc.then(V.tensor_scalar(o, src, w, None, ALU.mult))
                            elif k < TAPS - 1:
                                dc.then(V.scalar_tensor_tensor(o, src, w, o, ALU.mult, ALU.add))
                            else:
                                V.scalar_tensor_tensor(o, src, w, o, ALU.mult, ALU.add).then_inc(conv_done, 1)
                    for i, m in enumerate(MS):
                        dve.wait_ge(silu_done, u * 6 + i + 1)
                        for q in range(2):
                            dve.wait_ge(front.filled, front.full(u, ("p20", m, q)))
                            o = convo(i)[:, q * 512:(q + 1) * 512]
                            V.tensor_tensor(o, o, front["p20", m, q][:, :], ALU.add).then_inc(raw_ready, 1)
                            dve.wait_ge(raw_ready, u * 12 + 2 * i + q + 1)
                            freed_(front)
                        if m < 4:
                            dve.wait_ge(mrs_ready, u * 8 + 2 * i + 2)
                            V.tensor_tensor(kqi[:, (m % 2) * 64:(m % 2) * 64 + 64, 0 if m >= 2 else 1, :],
                                            convo(i).rearrange("p (g i) -> p g i", i=CHUNK),
                                            half(r11, 1).rearrange("p (g i) -> p g i", i=CHUNK), ALU.mult).then_inc(kq_ready, 1)
                    dve.wait_ge(sm_ready, u + 1)
                    dc.then(V.scalar_tensor_tensor(NBG, BJ, -1.0, NBG, ALU.mult, ALU.mult))
                    dve.wait_ge(fp_ready, u * 2 + 2)
                    for t in range(G // 8):
                        key = ("mm1", t)
                        dve.wait_ge(front.filled, front.full(u, key))
                        ps = front[key][:, 0:384].rearrange("p (g k i) -> p g k i", k=3, i=CHUNK)
                        gs = slice(8 * t, 8 * t + 8)
                        V.tensor_tensor(aT[:, :].rearrange("p (i g) -> p g i", i=CHUNK)[:, gs, :], ps[:, :, 0, :], g16(fA)[:, gs, :], ALU.mult)
                        V.tensor_tensor(g16(pT)[:, gs, :], ps[:, :, 1, :], g16(fP)[:, gs, :], ALU.mult)
                        V.tensor_copy(g16(kc)[:, gs, :], ps[:, :, 2, :]).then_inc(a_ready, 1)
                        dve.wait_ge(a_ready, u * 16 + t + 1)
                        freed_(front)
                    dve.wait_ge(ab_ready, u + 1)
                    aBv = aB[:, :].rearrange("p (i h j) -> p i h j", i=CHUNK, h=HPT)
                    for i in range(1, CHUNK):
                        pr = R[5][:, 0:HPT * i * i].rearrange("p (h c j) -> p h c j", h=HPT, c=i)
                        dc.then(V.tensor_tensor(pr, aBv[:, i, :, 0:i].unsqueeze(2).broadcast_to([P, HPT, i, i]),
                                                inv[:, 0:i, :, 0:i].rearrange("p j h c -> p h c j"), ALU.mult))
                        dc.then(V.tensor_reduce(inv[:, i, :, 0:i], pr, AX.X, ALU.add))
                    dve.sem_inc(inv_ready, 1)
                    for t in range(4):
                        dve.wait_ge(front.filled, front.full(u, ("v2", t)))
                        dc.then(V.tensor_tensor(g16(vbeta).rearrange("p g v -> p v g")[:, 4 * t:4 * t + 4, :],
                                                front["v2", t][:, :].rearrange("p (v g) -> p v g", v=4),
                                                BJ.unsqueeze(1).broadcast_to([P, 4, G]), ALU.mult))
                        freed_(front)
                    dve.wait_ge(tT_ready, u + 1)
                    X, Dd, Ee, Ed = (ch[:, k, :, :] for k in range(4))
                    colv = lambda t, c: t.rearrange("p (s c) -> p s c", c=NCH)[:, :, c].unsqueeze(2).broadcast_to([P, SETS, HD])
                    bps = lambda key: back[key][:, 0:SETS * HD].rearrange("p (s v) -> p s v", v=HD)
                    for c in range(NCH):
                        if c:
                            dve.wait_ge(back.filled, back.full(u, ("E", c - 1)))
                        bd(V, bdt[:, :, :], by_chunk(tT)[:, :, c, :]).then_inc(bdt_r, 1)
                        if c:
                            dve.wait_ge(back.filled, back.full(u, ("O", c - 1)))
                        bd(V, bds[:, :, :], state[:, :, :]).then_inc(bds_r, 1)
                        dve.wait_ge(back.filled, back.full(u, ("X", c)))
                        dc.then(V.tensor_tensor(X, bps(("X", c)), colv(NBG, c), ALU.mult))
                        freed_(back)
                        V.tensor_tensor(Dd, X, by_chunk(vbeta)[:, :, c, :], ALU.add).then_inc(d_ready, 1)
                        dve.wait_ge(back.filled, back.full(u, ("E", c)))
                        dc.then(V.tensor_copy(Ee, bps(("E", c))))
                        V.tensor_tensor(Ed, Ee, colv(ECJ, c), ALU.mult).then_inc(ed_ready, 1)
                        freed_(back)
                        bd(V, bde[:, :, :], Ee).then_inc(bde_r, 1)
                        dve.wait_ge(back.filled, back.full(u, ("dS", c)))
                        dc.then(V.tensor_tensor(state[:, :, :], state[:, :, :], colv(EC, c), ALU.mult))
                        dc.then(V.tensor_tensor(state[:, :, :], state[:, :, :], bps(("dS", c)), ALU.add))
                        freed_(back)
                        dve.sem_inc(st_ready, 1)
                    dve.wait_ge(ors_ready, u * 4 + 4)
                    V.tensor_tensor(R[3][:, :], R[3][:, :], orr[:, :], ALU.mult).then_inc(on_ready, 1)
                    dve.wait_ge(on_ready, u + 1)
                    dve.wait_ge(gate_ready, u + 1)
                    for b in range(BPU // 2):
                        dve.wait_ge(back.filled, back.full(u, ("proj", b)))
                        ys = y1[:, 2 * b:2 * b + 2, :]
                        dc.then(V.tensor_tensor(ys, back["proj", b][:, :].rearrange("p (b d) -> p b d", b=2),
                                                outb[:, :].unsqueeze(1).broadcast_to([P, 2, D]), ALU.add))
                        freed_(back)
                        dc.then(V.tensor_tensor(ys, ys, gate[:, 2 * b:2 * b + 2, :], ALU.mult))
                        dc.then(V.tensor_tensor(ys, ys, x[:, 2 * b:2 * b + 2, :], ALU.add))
                    for b in range(BPU):
                        ins = V.bn_stats(stats[:, b, :], y1[:, b, :])
                    dc.then(ins)
                    dve.sem_inc(passed, 1)
                    for b in range(BPU):
                        ins = V.bn_aggr(mv[:, b, :], stats[:, b, :])
                    ins.then_inc(var_ready, 1)
                    dve.wait_ge(rstd_ready, u + 1)
                    dve.wait_ge(var_ready, u + 1)
                    for b in range(BPU):
                        ins = V.tensor_scalar(y1[:, b, :], y1[:, b, :], mv[:, b, 0:1], rstd[:, b:b + 1], ALU.subtract, ALU.mult)
                    ins.then_inc(x1_ready, 1)
                    dc.end()

                def begin(grp):
                    V.memset(carry[:, :, :], 0.0)
                    V.memset(hist[:, :, :, :], 0.0)
                    V.memset(state[:, :, :], 0.0).then_inc(zeroed, 1)
                dc.per = 106
                loop(dve, body, begin)

            @block.tensor
            def _(pe):
                T = nc.tensor

                def body(u, grp, s):
                    pe.wait_ge(s_x, u * 16 + 16)
                    for q in range(2):
                        for e in range(2):
                            ps = front.take(pe, u, ("xT", q, e))
                            for j in range(4):
                                ins = T.transpose(ps[:, j * P:(j + 1) * P], x[:, 4 * q + j, :].rearrange("p (c e) -> p e c", e=2)[:, e, :], ident[:, :])
                            ins.then_inc(front.filled, 1)
                    pe.wait_ge(xT_ready, u * 4 + 4)
                    for b2 in range(BPU // 2):
                        ps = front.take(pe, u, ("gate", b2))
                        for j in range(2):
                            b = 2 * b2 + j
                            for e in range(2):
                                ins = T.matmul(ps[:, j * D:(j + 1) * D], xT[:, e, b * P:(b + 1) * P], ctrlW[:, e, 3 * D + 2 * H:], start=e == 0, stop=e == 1)
                        ins.then_inc(front.filled, 1)

                    def mm(key, mrows, parts):
                        ps = front.take(pe, u, key)
                        for k, (l, r) in enumerate(parts):
                            ins = T.matmul(ps[0:mrows, :], l, r, start=k == 0, stop=k == len(parts) - 1)
                        ins.then_inc(front.filled, 1)
                    for k, n in enumerate(("dec", "bet")):
                        for q in range(2):
                            mm((n, q), H, [(ctrlW[:, e, 3 * D + k * H:3 * D + (k + 1) * H], xT[:, e, q * 512:(q + 1) * 512]) for e in range(2)])
                    pe.wait_ge(sq_ready, u * 2 + 2)
                    for q in range(2):
                        mm(("pss", q), P, [(ones[:, :], R[4][:, e * COLS + q * 512:e * COLS + (q + 1) * 512]) for e in range(2)])
                    pe.wait_ge(gcum_ready, u + 1)
                    pe.wait_ge(bet_ready, u + 1)
                    for n, src in (("gi", gcum), ("bi", bet)):
                        for hh in range(2):
                            for q in range(2):
                                mm((n, hh, q), P, [(sel[:, hh, :], src[:, q * 512:(q + 1) * 512])])
                    for m in MS:
                        for q in range(2):
                            mm(("ctl", m, q), P, [(ctrlW[:, e, m * P:(m + 1) * P], xT[:, e, q * 512:(q + 1) * 512]) for e in range(2)])
                    pe.wait_ge(np_v, u + 1)
                    pe.wait_ge(np_p, u + 1)
                    for i, m in enumerate(MS):
                        for q in range(2):
                            mm(("p20", m, q), P, [(p20W[:, e, m * P:(m + 1) * P], npT[:, e, q * 512:(q + 1) * 512]) for e in range(2)])
                        if m < 4:
                            pe.wait_ge(msq_ready, u * 4 + i + 1)
                            for q in range(2):
                                mm(("nrm", m, q), P, [(blk[:, :], r11[:, q * 512:(q + 1) * 512])])
                    for t in range(G // 8):
                        if t % 2 == 0:
                            pe.wait_ge(bd1_ready, u * NCH + t // 2 + 1)
                        ps = front.take(pe, u, ("mm1", t))
                        for j in range(8):
                            ins = T.matmul(ps[:, j * 48:(j + 1) * 48], bdk[:, (t // 2) % 2, 8 * (t % 2) + j, :],
                                           kqi[:, 8 * t + j, :, :].rearrange("p k i -> p (k i)"), start=True, stop=True)
                        ins.then_inc(front.filled, 1)
                        if t % 2:
                            pe.wait_ge(front.filled, front.full(u, ("mm1", t)))
                            pe.sem_inc(bd1_used, 1)
                    for t in range(4):
                        ps = front.take(pe, u, ("v1", t))
                        for j in range(4):
                            ins = T.transpose(ps[:, j * P:(j + 1) * P], g16(vT)[:, :, 4 * t + j], ident[:, :])
                        ins.then_inc(front.filled, 1)
                    pe.wait_ge(vb_ready, u + 1)
                    for t in range(4):
                        ps = front.take(pe, u, ("aT", t))
                        for j in range(4):
                            i = 4 * t + j
                            ins = T.transpose(ps[:, j * P:(j + 1) * P], aT[:, i * P:(i + 1) * P], ident[:, :])
                        ins.then_inc(front.filled, 1)
                    for t in range(4):
                        ps = front.take(pe, u, ("v2", t))
                        for j in range(4):
                            v = 4 * t + j
                            ins = T.transpose(ps[:, j * P:(j + 1) * P], vB[:, v * P:(v + 1) * P], ident[:, :])
                        ins.then_inc(front.filled, 1)
                    pe.wait_ge(inv_ready, u + 1)
                    for t in range(4):
                        ps = front.take(pe, u, ("tT", t))
                        for j in range(4):
                            i = 4 * t + j
                            ins = T.transpose(ps[:, j * P:(j + 1) * P], inv[:, i, :, :].rearrange("p h c -> p (h c)"), ident[:, :])
                        ins.then_inc(front.filled, 1 + (front.pads if t == 3 else 0))
                    Xs, Dd, Ee, Ed = (ch[:, k, :, :] for k in range(4))
                    for c in range(NCH):
                        ps = back.take(pe, u, ("X", c))
                        pe.wait_ge(bdk_r, u * NCH + c + 1)
                        if c:
                            pe.wait_ge(st_ready, u * NCH + c)
                        for k in range(SETS):
                            ins = T.matmul(ps[:, k * HD:(k + 1) * HD], bdk[:, c % 2, k, :], state[:, k, :], start=True, stop=True)
                        ins.then_inc(back.filled, 1)
                        ps = back.take(pe, u, ("E", c))
                        pe.wait_ge(bdt_r, u * NCH + c + 1)
                        pe.wait_ge(d_ready, u * NCH + c + 1)
                        for k in range(SETS):
                            ins = T.matmul(ps[:, k * HD:(k + 1) * HD], bdt[:, k, :], Dd[:, k, :], start=True, stop=True)
                        ins.then_inc(back.filled, 1)
                        ps = back.take(pe, u, ("dS", c))
                        pe.wait_ge(bdc_r, u * NCH + c + 1)
                        pe.wait_ge(ed_ready, u * NCH + c + 1)
                        for k in range(SETS):
                            ins = T.matmul(ps[:, k * HD:(k + 1) * HD], bdc[:, k, :], Ed[:, k, :], start=True, stop=True)
                        ins.then_inc(back.filled, 1)
                        ps = back.take(pe, u, ("O", c))
                        pe.wait_ge(bds_r, u * NCH + c + 1)
                        pe.wait_ge(bde_r, u * NCH + c + 1)
                        for k in range(SETS):
                            T.matmul(ps[:, k * HD:(k + 1) * HD], bds[:, k, :], by_chunk(gq)[:, k, c, :], start=True, stop=False)
                            ins = T.matmul(ps[:, k * HD:(k + 1) * HD], bde[:, k, :], by_chunk(pT)[:, k, c, :], start=False, stop=True)
                        ins.then_inc(back.filled, 1)
                    pe.wait_ge(osq_ready, u + 1)
                    for hh in range(2):
                        for q in range(2):
                            ps = back.take(pe, u, ("on", hh, q))
                            T.matmul(ps[:, :], blk[:, :], osq[:, hh * COLS + q * 512:hh * COLS + (q + 1) * 512], start=True, stop=True).then_inc(back.filled, 1)
                    pe.wait_ge(on_ready, u + 1)
                    for b2 in range(BPU // 2):
                        ps = back.take(pe, u, ("proj", b2))
                        for j in range(2):
                            b = 2 * b2 + j
                            for k in range(4):
                                src = oT if k < 2 else npT
                                ins = T.matmul(ps[:, j * D:(j + 1) * D], src[:, k % 2, b * P:(b + 1) * P], outW[:, k, :], start=k == 0, stop=k == 3)
                        ins.then_inc(back.filled, 1)
                    pe.wait_ge(x1_ready, u + 1)
                    for b2 in range(BPU // 2):
                        ps = back.take(pe, u, ("x1T", b2))
                        for j in range(4):
                            ins = T.transpose(ps[:, j * P:(j + 1) * P], y1[:, 2 * b2 + j // 2, (j % 2) * P:(j % 2 + 1) * P], ident[:, :])
                        ins.then_inc(back.filled, 1)
                    pe.wait_ge(x1T_ready, u * 4 + 4)
                    ps = back.take(pe, u, ("lg", 0))
                    for b in range(BPU):
                        for k in range(2):
                            ins = T.matmul(ps[:, b * E:(b + 1) * E], x1T[:, (2 * b + k) * P:(2 * b + k + 1) * P], wgs[:, k, :], start=k == 0, stop=k == 1)
                    ins.then_inc(back.filled, 1 + back.pads)
                pe.wait_ge(s_ready, 1)
                loop(pe, body)


def route(nc, keep, ident, ones, banks, idx, slot, wk):
    ctx = ExitStack()
    with ctx:
        def sb(name, *shape, dt=F32):
            return ctx.enter_context(nc.sbuf_tensor(name, list(shape), dt))

        def sem(name):
            return ctx.enter_context(nc.semaphore(name))
        TE = TILES * E
        tri = sb("tri", P, P)
        pr = sb("probs", P, TILES, E)
        cand = sb("cand", P, TILES, E)
        rank = sb("rank", P, TILES, E)
        expert = sb("expert_id", P, TILES, E)
        oh = sb("one_hot", P, TOPK, TILES, E)
        tot = sb("totals", P, TOPK, E, TILES)
        run = sb("running", P, TOPK, E, TILES)
        again = sb("restart_at_tile0", P, E, TILES)
        pos = sb("positions", P, TOPK, TILES, E)
        m = sb("per_token", P, 8, TILES)
        own = sb("own_position", P, TOPK, TILES)
        kept = sb("kept", P, TOPK, TILES)
        row = sb("row_in_tile", P, TOPK, TILES)
        tile_ = sb("slot_tile", P, TOPK, TILES)
        ints = sb("ints", P, 3, TOPK * TILES, dt=I32)
        ramp_i = sb("ramp_int", P, TILES * E, dt=I32)
        token = sb("token_id", P, TILES)
        cols_r = sb("cols128", P, P)
        cols_b = sb("cols_blocks", P, BLKS)
        UN = 4
        ohr = sb("row_one_hot", P, UN * TOPK, P)
        rb = sb("tile_one_hot", P, UN * TOPK, BLKS)
        zero = sb("zeros", P, BLKS)
        steps, consts = sem("route_steps"), sem("route_consts")
        exped, cums, lists, used, listed = sem("exped"), sem("cums"), sem("list_operands"), sem("list_used"), sem("listed")
        ramp_used = sem("ramp_used")
        score = keep[:, :, :, :].rearrange("p b s e -> p (b s) e")
        with nc.Block() as block:
            @block.gpsimd
            def _(pool):
                pool.memset(tri[:, :], 1.0).then_inc(consts, 1)
                pool.wait_ge(consts, 1)
                pool.affine_select(out=tri[:, :], in_=tri[:, :], compare_op=ALU.is_ge, fill=0.0, base=0,
                                   pattern=[[1, P]], channel_multiplier=-1).then_inc(consts, 1)
                for k, (pattern, base, mult, width) in enumerate((
                        ([[0, TILES], [-1, E]], E, 0, TE), ([[0, TILES], [1, E]], 0, 0, TE),
                        ([[P, TILES]], 0, 1, TILES), ([[1, P]], 0, 0, P), ([[1, BLKS]], 0, 0, BLKS))):
                    if k:
                        pool.wait_ge(ramp_used, k)
                    pool.iota(ramp_i[:, 0:width], pattern=pattern, base=base, channel_multiplier=mult).then_inc(consts, 1)

            @block.scalar
            def _(act):
                act.wait_ge(steps, 2)
                nc.scalar.activation(pr[:, :, :], pr[:, :, :], ACT.Exp).then_inc(exped, 1)

            @block.vector
            def _(dve):
                V = nc.vector
                st = Steps(dve, steps, 0)
                st.start(0)
                bc = lambda t: t.unsqueeze(2).broadcast_to([P, TILES, E])
                flat = lambda t: t[:, :, :].rearrange("p t e -> p (t e)")
                st.then(V.tensor_reduce(m[:, 0, :], score, AX.X, ALU.max))
                st.then(V.tensor_tensor(pr[:, :, :], score, bc(m[:, 0, :]), ALU.subtract))
                for k, (dst, width) in enumerate(((flat(rank), TE), (flat(expert), TE), (token[:, :], TILES), (cols_r[:, :], P), (cols_b[:, :], BLKS))):
                    dve.wait_ge(consts, 3 + k)
                    V.tensor_copy(dst, ramp_i[:, 0:width]).then_inc(ramp_used, 1)
                V.memset(again[:, :, :], 1.0)
                V.memset(zero[:, :], 0.0)
                dve.wait_ge(ramp_used, 5)
                dve.wait_ge(exped, 1)
                st.then(V.tensor_reduce(m[:, 0, :], pr[:, :, :], AX.X, ALU.add))
                st.then(V.reciprocal(m[:, 0, :], m[:, 0, :]))
                V.memset(again[:, :, 0:1], 0.0)
                st.then(V.tensor_tensor(pr[:, :, :], pr[:, :, :], bc(m[:, 0, :]), ALU.mult))
                for k in range(TOPK):
                    st.then(V.tensor_reduce(m[:, 1 + k, :], pr[:, :, :], AX.X, ALU.max))
                    st.then(V.tensor_tensor(cand[:, :, :], pr[:, :, :], bc(m[:, 1 + k, :]), ALU.is_equal))
                    st.then(V.tensor_tensor(cand[:, :, :], cand[:, :, :], rank[:, :, :], ALU.mult))
                    st.then(V.tensor_reduce(m[:, 3, :], cand[:, :, :], AX.X, ALU.max))
                    st.then(V.tensor_tensor(oh[:, k, :, :], cand[:, :, :], bc(m[:, 3, :]), ALU.is_equal))
                    if k == 0:
                        st.then(V.scalar_tensor_tensor(flat(pr), oh[:, k, :, :].rearrange("p t e -> p (t e)"), -2.0, flat(pr), ALU.mult, ALU.add))
                dve.sem_inc(listed, 1)
                st.then(V.tensor_tensor(m[:, 4, :], m[:, 1, :], m[:, 2, :], ALU.add))
                st.then(V.tensor_scalar(m[:, 4, :], m[:, 4, :], EPS_GATE, None, ALU.max))
                st.then(V.reciprocal(m[:, 4, :], m[:, 4, :]))
                dve.wait_ge(cums, 8)
                for k in range(TOPK):
                    for q in range(2):
                        V.tensor_copy(tot[:, k, :, :].rearrange("p e t -> p t e")[:, q * 64:(q + 1) * 64, :],
                                      banks[4 + 2 * k + q][:, :].rearrange("p (t e) -> p t e", e=E))
                        ins = V.tensor_scalar(pos[:, k, q * 64:(q + 1) * 64, :], banks[2 * k + q][:, :].rearrange("p (t e) -> p t e", e=E), -1.0, None, ALU.add)
                    st.then(ins)
                for k in range(TOPK):
                    fl = lambda t: t.rearrange("p e t -> p (e t)")
                    st.then(V.tensor_tensor_scan(fl(run[:, k, :, :]), fl(again[:, :, :]), fl(tot[:, k, :, :]), 0.0, ALU.mult, ALU.add))
                    st.then(V.tensor_tensor(tot[:, k, :, :], run[:, k, :, :], tot[:, k, :, :], ALU.subtract))
                    if k:
                        st.then(V.tensor_tensor(tot[:, k, :, :], tot[:, k, :, :], run[:, 0, :, TILES - 1:TILES].broadcast_to([P, E, TILES]), ALU.add))
                    pk = pos[:, k, :, :]
                    st.then(V.tensor_tensor(pk, pk, tot[:, k, :, :].rearrange("p e t -> p t e"), ALU.add))
                    st.then(V.tensor_tensor(cand[:, :, :], pk, oh[:, k, :, :], ALU.mult))
                    st.then(V.tensor_reduce(own[:, k, :], cand[:, :, :], AX.X, ALU.add))
                    st.then(V.tensor_tensor(cand[:, :, :], expert[:, :, :], oh[:, k, :, :], ALU.mult))
                    st.then(V.tensor_reduce(m[:, 5, :], cand[:, :, :], AX.X, ALU.add))
                    st.then(V.tensor_scalar(kept[:, k, :], own[:, k, :], float(CAP), None, ALU.is_lt))
                    st.then(V.scalar_tensor_tensor(own[:, k, :], m[:, 5, :], float(CAP), own[:, k, :], ALU.mult, ALU.add))
                    st.then(V.tensor_tensor(m[:, 6, :], own[:, k, :], kept[:, k, :], ALU.mult))
                    V.tensor_copy(slot[:, :, k], m[:, 6, :])
                    st.then(V.tensor_copy(ints[:, 0, k * TILES:(k + 1) * TILES], m[:, 6, :]))
                    st.then(V.tensor_tensor(m[:, 7, :], m[:, 1 + k, :], m[:, 4, :], ALU.mult))
                    st.then(V.tensor_tensor(wk[:, k, :], m[:, 7, :], kept[:, k, :], ALU.mult))
                V.tensor_scalar(ints[:, 1, :], ints[:, 0, :], P - 1, None, ALU.bitwise_and)
                st.then(V.tensor_scalar(ints[:, 2, :], ints[:, 0, :], P.bit_length() - 1, None, ALU.logical_shift_right))
                f2 = lambda t: t[:, :, :].rearrange("p k t -> p (k t)")
                V.tensor_copy(f2(row), ints[:, 1, :])
                V.tensor_scalar(f2(kept), f2(kept), -float(BLKS), float(BLKS), ALU.mult, ALU.add)
                st.then(V.tensor_copy(f2(tile_), ints[:, 2, :]))
                st.then(V.tensor_tensor(f2(tile_), f2(tile_), f2(kept), ALU.add))
                dve.sem_inc(used, UN * TOPK)
                with dve.Fori(0, TILES // UN) as i:
                    for t in range(UN):
                        for k in range(TOPK):
                            n = t * TOPK + k
                            col = bass.ds(i * UN + t, 1)
                            dve.wait_ge(used, i * (UN * TOPK) + n + 1)
                            V.tensor_scalar(ohr[:, n, :], cols_r[:, :], row[:, k, col], None, ALU.is_equal)
                            V.tensor_scalar(rb[:, n, :], cols_b[:, :], tile_[:, k, col], token[:, col], ALU.is_equal, ALU.mult).then_inc(lists, 1)
                dve.wait_ge(cums, 9)
                V.tensor_copy(idx[:, :], banks[0][:, 0:BLKS])
                st.per = st.k

            @block.tensor
            def _(pe):
                pe.wait_ge(consts, 2)
                pe.wait_ge(listed, 1)
                for k in range(TOPK):
                    for q in range(2):
                        rhs = oh[:, k, q * 64:(q + 1) * 64, :].rearrange("p t e -> p (t e)")
                        nc.tensor.matmul(banks[2 * k + q][:, :], tri[:, :], rhs, start=True, stop=True).then_inc(cums, 1)
                        nc.tensor.matmul(banks[4 + 2 * k + q][:, :], ones[:, :], rhs, start=True, stop=True).then_inc(cums, 1)
                pe.wait_ge(lists, 1)
                nc.tensor.matmul(banks[0][:, 0:BLKS], zero[:, 0:P], zero[:, :], start=True, stop=False)
                with pe.Fori(0, TILES // UN) as i:
                    for n in range(UN * TOPK):
                        pe.wait_ge(lists, i * (UN * TOPK) + n + 1)
                        nc.tensor.matmul(banks[0][:, 0:BLKS], ohr[:, n, :], rb[:, n, :], start=False, stop=False).then_inc(used, 1)
                nc.tensor.matmul(banks[0][:, 0:BLKS], zero[:, 0:P], zero[:, :], start=False, stop=True).then_inc(cums, 1)


def experts(nc, x1d, yd, w1, b1, w2, b2, idx, ident, banks):
    ctx = ExitStack()
    with ctx:
        def sb(name, *shape, dt=F32):
            return ctx.enter_context(nc.sbuf_tensor(name, list(shape), dt))

        def sem(name):
            return ctx.enter_context(nc.semaphore(name))
        MT = HID // P
        BPE = CAP // (P * SPB)
        W = SPB * P
        w1s, w2s = sb("w1s", P, 2, 2, HID), sb("w2s", P, 2, MT, D)
        b2s = sb("b2s", P, 2, D)
        b1e = sb("b1_expert", P, 2, MT)
        b1r, b1t = sb("b1_rows", E * MT, P), sb("b1_cols", P, E * MT)
        icur = sb("block_index", P, 2, SPB, dt=U32)
        xg = sb("gathered_rows", P, 2, SPB, D)
        xgT = sb("gathered_T", P, 2, 2, W)
        hT = sb("hidden_T", P, 2, MT, W)
        ysb = sb("result_rows", P, 2, SPB, D)
        w_loaded, b_loaded, expert_done = sem("w_loaded"), sem("b_loaded"), sem("expert_done")
        idx_ready, xg_used = sem("idx_ready"), sem("xg_used")
        gathered = [sem(f"gathered{i}") for i in range(2)]
        xgT_ready, hT_ready, y_ready = sem("xgT_ready"), sem("hT_ready"), sem("y_ready")
        y_stored = [sem(f"y_stored{i}") for i in range(2)]
        filled, b1_ready, b1_cur, passed = sem("filled"), sem("b1_ready"), sem("b1_cur"), sem("wait_passed2")
        freed = {w: sem(f"freed_by_{w}") for w in ("act", "dve")}
        order = []
        for j in range(2):
            order += [(("xT", j, k), "dve") for k in range(2)]
            order += [(("h", j, m), "act") for m in range(MT)]
            order += [(("y", j, t), "dve") for t in range(SPB // 2)]
        ring = Bank(order, banks, filled, freed)

        def loop(eng, body, begin=None, end=None):
            with eng.Fori(0, E // 2) as e2:
                for par in range(2):
                    e = e2 * 2 + par
                    if begin is not None:
                        begin(e, par)
                    with eng.Fori(0, BPE // 2) as j2:
                        for j in range(2):
                            pair = e * (BPE // 2) + j2
                            body(e, par, pair, pair * 2 + j, j)
                    if end is not None:
                        end(e)

        with nc.Block() as block:
            @block.sync
            def _(sp):
                sp.dma_start(b1r[:, :], b1.rearrange("e (m p) -> (e m) p", p=P)).then_inc(b_loaded, 16)

                def body(e, par, pair, n, j):
                    sp.wait_ge(y_ready, n * 2 + 2)
                    sp.dma_start(yd.rearrange("(n i p) d -> p n i d", i=SPB, p=P)[:, bass.ds(n, 1), :, :],
                                 ysb[:, j:j + 1, :, :]).then_inc(y_stored[j], 16)
                loop(sp, body)
                for j in range(2):
                    sp.wait_ge(y_stored[j], 16 * (E * BPE // 2 + 1))

            @block.gpsimd
            def _(pool):
                def begin(e, par):
                    pool.wait_ge(expert_done, e + 1)
                    pool.dma_start(w1s[:, par:par + 1, :, :], w1[bass.ds(e, 1), :, :].rearrange("e (k p) n -> p e k n", p=P)).then_inc(w_loaded, 16)
                    pool.dma_start(w2s[:, par:par + 1, :, :], w2[bass.ds(e, 1), :, :].rearrange("e (k p) n -> p e k n", p=P)).then_inc(w_loaded, 16)
                    pool.dma_start(b2s[:, par, :], b2[bass.ds(e, 1), :].broadcast_to([P, D])).then_inc(w_loaded, 16)

                def body(e, par, pair, n, j):
                    pool.wait_ge(idx_ready, n + 1)
                    pool.wait_ge(xg_used, n + 1)
                    pool.sem_inc(passed, 1)
                    for i in range(SPB):
                        nc.gpsimd.indirect_dma_start(out=xg[:, j, i, :], out_offset=None, in_=x1d[:, :],
                                                     in_offset=bass.IndirectOffsetOnAxis(ap=icur[:, j, i:i + 1], axis=0)).then_inc(gathered[j], 16)
                loop(pool, body, begin)

            @block.vector
            def _(dve):
                V = nc.vector
                dve.sem_inc(xg_used, 2)
                for j in range(2):
                    dve.sem_inc(y_stored[j], 16)
                dve.sem_inc(ring.freed["dve"], ring.count["dve"])

                def body(e, par, pair, n, j):
                    dve.wait_ge(w_loaded, e * 48 + 48)
                    V.tensor_copy(icur[:, j, :], idx[:, bass.ds(n * SPB, SPB)]).then_inc(idx_ready, 1)
                    for k in range(2):
                        dve.wait_ge(filled, ring.full(pair, ("xT", j, k)))
                        V.tensor_copy(xgT[:, j, k, :], ring["xT", j, k][:, :]).then_inc(xgT_ready, 1)
                        dve.wait_ge(xgT_ready, n * 2 + k + 1)
                        dve.sem_inc(ring.freed["dve"], 1)
                    dve.sem_inc(xg_used, 1)
                    dve.wait_ge(y_stored[j], pair * 16 + 16)
                    for t in range(SPB // 2):
                        dve.wait_ge(filled, ring.full(pair, ("y", j, t)))
                        V.tensor_tensor(ysb[:, j, 2 * t:2 * t + 2, :], ring["y", j, t][:, :].rearrange("p (i d) -> p i d", i=2),
                                        b2s[:, par:par + 1, :].broadcast_to([P, 2, D]), ALU.add).then_inc(y_ready, 1)
                        dve.wait_ge(y_ready, n * 2 + t + 1)
                        dve.sem_inc(ring.freed["dve"], 1)
                loop(dve, body)

            @block.scalar
            def _(act):
                act.sem_inc(ring.freed["act"], ring.count["act"])
                act.wait_ge(b1_ready, 1)
                nc.scalar.activation(b1t[:, :], banks[7][:, 0:E * MT], ACT.Copy).then_inc(b1_ready, 1)
                act.wait_ge(b1_ready, 2)

                def begin(e, par):
                    nc.scalar.activation(b1e[:, par, :], b1t[:, bass.ds(e * MT, MT)], ACT.Copy).then_inc(b1_cur, 1)

                def body(e, par, pair, n, j):
                    act.wait_ge(b1_cur, e + 1)
                    for m in range(MT):
                        act.wait_ge(filled, ring.full(pair, ("h", j, m)))
                        nc.scalar.activation(hT[:, j, m, :], ring["h", j, m][:, :], ACT.Gelu,
                                             bias=b1e[:, par, m:m + 1]).then_inc(hT_ready, 1)
                        act.wait_ge(hT_ready, n * MT + m + 1)
                        act.sem_inc(ring.freed["act"], 1)
                loop(act, body, begin)

            @block.tensor
            def _(pe):
                pe.sem_inc(expert_done, 2)
                pe.wait_ge(b_loaded, 16)
                nc.tensor.transpose(banks[7][:, 0:E * MT], b1r[:, :], ident[0:E * MT, 0:E * MT]).then_inc(b1_ready, 1)
                pe.wait_ge(b1_ready, 2)

                def body(e, par, pair, n, j):
                    pe.wait_ge(w_loaded, e * 48 + 48)
                    pe.wait_ge(gathered[j], pair * (16 * SPB) + 16 * SPB)
                    for k in range(2):
                        ps = ring.take(pe, pair, ("xT", j, k))
                        for i in range(SPB):
                            ins = nc.tensor.transpose(ps[:, i * P:(i + 1) * P], xg[:, j, i, k * P:(k + 1) * P], ident[:, :])
                        ins.then_inc(filled, 1)
                    pe.wait_ge(xgT_ready, n * 2 + 2)
                    for m in range(MT):
                        ps = ring.take(pe, pair, ("h", j, m))
                        for k in range(2):
                            ins = nc.tensor.matmul(ps[:, :], w1s[:, par, k, m * P:(m + 1) * P], xgT[:, j, k, :], start=k == 0, stop=k == 1)
                        ins.then_inc(filled, 1)
                    for t in range(SPB // 2):
                        ps = ring.take(pe, pair, ("y", j, t))
                        for i in range(2):
                            for m in range(MT):
                                if t == 0 and i == 0:
                                    pe.wait_ge(hT_ready, n * MT + m + 1)
                                s0 = (2 * t + i) * P
                                ins = nc.tensor.matmul(ps[:, i * D:(i + 1) * D], hT[:, j, m, s0:s0 + P], w2s[:, par, m, :], start=m == 0, stop=m == MT - 1)
                        ins.then_inc(filled, 1)

                def end(e):
                    pe.wait_ge(filled, e * (BPE // 2 * len(order)) + BPE // 2 * len(order))
                    pe.sem_inc(expert_done, 1)
                loop(pe, body, end=end)


def combine(nc, x1d, yd, slot, wk, out):
    ctx = ExitStack()
    with ctx:
        def sb(name, *shape, dt=F32):
            return ctx.enter_context(nc.sbuf_tensor(name, list(shape), dt))

        def sem(name):
            return ctx.enter_context(nc.semaphore(name))
        Q = 4
        NB = 2
        xs, ys = sb("x1_rows_sb", P, NB, Q, D), sb("y_rows_sb", P, NB, Q * TOPK, D)
        o = sb("out_rows", P, NB, Q, D)
        scur = sb("turn_slots", P, NB, Q * TOPK, dt=U32)
        stats, mv, rstd = sb("stats2", P, NB, Q, 6), sb("mv2", P, NB, Q, 2), sb("rstd2", P, NB, Q)
        eps = sb("eps2", P, 1)
        x_loaded = [sem(f"x1_loaded{i}") for i in range(NB)]
        y_loaded = [sem(f"y_loaded{i}") for i in range(NB)]
        scur_ready, used, var_ready, rstd_ready = sem("scur_ready"), sem("rows_used"), sem("var_ready2"), sem("rstd_ready2")
        passed = sem("wait_passed3")
        lns, out_ready, stored, steps = sem("ln_done"), sem("out_ready"), [sem(f"out_stored{i}") for i in range(NB)], sem("combine_steps")
        TURNS = TILES // Q
        STEPS = 1 + TOPK

        def loop(eng, body):
            with eng.Fori(0, TURNS // NB) as i:
                for j in range(NB):
                    body(i * NB + j, i, j)

        rows = lambda t: t.rearrange("(q i p) d -> p q i d", p=P, i=Q)
        with nc.Block() as block:
            @block.sync
            def _(sp):
                def load(n, i, j):
                    sp.wait_ge(used, n + 1)
                    sp.dma_start(xs[:, j:j + 1, :, :], rows(x1d)[:, bass.ds(n, 1), :, :]).then_inc(x_loaded[j], 16)
                loop(sp, load)

            @block.gpsimd
            def _(pool):
                def body(n, i, j):
                    pool.wait_ge(scur_ready, n + 1)
                    pool.wait_ge(used, n + 1)
                    pool.sem_inc(passed, 1)
                    for k in range(Q * TOPK):
                        nc.gpsimd.indirect_dma_start(out=ys[:, j, k, :], out_offset=None, in_=yd[:, :],
                                                     in_offset=bass.IndirectOffsetOnAxis(ap=scur[:, j, k:k + 1], axis=0)).then_inc(y_loaded[j], 16)
                loop(pool, body)

            @block.scalar
            def _(act):
                def body(n, i, j):
                    act.wait_ge(var_ready, n + 2)
                    nc.scalar.activation(rstd[:, j, :], mv[:, j, :, 1], ACT.Ln, bias=eps[:, 0:1]).then_inc(lns, 1)
                    act.wait_ge(lns, n + 1)
                    nc.scalar.activation(rstd[:, j, :], rstd[:, j, :], ACT.Exp, scale=-0.5).then_inc(rstd_ready, 1)
                    act.wait_ge(out_ready, n + 1)
                    act.dma_start(rows(out)[:, bass.ds(n, 1), :, :], o[:, j:j + 1, :, :]).then_inc(stored[j], 16)
                loop(act, body)
                for j in range(NB):
                    act.wait_ge(stored[j], 16 * (TURNS // NB + 1))

            @block.vector
            def _(dve):
                V = nc.vector
                V.memset(eps[:, :], EPS_LN).then_inc(var_ready, 1)
                dve.sem_inc(used, NB)
                for j in range(NB):
                    dve.sem_inc(stored[j], 16)
                dve.wait_ge(var_ready, 1)
                sl = slot[:, :, :].rearrange("p t k -> p (t k)")

                def body(n, i, j):
                    V.tensor_copy(scur[:, j, :], sl[:, bass.ds(n * (Q * TOPK), Q * TOPK)]).then_inc(scur_ready, 1)
                    dve.wait_ge(x_loaded[j], i * 16 + 16)
                    dve.wait_ge(y_loaded[j], i * (16 * Q * TOPK) + 16 * Q * TOPK)
                    dve.wait_ge(stored[j], i * 16 + 16)
                    for k in range(TOPK):
                        for q in range(Q):
                            ins = V.scalar_tensor_tensor(o[:, j, q, :], ys[:, j, q * TOPK + k, :], wk[:, k, bass.ds(n * Q + q, 1)],
                                                         xs[:, j, q, :] if k == 0 else o[:, j, q, :], ALU.mult, ALU.add)
                        ins.then_inc(steps, 1)
                        dve.wait_ge(steps, n * STEPS + k + 1)
                    dve.sem_inc(used, 1)
                    for q in range(Q):
                        ins = V.bn_stats(stats[:, j, q, :], o[:, j, q, :])
                    ins.then_inc(steps, 1)
                    dve.wait_ge(steps, n * STEPS + TOPK + 1)
                    dve.sem_inc(passed, 1)
                    for q in range(Q):
                        ins = V.bn_aggr(mv[:, j, q, :], stats[:, j, q, :])
                    ins.then_inc(var_ready, 1)
                    dve.wait_ge(rstd_ready, n + 1)
                    dve.wait_ge(var_ready, n + 2)
                    for q in range(Q):
                        ins = V.tensor_scalar(o[:, j, q, :], o[:, j, q, :], mv[:, j, q, 0:1], rstd[:, j, q:q + 1], ALU.subtract, ALU.mult)
                    ins.then_inc(out_ready, 1)
                loop(dve, body)


_INS = ["L0_attn_hidden", "L0_attn_p20_decay_log", "L0_attn_p20_theta", "L0_attn_ctrl_W", "L0_attn_ctrl_b",
        "L0_attn_p20c_W", "L0_attn_qconv_w", "L0_attn_kconv_w", "L0_attn_vconv_w", "L0_attn_mnorm_scale",
        "L0_attn_vnorm_scale", "L0_attn_ramp_logit", "L0_attn_out_W", "L0_attn_out_b", "L0_ffn_wg",
        "L0_ffn_w1", "L0_ffn_b1", "L0_ffn_w2", "L0_ffn_b2"]


def kernel(**inputs):
    import numpy as _np
    import concourse.bacc as _bacc
    from concourse import mybir as _mybir
    from concourse.bass_utils import run_bass_kernel_spmd as _run

    nc = _bacc.Bacc("TRN2", target_bir_lowering=False, num_devices=1)
    arrays, args = {}, []
    for name in _INS:
        a = _np.ascontiguousarray(inputs[name])
        arrays[name] = a
        args.append(nc.dram_tensor(name, a.shape, _mybir.dt.from_np(a.dtype), kind="ExternalInput").ap())
    out = nc.dram_tensor("out", (B, S, D), F32, kind="ExternalOutput").ap()
    build(nc, *args, out)
    r = _run(nc, [arrays], core_ids=[0])
    return r.results[0]["out"]
```

```python
import numpy as np
import concourse.bass as bass
from concourse import mybir
from contextlib import ExitStack

F32 = mybir.dt.float32
I32 = mybir.dt.int32
U32 = mybir.dt.uint32
ALU = mybir.AluOpType
ACT = mybir.ActivationFunctionType
AX = mybir.AxisListType

P = 128
B, S, D, H = 16, 1024, 256, 16
HD = D // H
TAPS = 4
CHUNK = 16
HPT = P // HD
E, TOPK, HID = 8, 2, 1024
N = B * S
CAP = -(-TOPK * N // E)
BPU = 4
GROUPS = B // BPU
SLABS = S // P
COLS = BPU * P
NCH = P // CHUNK
SETS = 2 * BPU
G = SETS * NCH
TILES = N // P
BLKS = E * CAP // P
SPB = 4
TILE = 32
PAIRS = [slice(r, r + TILE) for r in range(0, P, TILE)]
FA_STEPS, BA_STEPS, FD_STEPS, BD_STEPS = 25, 14, 62, 23
EPS_RMS, EPS_LN, EPS_GATE = 1e-6, 1e-5, 1e-9
TWO_PI = 2.0 * np.pi


class Bank:

    def __init__(self, order, banks, filled, freed):
        self.order, self.banks, self.filled, self.freed = order, banks, filled, freed
        self.at = {key: i for i, (key, _) in enumerate(order)}
        assert len(self.at) == len(order) and len(order) % len(banks) == 0
        self.count = {w: sum(o == w for _, o in order) for w in freed}
        self.nth, seen = [], {w: 0 for w in freed}
        for _, w in order:
            seen[w] += 1
            self.nth.append(seen[w])
        self.pads = sum(key[0] == "pad" for key, _ in order)
        self.said = 0

    def __getitem__(self, key):
        return self.banks[self.at[key] % len(self.banks)]

    def full(self, u, key):
        return u * len(self.order) + self.at[key] + 1

    def take(self, pe, u, key):
        i = self.at[key]
        assert i == self.said % len(self.order), (key, self.order[self.said % len(self.order)])
        self.said += 1
        if self.said == len(self.order) - self.pads:
            self.said = 0
        j = i - len(self.banks)
        who = self.order[j][1]
        value = u * self.count[who] + self.nth[j] + (self.count[who] if j >= 0 else 0)
        pe.wait_ge(self.freed[who], value)
        return self[key]


class Steps:

    def __init__(self, eng, sem, per):
        self.eng, self.sem, self.per, self.k = eng, sem, per, 0

    def start(self, u):
        self.u, self.k = u, 0

    def then(self, ins):
        self.k += 1
        ins.then_inc(self.sem, 1)
        self.eng.wait_ge(self.sem, self.u * self.per + self.k)

    def end(self):
        assert self.k == self.per, (self.k, self.per)


def build(nc, hidden, decay_log, theta, ctrl_W, ctrl_b, p20c_W, qconv, kconv, vconv, mnorm, vnorm,
          ramp, out_W, out_b, wg, w1, b1, w2, b2, out, units=GROUPS * SLABS, stage=9):
    ctx = ExitStack()
    with ctx:
        x1d = nc.dram_tensor("x1_rows", [N, D], F32, kind="Internal").ap()
        yd = nc.dram_tensor("expert_rows", [E * CAP, D], F32, kind="Internal").ap()
        keep = ctx.enter_context(nc.sbuf_tensor("router_scores", [P, B, SLABS, E], F32))
        ident = ctx.enter_context(nc.sbuf_tensor("ident", [P, P], F32))
        ones = ctx.enter_context(nc.sbuf_tensor("ones", [P, P], F32))
        banks = [ctx.enter_context(nc.psum_tensor(f"bank{i}", [P, 512], F32)) for i in range(8)]
        attention(nc, hidden, decay_log, theta, ctrl_W, ctrl_b, p20c_W, qconv, kconv, vconv, mnorm,
                  vnorm, ramp, out_W, out_b, wg, x1d, keep, ident, ones, banks, units)
        if stage < 2:
            return
        idx = ctx.enter_context(nc.sbuf_tensor("slot_token", [P, BLKS], U32))
        slot = ctx.enter_context(nc.sbuf_tensor("token_slot", [P, TILES, TOPK], U32))
        wk = ctx.enter_context(nc.sbuf_tensor("token_weight", [P, TOPK, TILES], F32))
        route(nc, keep, ident, ones, banks, idx, slot, wk)
        if stage < 3:
            return
        experts(nc, x1d, yd, w1, b1, w2, b2, idx, ident, banks)
        combine(nc, x1d, yd, slot, wk, out.rearrange("b t d -> (b t) d"))


def attention(nc, hidden, decay_log, theta, ctrl_W, ctrl_b, p20c_W, qconv, kconv, vconv, mnorm,
              vnorm, ramp, out_W, out_b, wg, x1d, keep, ident, ones, banks, units):
    ctx = ExitStack()
    with ctx:
        def sb(name, *shape, dt=F32):
            return ctx.enter_context(nc.sbuf_tensor(name, list(shape), dt))

        def sem(name):
            return ctx.enter_context(nc.semaphore(name))

        ctrlW = sb("ctrlW", P, 2, 3 * D + 2 * H + D)
        p20W = sb("p20W", P, 2, 3 * D)
        outW = sb("outW", P, 4, D)
        wgs = sb("wgs", P, 2, E)
        cb = sb("ctrl_bias", P, 6)
        gb = sb("gate_bias", H, 2)
        convw = sb("convw", P, 6, TAPS)
        mn = sb("mn", P, 1)
        vn = sb("vn", P, 2)
        outb = sb("outb_rows", P, D)
        gateb = sb("gateb_rows", P, D)
        blk = sb("head_blocks", P, P)
        hmask = sb("head_mask", P, HPT)
        pmask = sb("pair_mask", P, 2)
        diag = sb("diag16", P, CHUNK)
        upto = sb("upto16", P, CHUNK)
        below = sb("neg_below16", P, CHUNK)
        sel = sb("head_select", H, 2, P)
        eps = sb("eps", P, 4)
        cosT = sb("cosT", P, P)
        sinT = sb("sinT", P, P)
        pw = sb("powers", P, 4, 2)
        rdec = sb("rdec", P, 4)
        decay0 = sb("decay_pattern", P, COLS)
        restart = sb("restart_pattern", H, COLS)
        carry = sb("scan_carry", P, GROUPS, 2, BPU)
        csm = sb("carry_small", P, 4, BPU)
        hist = sb("conv_history", P, GROUPS, 6, BPU, TAPS - 1)
        kept_state = sb("delta_state", P, GROUPS, SETS, HD)
        state = sb("delta_state_now", P, SETS, HD)
        W2 = 2 * COLS
        R = {k: sb(f"front{k}", P, W2) for k in (1, 2, 3, 4, 5, 8, 9, 11)}
        r10 = sb("front10", P, 2 * BPU * (P + TAPS - 1))
        inv = sb("inverse", P, CHUNK, HPT // 2, CHUNK)
        bd1 = sb("bd_first", P, 2, 8, TILE)
        vB = sb("values_by_group", P, HD * P)
        def pair(name, *shape):
            return [sb(f"{name}{k}", P, *shape) for k in range(2)]
        xs, gates, nps = pair("x", BPU, D), pair("gate", BPU, D), pair("np", 2, COLS)
        kqis, gjs = pair("kqi", G, 3, CHUNK), pair("gj", 6, G)
        gqs, pTs, tTs, kcs, vbs = pair("gq", W2), pair("pT", W2), pair("tT", W2), pair("kc", W2), pair("vbeta", W2)
        bdk = sb("bd_k", P, 2, SETS, TILE)
        bdt = sb("bd_t", P, SETS, TILE)
        bdc = sb("bd_kc", P, SETS, TILE)
        bds = sb("bd_s", P, SETS, TILE)
        bde = sb("bd_e", P, SETS, TILE)
        ch = sb("chain_small", P, 4, SETS, HD)
        oTr = sb("oT", P, W2)
        osq, orr = sb("out_squares", P, W2), sb("out_scales", P, W2)
        x1T = oTr
        stats = sb("stats", P, BPU, 6)
        mv = sb("mv", P, BPU, 2)
        rstd = sb("rstd", P, BPU)

        def half(t, i):
            return t[:, i * COLS:(i + 1) * COLS]

        xT = R[1][:, :].rearrange("p (e n) -> p e n", e=2)
        prod_v, prod_p = R[2], R[3]
        zin, zout = R[4], R[5]
        vT = R[8]
        gi, bi, fdec = R[2], R[3], R[4]
        fP, fA, aT = R[1], R[5], R[2]
        aB = R[3]
        r11 = R[11]
        oT = oTr[:, :].rearrange("p (e n) -> p e n", e=2)
        y1 = orr[:, :].rearrange("p (b d) -> p b d", b=BPU)
        cin = r10[:, :].rearrange("p (a b t) -> p a b t", a=2, t=P + TAPS - 1)
        decx, logx = R[2][0:H, 0:COLS], R[2][0:H, COLS:]
        gcum, bet = R[5][0:H, 0:COLS], R[5][0:H, COLS:]
        g16 = lambda t: t[:, 0:G * CHUNK].rearrange("p (g i) -> p g i", i=CHUNK)
        by_chunk = lambda t: t[:, 0:G * CHUNK].rearrange("p (s c i) -> p s c i", s=SETS, c=NCH)
        conv_at = [half(R[9], 0), half(R[9], 1), half(R[5], 0), half(R[5], 1), half(vT, 0), half(vT, 1)]
        Xs, Dd, Ee, Ed = (ch[:, k, :, :] for k in range(4))

        passed = sem("wait_passed")
        s_load, s_const, s_x1 = sem("weights_loaded"), sem("constants"), sem("x1_stored")
        s_x = sem("x_loaded")
        s_prep, s_ready = sem("prepared"), sem("setup_done")
        front_done, back_done = sem("front_done"), sem("back_done")
        xT_ready, rot_p, scanned = sem("xT_ready"), sem("rotated_by_pool"), sem("scanned")
        y_v, y_p, sq_ready, rs_ready = sem("y_even"), sem("y_odd"), sem("p20_squares"), sem("p20_rs")
        np_v, np_p = sem("np_even"), sem("np_odd")
        gate_added, gate_ready = sem("gate_added"), sem("gate_ready")
        dec_log, bet_ready, gcum_ready = sem("dec_log"), sem("bet_ready"), sem("gcum_ready")
        gi_ready, bi_ready = sem("gi_ready"), sem("bi_ready")
        cin_ready, conv_done, silu_done, raw_ready = sem("cin_ready"), sem("conv_done"), sem("silu_done"), sem("raw_ready")
        msq_ready, mrs_ready, kq_ready = sem("msq_ready"), sem("mrs_ready"), sem("kq_ready")
        diag_mul, gj_ready, diff_ready = sem("diag_mul"), sem("gj_ready"), sem("diff_ready")
        f_ready, e_ready, fp_ready, sm_ready = sem("f_ready"), sem("e_ready"), sem("fp_ready"), sem("sm_ready")
        bd1_ready, kc_ready = sem("bd1_ready"), sem("kc_ready")
        a_ready, ab_ready, inv_ready = sem("a_ready"), sem("ab_ready"), sem("inv_ready")
        vb_ready = sem("vb_ready")
        bdk_r, bdt_r, bdc_r, bds_r, bde_r = sem("bdk_r"), sem("bdt_r"), sem("bdc_r"), sem("bds_r"), sem("bde_r")
        d_ready, ed_ready, st_ready, ee_ready = sem("d_ready"), sem("ed_ready"), sem("st_ready"), sem("ee_ready")
        osq_ready, ors_ready, on_ready = sem("osq_ready"), sem("ors_ready"), sem("on_ready")
        var_ready, rstd_ready, x1_ready, x1T_ready = sem("var_ready"), sem("rstd_ready"), sem("x1_ready"), sem("x1T_ready")
        filled_f, filled_b = sem("front_filled"), sem("back_filled")
        freed = {(r, w): sem(f"{r}_freed_by_{w}") for r in "fb" for w in ("act", "dve")}
        setup_steps = sem("setup_steps")
        steps = {(r, w): sem(f"{r}_{w}_steps") for r in "fb" for w in ("act", "dve", "pool")}

        MS = (2, 3, 0, 1, 4, 5)
        order = [(("xT", e), "act") for e in range(2)]
        order += [(("gate", b), "dve") for b in range(BPU // 2)]
        order += [((n,), "act") for n in ("dec", "bet")]
        order += [(("ctl", MS[0]), "act"), (("ctl", MS[1]), "act"), (("pss",), "act"), (("ctl", MS[2]), "act")]
        order += [(("gi", 0), "act"), (("gi", 1), "act"), (("ctl", MS[3]), "act")]
        order += [(("bi", 0), "act"), (("bi", 1), "act"), (("ctl", MS[4]), "act"), (("ctl", MS[5]), "act")]
        for i, m in enumerate(MS):
            order += [(("p20", m), "dve")]
            if 0 < i < 5:
                order += [(("nrm", MS[i - 1]), "act")]
        order += [(("mm1", t), "dve") for t in range(G // 8)]
        order += [(("aT", t), "act") for t in range(2)]
        order += [(("v1", t), "dve") for t in range(4)]
        order += [(("v2", t), "dve") for t in range(2)]
        order += [(("tT", t), "act") for t in range(2)]
        while len(order) % 4:
            order.append((("pad", len(order)), "act"))
        front = Bank(order, banks[0:4], filled_f, {w: freed["f", w] for w in ("act", "dve")})
        order = []
        for c in range(NCH):
            order += [(("X", c), "dve")] + [(("O", c - 1), "act")] * (c > 0) + [(("E", c), "act"), (("dS", c), "dve")]
        order.append((("O", NCH - 1), "act"))
        order += [(("on", hh), "act") for hh in range(2)]
        order += [(("proj", b), "dve") for b in range(BPU // 2)]
        order += [(("x1T", b), "act") for b in range(BPU // 2)]
        order += [(("lg", 0), "act")]
        while len(order) % 4:
            order.append((("pad", len(order)), "act"))
        back = Bank(order, banks[4:8], filled_b, {w: freed["b", w] for w in ("act", "dve")})

        STAGES = 30
        MM1_STAGE, INV_STAGE = 16, 21
        ROWS = [(1, 6), (6, 8), (8, 10), (10, 12), (12, 13), (13, 14), (14, 15), (15, 16)]

        def weave(fr, bk, lead):
            if lead and fr is not None:
                next(fr, None)
            for _ in range(STAGES):
                for part in ((bk, fr) if lead else (fr, bk)):
                    if part is not None:
                        next(part, None)
            for part in (fr, bk):
                assert part is None or next(part, "end") == "end"

        def run(eng, fr, bk, lead=False):
            def at(f, u, par):
                return f(u, par, u % GROUPS, u // GROUPS)
            weave(at(fr, 0, 0), None, lead)
            if units > 2:
                with eng.Fori(0, units // 2 - 1) as w:
                    weave(at(fr, w * 2 + 1, 1), at(bk, w * 2, 0), lead)
                    weave(at(fr, w * 2 + 2, 0), at(bk, w * 2 + 1, 1), lead)
            weave(at(fr, units - 1, 1), at(bk, units - 2, 0), lead)
            weave(None, at(bk, units - 1, 1), lead)

        NLOAD = 16 + HPT
        with nc.Block() as block:
            def bd(eng, out_, in_):
                n = in_.shape[1]
                return eng.tensor_tensor(out_.rearrange("p s (h i) -> p s h i", h=2),
                                         in_.unsqueeze(2).broadcast_to([P, n, 2, CHUNK]),
                                         pmask[:, :].unsqueeze(1).unsqueeze(3).broadcast_to([P, n, 2, CHUNK]),
                                         ALU.mult)

            @block.sync
            def _(sp):
                for dst, src in (
                    (ctrlW[:, :, :], ctrl_W.rearrange("(p e) n -> p e n", e=2)),
                    (p20W[:, :, :], p20c_W.rearrange("(p e) n -> p e n", e=2)),
                    (outW[:, 0:2, :], out_W[0:D, :].rearrange("(k p) n -> p k n", p=P)),
                    (outW[:, 2:4, :], out_W[D:2 * D, :].rearrange("(p e) n -> p e n", e=2)),
                    (wgs[:, :, :], wg.rearrange("(k p) n -> p k n", p=P)),
                    (cb[:, :], ctrl_b[0:3 * D].rearrange("(m p) -> p m", p=P)),
                    (gb[:, :], ctrl_b[3 * D:3 * D + 2 * H].rearrange("(k p) -> p k", p=H)),
                    (convw[:, 0:2, :], qconv.rearrange("(m p) t -> p m t", p=P)),
                    (convw[:, 2:4, :], kconv.rearrange("(m p) t -> p m t", p=P)),
                    (convw[:, 4:6, :], vconv.rearrange("(m p) t -> p m t", p=P)),
                    (vn[:, :], vnorm.rearrange("(p e) -> p e", e=2)),
                    (outb[:, :], out_b.partition_broadcast(P)),
                    (gateb[:, :], ctrl_b[3 * D + 2 * H:].partition_broadcast(P)),
                    (rdec[:, 0:1], decay_log.rearrange("(p o) -> p o", o=1)),
                    (rdec[:, 1:2], theta.rearrange("(p o) -> p o", o=1)),
                    (r11[:, 0:D], ramp.partition_broadcast(P)),
                ):
                    sp.dma_start(dst, src, allow_slow_non_contiguous=True).then_inc(s_load, 16)
                for h in range(HPT):
                    sp.dma_start(mn[h * HD:(h + 1) * HD, :], mnorm.rearrange("(p o) -> p o", o=1)).then_inc(s_load, 16)

                def fr(u, par, grp, s):
                    sp.wait_ge(back_done, u + 1)
                    sp.wait_ge(s_x, u * 16 + 16)
                    sp.dma_start(xs[par][:, :, :], hidden[bass.ds(grp * BPU, BPU), bass.ds(s * P, P), :]
                                 .rearrange("b t d -> t b d")).then_inc(s_x, 16)
                    yield

                def bk(u, par, grp, s):
                    for _ in range(STAGES - 1):
                        yield
                    sp.wait_ge(x1_ready, u + 1)
                    sp.dma_start(x1d.rearrange("(b t) d -> t b d", b=B)[bass.ds(s * P, P), bass.ds(grp * BPU, BPU), :],
                                 y1).then_inc(s_x1, 16)
                    yield
                sp.wait_ge(s_ready, 1)
                run(sp, fr, bk)
                sp.wait_ge(s_x1, units * 16 + 16)

            @block.gpsimd
            def _(pool):
                fc = Steps(pool, steps["f", "pool"], 4)
                pool.memset(ident[:, :], 0.0).then_inc(s_const, 1)
                pool.memset(hmask[:, :], 1.0).then_inc(s_const, 1)
                pool.memset(sel[:, :, :], 0.0).then_inc(s_const, 1)
                pool.memset(ones[:, :], 1.0).then_inc(s_const, 1)
                pool.wait_ge(s_const, 4)
                pool.affine_select(out=ident[:, :], in_=ident[:, :], compare_op=ALU.not_equal, fill=1.0, base=0,
                                   pattern=[[-1, P]], channel_multiplier=1).then_inc(s_const, 1)
                pool.affine_select(out=hmask[:, :], in_=hmask[:, :], compare_op=ALU.is_ge, fill=0.0, base=0,
                                   pattern=[[-HD, HPT]], channel_multiplier=1).then_inc(s_const, 1)
                pool.affine_select(out=sel[:, :, :].rearrange("k a (h j) -> k a h j", j=HD),
                                   in_=sel[:, :, :].rearrange("k a (h j) -> k a h j", j=HD),
                                   compare_op=ALU.not_equal, fill=1.0, base=0,
                                   pattern=[[-HPT, 2], [-1, HPT], [0, HD]], channel_multiplier=1).then_inc(s_const, 1)
                pool.wait_ge(s_const, 7)
                pool.affine_select(out=hmask[:, :], in_=hmask[:, :], compare_op=ALU.is_ge, fill=0.0, base=HD - 1,
                                   pattern=[[HD, HPT]], channel_multiplier=-1).then_inc(s_const, 1)
                pool.wait_ge(s_const, 8)
                pool.tensor_tensor(blk[:, :].rearrange("p (h j) -> p h j", j=HD),
                                   hmask[:, :].unsqueeze(2).broadcast_to([P, HPT, HD]),
                                   ones[:, :].rearrange("p (h j) -> p h j", j=HD), ALU.mult).then_inc(s_const, 1)
                pool.wait_ge(s_const, 9)
                pool.affine_select(out=osq[:, 0:P], in_=blk[:, :], compare_op=ALU.is_ge, fill=0.0, base=0,
                                   pattern=[[1, P]], channel_multiplier=-1).then_inc(s_const, 1)
                pool.wait_ge(s_ready, 1)
                tab = lambda t: t[:, :].unsqueeze(1).broadcast_to([P, BPU, P])
                v3 = lambda t, i: half(t, i).rearrange("p (b t) -> p b t", b=BPU)
                m16 = lambda t: t[:, :].unsqueeze(1).broadcast_to([P, G, CHUNK])

                def fr(u, par, grp, s):
                    npT, kqi = nps[par], kqis[par]
                    fc.start(u)
                    pool.wait_ge(front_done, u + 1)
                    pool.wait_ge(back_done, u + 1)
                    yield
                    pool.wait_ge(xT_ready, u * 2 + 2)
                    pool.tensor_tensor(v3(prod_p, 0), xT[:, 1, :].rearrange("p (b t) -> p b t", b=BPU), tab(cosT), ALU.mult)
                    fc.then(pool.tensor_tensor(v3(prod_p, 1), xT[:, 0, :].rearrange("p (b t) -> p b t", b=BPU), tab(sinT), ALU.mult))
                    pool.tensor_tensor(half(zin, 1), half(prod_p, 0), half(prod_p, 1), ALU.subtract).then_inc(rot_p, 1)
                    yield
                    yield
                    pool.wait_ge(scanned, u * 2 + 2)
                    pool.wait_ge(rot_p, u + 1)
                    pool.tensor_tensor(v3(prod_p, 0), v3(zout, 1), tab(cosT), ALU.mult)
                    fc.then(pool.tensor_tensor(v3(prod_p, 1), v3(zout, 0), tab(sinT), ALU.mult))
                    pool.tensor_tensor(npT[:, 1, :], half(prod_p, 0), half(prod_p, 1), ALU.add).then_inc(y_p, 1)
                    yield
                    yield
                    yield
                    pool.wait_ge(rs_ready, u + 1)
                    pool.wait_ge(y_p, u + 1)
                    pool.tensor_tensor(npT[:, 1, :], npT[:, 1, :], half(R[4], 0), ALU.mult).then_inc(np_p, 1)
                    yield
                    pool.wait_ge(gi_ready, u * 2 + 2)
                    pool.wait_ge(np_v, u + 1)
                    pool.wait_ge(np_p, u + 1)
                    pool.tensor_tensor(g16(R[4]), g16(gi), m16(diag), ALU.mult).then_inc(diag_mul, 1)
                    yield
                    pool.wait_ge(bi_ready, u * 2 + 2)
                    pool.wait_ge(gj_ready, u * 2 + 1)
                    pool.tensor_tensor(g16(R[4]), g16(bi), m16(diag), ALU.mult).then_inc(diag_mul, 1)
                    yield
                    for _ in range(9, 15):
                        yield
                    pool.wait_ge(f_ready, u + 1)
                    pool.wait_ge(kq_ready, u * 4 + 4)
                    fc.then(pool.tensor_tensor(g16(fP), g16(fdec), m16(upto), ALU.mult))
                    fc.then(pool.tensor_tensor(g16(fdec), g16(fdec), m16(below), ALU.mult))
                    pool.tensor_tensor(g16(fA), g16(fdec), g16(bi), ALU.mult).then_inc(fp_ready, 1)
                    first(u, kqi, 0)
                    first(u, kqi, 1)
                    yield
                    for t in range(2, 8):
                        first(u, kqi, t)
                        if t % 2:
                            yield
                    pool.wait_ge(e_ready, u + 1)
                    pool.tensor_tensor(g16(gqs[par]), kqi[:, :, 1, :], g16(r11), ALU.mult).then_inc(fp_ready, 1)
                    yield
                    fc.end()

                def first(u, kqi, t):
                    if t >= 2:
                        pool.wait_ge(front.filled, front.full(u, ("mm1", t - 2)))
                    bd(pool, bd1[:, t % 2, :, :], kqi[:, 8 * t:8 * t + 8, 0, :]).then_inc(bd1_ready, 1)

                def bk(u, par, grp, s):
                    kqi, kc = kqis[par], kcs[par]
                    kview = kqi[:, :, 0, :].rearrange("p (s c) i -> p s c i", c=NCH)
                    pool.wait_ge(back_done, u + 2)
                    pool.wait_ge(front_done, u + 2)
                    bd(pool, bdk[:, 0, :, :], kview[:, :, 0, :]).then_inc(bdk_r, 1)
                    for c in range(NCH):
                        if c:
                            pool.wait_ge(back.filled, back.full(u, ("dS", c - 1)))
                        bd(pool, bdc[:, :, :], by_chunk(kc)[:, :, c, :]).then_inc(bdc_r, 1)
                        yield
                        if c + 1 < NCH:
                            if c:
                                pool.wait_ge(back.filled, back.full(u, ("X", c - 1)))
                            bd(pool, bdk[:, (c + 1) % 2, :, :], kview[:, :, c + 1, :]).then_inc(bdk_r, 1)
                        yield
                        yield
                run(pool, fr, bk)

            @block.scalar
            def _(act):
                A = nc.scalar.activation
                act.wait_ge(s_load, NLOAD * 16)
                act.wait_ge(s_prep, 1)
                A(rdec[:, 0:1], rdec[:, 0:1], ACT.Exp).then_inc(s_prep, 1)
                act.wait_ge(s_prep, 2)
                A(rdec[:, 0:1], rdec[:, 0:1], ACT.Exp, scale=-1.0).then_inc(s_prep, 1)
                A(pw[:, 0, 1:2], rdec[:, 1:2], ACT.Sin).then_inc(s_prep, 1)
                A(pw[:, 0, 0:1], rdec[:, 2:3], ACT.Sin).then_inc(s_prep, 1)
                A(r11[:, 0:D], r11[:, 0:D], ACT.Sigmoid).then_inc(s_prep, 1)
                act.wait_ge(s_ready, 1)
                act.sem_inc(front_done, 1)
                act.sem_inc(back_done, 2)
                act.sem_inc(front.freed["act"], front.count["act"])
                act.sem_inc(back.freed["act"], back.count["act"])
                fc, bc_ = Steps(act, steps["f", "act"], FA_STEPS), Steps(act, steps["b", "act"], BA_STEPS)

                def copy(st, bank, u, key, out_, in_, func=ACT.Copy, sig=None, **kw):
                    act.wait_ge(bank.filled, bank.full(u, key))
                    st.then(A(out_, in_, func, **kw))
                    act.sem_inc(bank.freed["act"], 1)
                    if sig is not None:
                        act.sem_inc(sig, 1)

                def rs(st, bank, u, key, out_, scale, e, sig):
                    act.wait_ge(bank.filled, bank.full(u, key))
                    st.then(A(out_, bank[key][:, :], ACT.Ln, scale=scale, bias=eps[:, e:e + 1]))
                    act.sem_inc(bank.freed["act"], 1)
                    A(out_, out_, ACT.Exp, scale=-0.5).then_inc(sig, 1)

                def conv_in(u, grp, i):
                    m = MS[i]
                    if i >= 2:
                        act.wait_ge(conv_done, u * 6 + i - 1)
                    act.sem_inc(passed, 1)
                    A(cin[:, i % 2, :, 0:TAPS - 1], hist[:, bass.ds(grp, 1), m, :, :].rearrange("p o b t -> p (o b) t"), ACT.Copy)
                    act.wait_ge(front.filled, front.full(u, ("ctl", m)))
                    fc.then(A(cin[:, i % 2, :, TAPS - 1:], front["ctl", m][:, :].rearrange("p (b t) -> p b t", b=BPU),
                              ACT.Identity, bias=cb[:, m:m + 1]))
                    act.sem_inc(front.freed["act"], 1)
                    act.sem_inc(cin_ready, 1)
                    A(hist[:, bass.ds(grp, 1), m, :, :].rearrange("p o b t -> p (o b) t"), cin[:, i % 2, :, P:], ACT.Copy).then_inc(cin_ready, 1)

                def norm(u, i, new):
                    if new > 0:
                        if i > 1:
                            act.wait_ge(kq_ready, u * 4 + i - 1)
                        m = MS[i - 1]
                        rs(fc, front, u, ("nrm", m), half(r11, 1), float(HD) if m < 2 else 1.0, 1 if m < 2 else 0, mrs_ready)
                    if i < 4:
                        act.wait_ge(raw_ready, u * 6 + i + 1)
                        A(half(r11, 0), conv_at[i], ACT.Square).then_inc(msq_ready, 1)

                def fr(u, par, grp, s):
                    npT, gj = nps[par], gjs[par]
                    GJ, BJ, EC, ECJ, NBG = (gj[:, k, :] for k in range(5))
                    fc.start(u)
                    act.wait_ge(front_done, u + 1)
                    act.wait_ge(back_done, u + 1)
                    for e in range(2):
                        copy(fc, front, u, ("xT", e), xT[:, e, :], front["xT", e][:, :], sig=xT_ready)
                    yield
                    yield
                    yield
                    act.wait_ge(gate_added, u * 2 + 2)
                    A(gates[par][:, :, :], gates[par][:, :, :], ACT.Sigmoid).then_inc(gate_ready, 1)
                    act.wait_ge(y_v, u + 1)
                    act.wait_ge(y_p, u + 1)
                    copy(fc, front, u, ("dec",), decx, front["dec",][0:H, :], ACT.Identity, bias=gb[:, 0:1])
                    copy(fc, front, u, ("bet",), bet, front["bet",][0:H, :], ACT.Sigmoid, bias=gb[:, 1:2], sig=bet_ready)
                    conv_in(u, grp, 0)
                    yield
                    A(half(R[4], 0), npT[:, 0, :], ACT.Square).then_inc(sq_ready, 1)
                    A(half(R[4], 1), npT[:, 1, :], ACT.Square).then_inc(sq_ready, 1)
                    fc.then(A(logx, decx, ACT.Abs))
                    fc.then(A(logx, logx, ACT.Exp, scale=-1.0))
                    A(logx, logx, ACT.Ln, bias=1.0).then_inc(dec_log, 1)
                    conv_in(u, grp, 1)
                    yield
                    rs(fc, front, u, ("pss",), half(R[4], 0), 1.0 / D, 0, rs_ready)
                    conv_in(u, grp, 2)
                    yield
                    for hh in range(2):
                        copy(fc, front, u, ("gi", hh), half(gi, hh), front["gi", hh][:, :], sig=gi_ready)
                    conv_in(u, grp, 3)
                    yield
                    for hh in range(2):
                        copy(fc, front, u, ("bi", hh), half(bi, hh), front["bi", hh][:, :], sig=bi_ready)
                    conv_in(u, grp, 4)
                    yield
                    conv_in(u, grp, 5)
                    yield
                    for i in range(6):
                        act.wait_ge(conv_done, u * 6 + i + 1)
                        A(conv_at[i], conv_at[i], ACT.Silu).then_inc(silu_done, 1)
                    yield
                    norm(u, 0, 0)
                    yield
                    for i in range(1, 4):
                        norm(u, i, 1)
                        yield
                    norm(u, 4, 1)
                    act.wait_ge(diff_ready, u + 1)
                    A(g16(fdec), g16(fdec), ACT.Exp).then_inc(f_ready, 1)
                    A(EC, g16(gi)[:, :, CHUNK - 1], ACT.Exp)
                    A(ECJ, ECJ, ACT.Exp)
                    A(NBG, GJ, ACT.Exp).then_inc(sm_ready, 1)
                    yield
                    act.wait_ge(kq_ready, u * 4 + 4)
                    A(r11[:, :], gi[:, :], ACT.Exp).then_inc(e_ready, 1)
                    yield
                    for t in range(8):
                        key = ("mm1", t)
                        act.wait_ge(front.filled, front.full(u, key))
                        A(g16(kcs[par])[:, 8 * t:8 * t + 8, :],
                          front[key][:, 0:384].rearrange("p (g k i) -> p g k i", k=3, i=CHUNK)[:, :, 2, :], ACT.Copy).then_inc(kc_ready, 1)
                        if t % 2:
                            yield
                    act.wait_ge(a_ready, u * 8 + 8)
                    for t in range(2):
                        copy(fc, front, u, ("aT", t), aB[:, t * 512:(t + 1) * 512], front["aT", t][:, :], sig=ab_ready)
                    yield
                    for _ in range(21, 29):
                        yield
                    for t in range(2):
                        act.wait_ge(front.filled, front.full(u, ("tT", t)))
                        fc.then(A(g16(tTs[par]).rearrange("p g i -> p i g")[:, 8 * t:8 * t + 8, :],
                                  front["tT", t][:, :].rearrange("p (i g) -> p i g", i=8), ACT.Copy))
                        act.sem_inc(front.freed["act"], 1 + (front.pads if t else 0))
                    act.sem_inc(front_done, 1)
                    yield
                    fc.end()

                def o_copy(u, c):
                    copy(bc_, back, u, ("O", c), oTr[:, :].rearrange("p (s c i) -> p s c i", s=SETS, c=NCH)[:, :, c, :],
                         back["O", c][:, 0:SETS * CHUNK].rearrange("p (s i) -> p s i", i=CHUNK))

                def bk(u, par, grp, s):
                    bc_.start(u)
                    act.wait_ge(back_done, u + 2)
                    act.wait_ge(s_x1, u * 16 + 16)
                    for c in range(NCH):
                        yield
                        if c:
                            o_copy(u, c - 1)
                        act.wait_ge(back.filled, back.full(u, ("E", c)))
                        act.wait_ge(ed_ready, u * NCH + c + 1)
                        act.sem_inc(passed, 1)
                        A(Ee, back["E", c][:, 0:SETS * HD].rearrange("p (s v) -> p s v", v=HD), ACT.Copy).then_inc(ee_ready, 1)
                        act.wait_ge(ee_ready, u * NCH + c + 1)
                        act.sem_inc(back.freed["act"], 1)
                        yield
                        yield
                    o_copy(u, NCH - 1)
                    A(osq[:, :], oTr[:, :], ACT.Square).then_inc(osq_ready, 1)
                    yield
                    for hh in range(2):
                        rs(bc_, back, u, ("on", hh), half(orr, hh), 1.0 / HD, 0, ors_ready)
                    yield
                    yield
                    act.wait_ge(var_ready, u + 1)
                    bc_.then(A(rstd[:, :], mv[:, :, 1], ACT.Ln, bias=eps[:, 2:3]))
                    A(rstd[:, :], rstd[:, :], ACT.Exp, scale=-0.5).then_inc(rstd_ready, 1)
                    yield
                    for b in range(BPU // 2):
                        copy(bc_, back, u, ("x1T", b), x1T[:, b * 512:(b + 1) * 512], back["x1T", b][:, :], sig=x1T_ready)
                    yield
                    act.wait_ge(back.filled, back.full(u, ("lg", 0)))
                    act.sem_inc(passed, 1)
                    bc_.then(A(keep[:, bass.ds(grp * BPU, BPU), bass.ds(s, 1), :],
                               back["lg", 0][:, 0:BPU * E].rearrange("p (b o e) -> p b o e", o=1, e=E), ACT.Copy))
                    act.sem_inc(back.freed["act"], 1 + back.pads)
                    act.sem_inc(back_done, 1)
                    yield
                    bc_.end()

                run(act, fr, bk)

            @block.vector
            def _(dve):
                V = nc.vector
                setup = [0]

                def link(ins):
                    setup[0] += 1
                    ins.then_inc(setup_steps, 1)
                    dve.wait_ge(setup_steps, setup[0])
                dve.wait_ge(s_load, NLOAD * 16)
                dve.wait_ge(s_const, 10)
                link(V.tensor_scalar(rdec[:, 2:3], rdec[:, 1:2], 1.0 / TWO_PI, 12582912.0, ALU.mult, ALU.add))
                link(V.tensor_scalar(rdec[:, 2:3], rdec[:, 2:3], -12582912.0, None, ALU.add))
                link(V.scalar_tensor_tensor(rdec[:, 1:2], rdec[:, 2:3], -6.28125, rdec[:, 1:2], ALU.mult, ALU.add))
                link(V.scalar_tensor_tensor(rdec[:, 1:2], rdec[:, 2:3], -(TWO_PI - 6.28125), rdec[:, 1:2], ALU.mult, ALU.add))
                link(V.tensor_scalar(rdec[:, 1:2], rdec[:, 1:2], float(np.float32(3.1415925)), float(np.float32(-3.1415925)), ALU.min, ALU.max))
                link(V.tensor_scalar(rdec[:, 2:3], rdec[:, 1:2], -1.0, None, ALU.mult))
                link(V.tensor_tensor(rdec[:, 2:3], rdec[:, 1:2], rdec[:, 2:3], ALU.max))
                link(V.tensor_scalar(rdec[:, 2:3], rdec[:, 2:3], -1.0, float(np.pi / 2), ALU.mult, ALU.add))
                V.memset(eps[:, 0:1], EPS_RMS)
                V.memset(eps[:, 1:2], HD * EPS_RMS)
                V.memset(carry[:, :, :, :], 0.0)
                V.memset(hist[:, :, :, :, :], 0.0)
                V.memset(kept_state[:, :, :, :], 0.0)
                link(V.memset(eps[:, 2:3], EPS_LN))
                dve.sem_inc(s_prep, 1)
                link(V.tensor_reduce(diag[:, :], ident[:, :].rearrange("p (h i) -> p i h", h=HPT), AX.X, ALU.add))
                link(V.tensor_reduce(upto[:, :], osq[:, 0:P].rearrange("p (h i) -> p i h", h=HPT), AX.X, ALU.add))
                link(V.tensor_reduce(pmask[:, :], hmask[:, :].rearrange("p (q a) -> p a q", a=2), AX.X, ALU.add))
                link(V.tensor_tensor(below[:, :], diag[:, :], upto[:, :], ALU.subtract))
                for kqi in kqis:
                    V.tensor_copy(kqi[:, :, 2, :], diag[:, :].unsqueeze(1).broadcast_to([P, G, CHUNK]))
                V.memset(inv[:, :, :, :], 0.0)
                V.memset(restart[:, :], 1.0)
                V.memset(cosT[:, 0:1], 1.0)
                link(V.memset(sinT[:, 0:1], 0.0))
                for i in range(CHUNK):
                    V.memset(inv[:, i, :, i:i + 1], 1.0)
                link(V.memset(restart[:, :].rearrange("p (g i) -> p g i", i=CHUNK)[:, :, 0:1], 0.0))
                for e in range(2):
                    V.tensor_scalar(p20W[:, e, :], p20W[:, e, :], vn[:, e:e + 1], None, ALU.mult)
                    V.tensor_scalar(outW[:, 2 + e, :], outW[:, 2 + e, :], vn[:, e:e + 1], None, ALU.mult)
                    link(V.tensor_scalar(outW[:, e, :], outW[:, e, :], mn[:, 0:1], None, ALU.mult))
                dve.wait_ge(s_prep, 6)
                for e in range(2):
                    link(V.tensor_tensor(p20W[:, e, :].rearrange("p (k n) -> p k n", k=3), p20W[:, e, :].rearrange("p (k n) -> p k n", k=3),
                                         r11[:, 0:D].unsqueeze(1).broadcast_to([P, 3, D]), ALU.mult))
                link(V.memset(decay0[:, :], 1.0))
                link(V.tensor_scalar(decay0[:, :], decay0[:, :], rdec[:, 0:1], None, ALU.mult))
                link(V.memset(decay0[:, :].rearrange("p (b t) -> p b t", b=BPU)[:, :, 0:1], 0.0))
                n = 1
                while n < P:
                    link(V.tensor_scalar(pw[:, 2, :], pw[:, 0, :], pw[:, 0, 1:2], None, ALU.mult))
                    c0, s0 = pw[:, 0, 0:1], pw[:, 0, 1:2]
                    link(V.tensor_scalar(cosT[:, n:2 * n], sinT[:, 0:n], s0, -1.0, ALU.mult, ALU.mult))
                    link(V.scalar_tensor_tensor(cosT[:, n:2 * n], cosT[:, 0:n], c0, cosT[:, n:2 * n], ALU.mult, ALU.add))
                    link(V.tensor_scalar(sinT[:, n:2 * n], cosT[:, 0:n], s0, None, ALU.mult))
                    link(V.scalar_tensor_tensor(sinT[:, n:2 * n], sinT[:, 0:n], c0, sinT[:, n:2 * n], ALU.mult, ALU.add))
                    link(V.scalar_tensor_tensor(pw[:, 1, 0:1], c0, c0, pw[:, 2, 1:2], ALU.mult, ALU.subtract))
                    link(V.tensor_scalar(pw[:, 1, 1:2], pw[:, 2, 0:1], 2.0, None, ALU.mult))
                    link(V.tensor_copy(pw[:, 0, :], pw[:, 1, :]))
                    n *= 2
                dve.sem_inc(front.freed["dve"], front.count["dve"])
                dve.sem_inc(back.freed["dve"], back.count["dve"])
                dve.sem_inc(s_x1, 16)
                dve.sem_inc(s_x, 16)
                dve.sem_inc(s_ready, 1)
                fc, bc_ = Steps(dve, steps["f", "dve"], FD_STEPS), Steps(dve, steps["b", "dve"], BD_STEPS)
                tab = lambda t: t[:, :].unsqueeze(1).broadcast_to([P, BPU, P])
                v3 = lambda t, i: half(t, i).rearrange("p (b t) -> p b t", b=BPU)
                xb = lambda e: xT[:, e, :].rearrange("p (b t) -> p b t", b=BPU)

                def freed_(bank, n=1):
                    dve.sem_inc(bank.freed["dve"], n)

                def conv(u, i):
                    m = MS[i]
                    dve.wait_ge(cin_ready, u * 12 + 2 * i + 1)
                    o = conv_at[i].rearrange("p (b t) -> p b t", b=BPU)
                    for k in range(TAPS):
                        src = cin[:, i % 2, :, TAPS - 1 - k:TAPS - 1 - k + P]
                        w = convw[:, m, TAPS - 1 - k:TAPS - k]
                        if k == 0:
                            fc.then(V.tensor_scalar(o, src, w, None, ALU.mult))
                        elif k < TAPS - 1:
                            fc.then(V.scalar_tensor_tensor(o, src, w, o, ALU.mult, ALU.add))
                        else:
                            V.scalar_tensor_tensor(o, src, w, o, ALU.mult, ALU.add).then_inc(conv_done, 1)

                def raw(u, i):
                    key = ("p20", MS[i])
                    dve.wait_ge(silu_done, u * 6 + i + 1)
                    dve.wait_ge(front.filled, front.full(u, key))
                    V.tensor_tensor(conv_at[i], conv_at[i], front[key][:, :], ALU.add).then_inc(raw_ready, 1)
                    dve.wait_ge(raw_ready, u * 6 + i + 1)
                    freed_(front)

                def kq(u, i, kqi):
                    m = MS[i]
                    dve.wait_ge(mrs_ready, u * 4 + i + 1)
                    V.tensor_tensor(kqi[:, (m % 2) * (G // 2):(m % 2 + 1) * (G // 2), 0 if m >= 2 else 1, :],
                                    conv_at[i].rearrange("p (g i) -> p g i", i=CHUNK),
                                    half(r11, 1).rearrange("p (g i) -> p g i", i=CHUNK), ALU.mult).then_inc(kq_ready, 1)

                def fr(u, par, grp, s):
                    npT, kqi, gate, pT = nps[par], kqis[par], gates[par], pTs[par]
                    GJ, BJ, EC, ECJ, NBG = (gjs[par][:, k, :] for k in range(5))
                    fc.start(u)
                    dve.wait_ge(front_done, u + 1)
                    dve.wait_ge(back_done, u + 1)
                    yield
                    dve.wait_ge(xT_ready, u * 2 + 2)
                    V.tensor_tensor(v3(prod_v, 0), xb(0), tab(cosT), ALU.mult)
                    fc.then(V.tensor_tensor(v3(prod_v, 1), xb(1), tab(sinT), ALU.mult))
                    fc.then(V.tensor_tensor(half(zin, 0), half(prod_v, 0), half(prod_v, 1), ALU.add))
                    yield
                    dve.wait_ge(rot_p, u + 1)
                    cr = carry[:, bass.ds(grp, 1), :, :].rearrange("p o e b -> p (o e) b")
                    for e in range(2):
                        fc.then(V.scalar_tensor_tensor(v3(zin, e)[:, :, 0], cr[:, e, :], rdec[:, 0:1], v3(zin, e)[:, :, 0], ALU.mult, ALU.add))
                    for e in range(2):
                        V.tensor_tensor_scan(half(zout, e), decay0[:, :], half(zin, e), 0.0, ALU.mult, ALU.add).then_inc(scanned, 1)
                    for b in range(BPU // 2):
                        dve.wait_ge(front.filled, front.full(u, ("gate", b)))
                        V.tensor_tensor(gate[:, 2 * b:2 * b + 2, :], front["gate", b][:, :].rearrange("p (b d) -> p b d", b=2),
                                        gateb[:, :].unsqueeze(1).broadcast_to([P, 2, D]), ALU.add).then_inc(gate_added, 1)
                        dve.wait_ge(gate_added, u * 2 + b + 1)
                        freed_(front)
                    yield
                    dve.wait_ge(scanned, u * 2 + 2)
                    zr, zi = v3(zout, 0)[:, :, P - 1], v3(zout, 1)[:, :, P - 1]
                    V.tensor_scalar(csm[:, 0, :], zi, pw[:, 0, 1:2], None, ALU.mult)
                    fc.then(V.tensor_scalar(csm[:, 1, :], zr, pw[:, 0, 1:2], None, ALU.mult))
                    V.scalar_tensor_tensor(cr[:, 0, :], zr, pw[:, 0, 0:1], csm[:, 0, :], ALU.mult, ALU.subtract)
                    V.scalar_tensor_tensor(cr[:, 1, :], zi, pw[:, 0, 0:1], csm[:, 1, :], ALU.mult, ALU.add)
                    V.tensor_tensor(v3(prod_v, 0), v3(zout, 0), tab(cosT), ALU.mult)
                    fc.then(V.tensor_tensor(v3(prod_v, 1), v3(zout, 1), tab(sinT), ALU.mult))
                    V.tensor_tensor(npT[:, 0, :], half(prod_v, 0), half(prod_v, 1), ALU.subtract).then_inc(y_v, 1)
                    yield
                    conv(u, 0)
                    yield
                    dve.wait_ge(dec_log, u + 1)
                    fc.then(V.scalar_tensor_tensor(logx, decx, 0.0, logx, ALU.min, ALU.subtract))
                    V.tensor_tensor_scan(gcum, restart[:, :], logx, 0.0, ALU.mult, ALU.add).then_inc(gcum_ready, 1)
                    conv(u, 1)
                    yield
                    dve.wait_ge(rs_ready, u + 1)
                    dve.wait_ge(y_v, u + 1)
                    V.tensor_tensor(npT[:, 0, :], npT[:, 0, :], half(R[4], 0), ALU.mult).then_inc(np_v, 1)
                    yield
                    dve.wait_ge(diag_mul, u * 2 + 1)
                    V.tensor_reduce(GJ, g16(R[4]), AX.X, ALU.add).then_inc(gj_ready, 1)
                    dve.wait_ge(bi_ready, u * 2 + 2)
                    conv(u, 2)
                    yield
                    dve.wait_ge(diag_mul, u * 2 + 2)
                    V.tensor_reduce(BJ, g16(R[4]), AX.X, ALU.add).then_inc(gj_ready, 1)
                    conv(u, 3)
                    dve.wait_ge(gj_ready, u * 2 + 2)
                    fc.then(V.tensor_tensor(g16(fdec), g16(gi), GJ.unsqueeze(2).broadcast_to([P, G, CHUNK]), ALU.subtract))
                    V.tensor_scalar(g16(fdec), g16(fdec), 0.0, None, ALU.min)
                    V.tensor_tensor(ECJ, g16(gi)[:, :, CHUNK - 1], GJ, ALU.subtract).then_inc(diff_ready, 1)
                    yield
                    conv(u, 4)
                    conv(u, 5)
                    yield
                    raw(u, 0)
                    yield
                    raw(u, 1)
                    yield
                    raw(u, 2)
                    kq(u, 0, kqi)
                    yield
                    raw(u, 3)
                    kq(u, 1, kqi)
                    yield
                    raw(u, 4)
                    kq(u, 2, kqi)
                    yield
                    raw(u, 5)
                    kq(u, 3, kqi)
                    dve.wait_ge(sm_ready, u + 1)
                    V.scalar_tensor_tensor(NBG, BJ, -1.0, NBG, ALU.mult, ALU.mult)
                    yield
                    dve.wait_ge(fp_ready, u * 2 + 1)
                    for t in range(G // 8):
                        key = ("mm1", t)
                        dve.wait_ge(front.filled, front.full(u, key))
                        dve.wait_ge(kc_ready, u * 8 + t + 1)
                        ps = front[key][:, 0:384].rearrange("p (g k i) -> p g k i", k=3, i=CHUNK)
                        gs = slice(8 * t, 8 * t + 8)
                        if t == 0:
                            dve.wait_ge(e_ready, u + 1)
                        V.tensor_tensor(aT[:, :].rearrange("p (i g) -> p g i", i=CHUNK)[:, gs, :], ps[:, :, 0, :], g16(fA)[:, gs, :], ALU.mult)
                        V.tensor_tensor(g16(pT)[:, gs, :], ps[:, :, 1, :], g16(fP)[:, gs, :], ALU.mult).then_inc(a_ready, 1)
                        dve.wait_ge(a_ready, u * 8 + t + 1)
                        freed_(front)
                        if t % 2:
                            yield
                    for t in range(4):
                        dve.wait_ge(front.filled, front.full(u, ("v1", t)))
                        fc.then(V.tensor_copy(vB[0:G, :].rearrange("p (v h j) -> p j h v", v=HD, h=HPT)[:, 4 * t:4 * t + 4, :, :],
                                              front["v1", t][0:G, :].rearrange("p (j h v) -> p j h v", j=4, h=HPT)))
                        freed_(front)
                        dve.sem_inc(vb_ready, 1)
                    yield
                    dve.wait_ge(ab_ready, u * 2 + 2)
                    aBv = aB[:, :].rearrange("p (i h j) -> p i h j", i=CHUNK, h=HPT // 2)
                    for k, (i0, i1) in enumerate(ROWS):
                        for i in range(i0, i1):
                            pr = R[5][:, 0:HPT // 2 * i * i].rearrange("p (h c j) -> p h c j", h=HPT // 2, c=i)
                            fc.then(V.tensor_tensor(pr, aBv[:, i, :, 0:i].unsqueeze(2).broadcast_to([P, HPT // 2, i, i]),
                                                    inv[:, 0:i, :, 0:i].rearrange("p j h c -> p h c j"), ALU.mult))
                            fc.then(V.tensor_reduce(inv[:, i, :, 0:i], pr, AX.X, ALU.add))
                        if k == 1:
                            for t in range(2):
                                dve.wait_ge(front.filled, front.full(u, ("v2", t)))
                                fc.then(V.tensor_tensor(g16(vbs[par]).rearrange("p g v -> p v g")[:, 8 * t:8 * t + 8, :],
                                                        front["v2", t][:, :].rearrange("p (v g) -> p v g", v=8),
                                                        BJ.unsqueeze(1).broadcast_to([P, 8, G]), ALU.mult))
                                freed_(front)
                        if k + 1 == len(ROWS):
                            dve.sem_inc(inv_ready, 1)
                        yield
                    fc.end()

                def bk(u, par, grp, s):
                    tT, vbeta, gate, x = tTs[par], vbs[par], gates[par], xs[par]
                    GJ, BJ, EC, ECJ, NBG = (gjs[par][:, k, :] for k in range(5))
                    colv = lambda t, c: t.rearrange("p (s c) -> p s c", c=NCH)[:, :, c].unsqueeze(2).broadcast_to([P, SETS, HD])
                    bps = lambda key: back[key][:, 0:SETS * HD].rearrange("p (s v) -> p s v", v=HD)
                    here = kept_state[:, bass.ds(grp, 1), :, :].rearrange("p o s v -> p (o s) v")
                    bc_.start(u)
                    dve.wait_ge(back_done, u + 2)
                    dve.wait_ge(front_done, u + 2)
                    dve.wait_ge(s_x1, u * 16 + 16)
                    dve.sem_inc(passed, 1)
                    V.tensor_copy(state[:, :, :], here).then_inc(st_ready, 1)
                    bd(V, bdt[:, :, :], by_chunk(tT)[:, :, 0, :]).then_inc(bdt_r, 1)
                    dve.wait_ge(st_ready, u * (NCH + 1) + 1)
                    for c in range(NCH):
                        dve.wait_ge(back.filled, back.full(u, ("X", c)))
                        bc_.then(V.tensor_tensor(Xs, bps(("X", c)), colv(NBG, c), ALU.mult))
                        freed_(back)
                        V.tensor_tensor(Dd, Xs, by_chunk(vbeta)[:, :, c, :], ALU.add).then_inc(d_ready, 1)
                        if c:
                            dve.wait_ge(back.filled, back.full(u, ("O", c - 1)))
                        bd(V, bds[:, :, :], state[:, :, :]).then_inc(bds_r, 1)
                        yield
                        dve.wait_ge(back.filled, back.full(u, ("E", c)))
                        V.tensor_tensor(Ed, bps(("E", c)), colv(ECJ, c), ALU.mult).then_inc(ed_ready, 1)
                        yield
                        dve.wait_ge(bds_r, u * NCH + c + 1)
                        bc_.then(V.tensor_tensor(state[:, :, :], state[:, :, :], colv(EC, c), ALU.mult))
                        dve.wait_ge(back.filled, back.full(u, ("dS", c)))
                        V.tensor_tensor(state[:, :, :], state[:, :, :], bps(("dS", c)), ALU.add).then_inc(st_ready, 1)
                        if c + 1 < NCH:
                            bd(V, bdt[:, :, :], by_chunk(tT)[:, :, c + 1, :]).then_inc(bdt_r, 1)
                        dve.wait_ge(ee_ready, u * NCH + c + 1)
                        bd(V, bde[:, :, :], Ee).then_inc(bde_r, 1)
                        dve.wait_ge(st_ready, u * (NCH + 1) + c + 2)
                        freed_(back)
                        yield
                    dve.sem_inc(passed, 1)
                    V.tensor_copy(here, state[:, :, :])
                    yield
                    dve.wait_ge(ors_ready, u * 2 + 2)
                    V.tensor_tensor(oTr[:, :], oTr[:, :], orr[:, :], ALU.mult).then_inc(on_ready, 1)
                    yield
                    dve.wait_ge(on_ready, u + 1)
                    dve.wait_ge(gate_ready, u + 1)
                    for b in range(BPU // 2):
                        dve.wait_ge(back.filled, back.full(u, ("proj", b)))
                        ys = y1[:, 2 * b:2 * b + 2, :]
                        bc_.then(V.tensor_tensor(ys, back["proj", b][:, :].rearrange("p (b d) -> p b d", b=2),
                                                 outb[:, :].unsqueeze(1).broadcast_to([P, 2, D]), ALU.add))
                        freed_(back)
                        bc_.then(V.tensor_tensor(ys, ys, gate[:, 2 * b:2 * b + 2, :], ALU.mult))
                        bc_.then(V.tensor_tensor(ys, ys, x[:, 2 * b:2 * b + 2, :], ALU.add))
                    yield
                    for b in range(BPU):
                        ins = V.bn_stats(stats[:, b, :], y1[:, b, :])
                    bc_.then(ins)
                    dve.sem_inc(passed, 1)
                    for b in range(BPU):
                        ins = V.bn_aggr(mv[:, b, :], stats[:, b, :])
                    ins.then_inc(var_ready, 1)
                    yield
                    dve.wait_ge(rstd_ready, u + 1)
                    dve.wait_ge(var_ready, u + 1)
                    for b in range(BPU):
                        ins = V.tensor_scalar(y1[:, b, :], y1[:, b, :], mv[:, b, 0:1], rstd[:, b:b + 1], ALU.subtract, ALU.mult)
                    ins.then_inc(x1_ready, 1)
                    yield
                    bc_.end()

                run(dve, fr, bk)

            @block.tensor
            def _(pe):
                T = nc.tensor

                def fr(u, par, grp, s):
                    x, npT, kqi = xs[par], nps[par], kqis[par]

                    def mm(key, mrows, parts):
                        ps = front.take(pe, u, key)
                        for k, (l, r) in enumerate(parts):
                            ins = T.matmul(ps[0:mrows, :], l, r, start=k == 0, stop=k == len(parts) - 1)
                        ins.then_inc(front.filled, 1)

                    def ctl(m):
                        mm(("ctl", m), P, [(ctrlW[:, e, m * P:(m + 1) * P], xT[:, e, :]) for e in range(2)])

                    def p20(i):
                        mm(("p20", MS[i]), P, [(p20W[:, e, MS[i] * P:(MS[i] + 1) * P], npT[:, e, :]) for e in range(2)])

                    def nrm(i):
                        pe.wait_ge(msq_ready, u * 4 + i + 1)
                        mm(("nrm", MS[i]), P, [(blk[:, :], half(r11, 0))])

                    pe.wait_ge(front_done, u + 1)
                    pe.wait_ge(s_x, u * 16 + 32)
                    for e in range(2):
                        ps = front.take(pe, u, ("xT", e))
                        for j in range(4):
                            ins = T.transpose(ps[:, j * P:(j + 1) * P], x[:, j, :].rearrange("p (c e) -> p e c", e=2)[:, e, :], ident[:, :])
                        ins.then_inc(front.filled, 1)
                    yield
                    pe.wait_ge(xT_ready, u * 2 + 2)
                    for b2 in range(BPU // 2):
                        ps = front.take(pe, u, ("gate", b2))
                        for j in range(2):
                            b = 2 * b2 + j
                            for e in range(2):
                                ins = T.matmul(ps[:, j * D:(j + 1) * D], xT[:, e, b * P:(b + 1) * P], ctrlW[:, e, 3 * D + 2 * H:], start=e == 0, stop=e == 1)
                        ins.then_inc(front.filled, 1)
                    yield
                    for k, n in enumerate(("dec", "bet")):
                        mm((n,), H, [(ctrlW[:, e, 3 * D + k * H:3 * D + (k + 1) * H], xT[:, e, :]) for e in range(2)])
                    yield
                    ctl(MS[0])
                    yield
                    ctl(MS[1])
                    yield
                    pe.wait_ge(sq_ready, u * 2 + 2)
                    mm(("pss",), P, [(ones[:, :], half(R[4], e)) for e in range(2)])
                    ctl(MS[2])
                    yield
                    pe.wait_ge(gcum_ready, u + 1)
                    for hh in range(2):
                        mm(("gi", hh), P, [(sel[:, hh, :], gcum)])
                    ctl(MS[3])
                    yield
                    pe.wait_ge(bet_ready, u + 1)
                    for hh in range(2):
                        mm(("bi", hh), P, [(sel[:, hh, :], bet)])
                    ctl(MS[4])
                    yield
                    ctl(MS[5])
                    yield
                    pe.wait_ge(np_v, u + 1)
                    pe.wait_ge(np_p, u + 1)
                    p20(0)
                    yield
                    p20(1)
                    nrm(0)
                    yield
                    p20(2)
                    nrm(1)
                    yield
                    p20(3)
                    nrm(2)
                    yield
                    p20(4)
                    nrm(3)
                    yield
                    p20(5)
                    yield
                    yield
                    for t in range(G // 8):
                        pe.wait_ge(bd1_ready, u * 8 + t + 1)
                        ps = front.take(pe, u, ("mm1", t))
                        pe.sem_inc(passed, 1)
                        for j in range(8):
                            for r in PAIRS:
                                ins = T.matmul(ps[r, j * 48:(j + 1) * 48], bd1[r, t % 2, j, :],
                                               kqi[r, 8 * t + j, :, :].rearrange("p k i -> p (k i)"), start=True, stop=True)
                        ins.then_inc(front.filled, 1)
                        if t % 2:
                            yield
                    HF = P // 2
                    pe.wait_ge(a_ready, u * 8 + 8)
                    for t in range(2):
                        ps = front.take(pe, u, ("aT", t))
                        pe.sem_inc(passed, 1)
                        for j in range(8):
                            i = 8 * t + j
                            for q in range(2):
                                r = slice(q * HF, (q + 1) * HF)
                                ins = T.matmul(ps[r, j * HF:(j + 1) * HF], aT[r, i * G:(i + 1) * G], ident[r, r], start=True, stop=True)
                        ins.then_inc(front.filled, 1)
                    for t in range(4):
                        ps = front.take(pe, u, ("v1", t))
                        pe.sem_inc(passed, 1)
                        for j in range(4):
                            ins = T.transpose(ps[0:G, j * P:(j + 1) * P], g16(vT)[:, :, 4 * t + j], ident[:, :])
                        ins.then_inc(front.filled, 1)
                    yield
                    pe.wait_ge(vb_ready, u * 4 + 4)
                    for t in range(2):
                        ps = front.take(pe, u, ("v2", t))
                        pe.sem_inc(passed, 1)
                        for j in range(8):
                            v = 8 * t + j
                            ins = T.transpose(ps[:, j * G:(j + 1) * G], vB[0:G, v * P:(v + 1) * P], ident[0:G, 0:G])
                        ins.then_inc(front.filled, 1)
                    yield
                    for _ in range(22, 29):
                        yield
                    pe.wait_ge(inv_ready, u + 1)
                    for t in range(2):
                        ps = front.take(pe, u, ("tT", t))
                        pe.sem_inc(passed, 1)
                        for j in range(8):
                            i = 8 * t + j
                            for q in range(2):
                                r = slice(q * HF, (q + 1) * HF)
                                ins = T.matmul(ps[r, j * G:(j + 1) * G], inv[r, i, :, :].rearrange("p h c -> p (h c)"), ident[r, r], start=True, stop=True)
                        ins.then_inc(front.filled, 1 + (front.pads if t else 0))
                    yield

                def bk(u, par, grp, s):
                    gq, pT, npT = gqs[par], pTs[par], nps[par]

                    def each(key, lhs, rhs):
                        ps = back.take(pe, u, key)
                        pe.sem_inc(passed, 1)
                        for k in range(SETS):
                            for r in PAIRS:
                                ins = T.matmul(ps[r, k * HD:(k + 1) * HD], lhs[r, k, :], rhs[r, k, :], start=True, stop=True)
                        ins.then_inc(back.filled, 1)

                    def outputs(c):
                        ps = back.take(pe, u, ("O", c))
                        pe.wait_ge(bds_r, u * NCH + c + 1)
                        pe.wait_ge(bde_r, u * NCH + c + 1)
                        pe.sem_inc(passed, 1)
                        for k in range(SETS):
                            for r in PAIRS:
                                T.matmul(ps[r, k * HD:(k + 1) * HD], bds[r, k, :], by_chunk(gq)[r, k, c, :], start=True, stop=False)
                            for r in PAIRS:
                                ins = T.matmul(ps[r, k * HD:(k + 1) * HD], bde[r, k, :], by_chunk(pT)[r, k, c, :], start=False, stop=True)
                        ins.then_inc(back.filled, 1)

                    pe.wait_ge(fp_ready, u * 2 + 2)
                    for c in range(NCH):
                        pe.wait_ge(bdk_r, u * NCH + c + 1)
                        pe.wait_ge(st_ready, u * (NCH + 1) + c + 1)
                        each(("X", c), bdk[:, c % 2, :, :], state)
                        if c:
                            outputs(c - 1)
                        yield
                        pe.wait_ge(bdt_r, u * NCH + c + 1)
                        pe.wait_ge(d_ready, u * NCH + c + 1)
                        each(("E", c), bdt, Dd)
                        yield
                        pe.wait_ge(bdc_r, u * NCH + c + 1)
                        pe.wait_ge(ed_ready, u * NCH + c + 1)
                        each(("dS", c), bdc, Ed)
                        yield
                    outputs(NCH - 1)
                    yield
                    pe.wait_ge(osq_ready, u + 1)
                    for hh in range(2):
                        ps = back.take(pe, u, ("on", hh))
                        T.matmul(ps[:, :], blk[:, :], osq[:, hh * COLS:(hh + 1) * COLS], start=True, stop=True).then_inc(back.filled, 1)
                    yield
                    pe.wait_ge(on_ready, u + 1)
                    for b2 in range(BPU // 2):
                        ps = back.take(pe, u, ("proj", b2))
                        for j in range(2):
                            b = 2 * b2 + j
                            for k in range(4):
                                src = oT if k < 2 else npT
                                ins = T.matmul(ps[:, j * D:(j + 1) * D], src[:, k % 2, b * P:(b + 1) * P], outW[:, k, :], start=k == 0, stop=k == 3)
                        ins.then_inc(back.filled, 1)
                    yield
                    yield
                    pe.wait_ge(x1_ready, u + 1)
                    for b2 in range(BPU // 2):
                        ps = back.take(pe, u, ("x1T", b2))
                        for j in range(4):
                            ins = T.transpose(ps[:, j * P:(j + 1) * P], y1[:, 2 * b2 + j // 2, (j % 2) * P:(j % 2 + 1) * P], ident[:, :])
                        ins.then_inc(back.filled, 1)
                    yield
                    pe.wait_ge(x1T_ready, u * 2 + 2)
                    ps = back.take(pe, u, ("lg", 0))
                    for b in range(BPU):
                        for k in range(2):
                            ins = T.matmul(ps[:, b * E:(b + 1) * E], x1T[:, (2 * b + k) * P:(2 * b + k + 1) * P], wgs[:, k, :], start=k == 0, stop=k == 1)
                    ins.then_inc(back.filled, 1 + back.pads)
                    yield
                pe.wait_ge(s_ready, 1)
                run(pe, fr, bk, lead=True)


def route(nc, keep, ident, ones, banks, idx, slot, wk):
    ctx = ExitStack()
    with ctx:
        def sb(name, *shape, dt=F32):
            return ctx.enter_context(nc.sbuf_tensor(name, list(shape), dt))

        def sem(name):
            return ctx.enter_context(nc.semaphore(name))
        TE = TILES * E
        tri = sb("tri", P, P)
        pr = sb("probs", P, TILES, E)
        cand = sb("cand", P, TILES, E)
        rank = sb("rank", P, TILES, E)
        expert = sb("expert_id", P, TILES, E)
        oh = sb("one_hot", P, TOPK, TILES, E)
        tot = sb("totals", P, TOPK, E, TILES)
        run = sb("running", P, TOPK, E, TILES)
        again = sb("restart_at_tile0", P, E, TILES)
        pos = sb("positions", P, TOPK, TILES, E)
        m = sb("per_token", P, 8, TILES)
        own = sb("own_position", P, TOPK, TILES)
        kept = sb("kept", P, TOPK, TILES)
        row = sb("row_in_tile", P, TOPK, TILES)
        tile_ = sb("slot_tile", P, TOPK, TILES)
        ints = sb("ints", P, 3, TOPK * TILES, dt=I32)
        ramp_i = sb("ramp_int", P, TILES * E, dt=I32)
        token = sb("token_id", P, TILES)
        cols_r = sb("cols128", P, P)
        cols_b = sb("cols_blocks", P, BLKS)
        UN = 4
        ohr = sb("row_one_hot", P, UN * TOPK, P)
        rb = sb("tile_one_hot", P, UN * TOPK, BLKS)
        zero = sb("zeros", P, BLKS)
        steps, consts = sem("route_steps"), sem("route_consts")
        exped, cums, lists, used, listed = sem("exped"), sem("cums"), sem("list_operands"), sem("list_used"), sem("listed")
        ramp_used = sem("ramp_used")
        score = keep[:, :, :, :].rearrange("p b s e -> p (b s) e")
        with nc.Block() as block:
            @block.gpsimd
            def _(pool):
                pool.memset(tri[:, :], 1.0).then_inc(consts, 1)
                pool.wait_ge(consts, 1)
                pool.affine_select(out=tri[:, :], in_=tri[:, :], compare_op=ALU.is_ge, fill=0.0, base=0,
                                   pattern=[[1, P]], channel_multiplier=-1).then_inc(consts, 1)
                for k, (pattern, base, mult, width) in enumerate((
                        ([[0, TILES], [-1, E]], E, 0, TE), ([[0, TILES], [1, E]], 0, 0, TE),
                        ([[P, TILES]], 0, 1, TILES), ([[1, P]], 0, 0, P), ([[1, BLKS]], 0, 0, BLKS))):
                    if k:
                        pool.wait_ge(ramp_used, k)
                    pool.iota(ramp_i[:, 0:width], pattern=pattern, base=base, channel_multiplier=mult).then_inc(consts, 1)

            @block.scalar
            def _(act):
                act.wait_ge(steps, 2)
                nc.scalar.activation(pr[:, :, :], pr[:, :, :], ACT.Exp).then_inc(exped, 1)

            @block.vector
            def _(dve):
                V = nc.vector
                st = Steps(dve, steps, 0)
                st.start(0)
                bc = lambda t: t.unsqueeze(2).broadcast_to([P, TILES, E])
                flat = lambda t: t[:, :, :].rearrange("p t e -> p (t e)")
                st.then(V.tensor_reduce(m[:, 0, :], score, AX.X, ALU.max))
                st.then(V.tensor_tensor(pr[:, :, :], score, bc(m[:, 0, :]), ALU.subtract))
                for k, (dst, width) in enumerate(((flat(rank), TE), (flat(expert), TE), (token[:, :], TILES), (cols_r[:, :], P), (cols_b[:, :], BLKS))):
                    dve.wait_ge(consts, 3 + k)
                    V.tensor_copy(dst, ramp_i[:, 0:width]).then_inc(ramp_used, 1)
                V.memset(again[:, :, :], 1.0)
                V.memset(zero[:, :], 0.0)
                dve.wait_ge(ramp_used, 5)
                dve.wait_ge(exped, 1)
                st.then(V.tensor_reduce(m[:, 0, :], pr[:, :, :], AX.X, ALU.add))
                st.then(V.reciprocal(m[:, 0, :], m[:, 0, :]))
                V.memset(again[:, :, 0:1], 0.0)
                st.then(V.tensor_tensor(pr[:, :, :], pr[:, :, :], bc(m[:, 0, :]), ALU.mult))
                for k in range(TOPK):
                    st.then(V.tensor_reduce(m[:, 1 + k, :], pr[:, :, :], AX.X, ALU.max))
                    st.then(V.tensor_tensor(cand[:, :, :], pr[:, :, :], bc(m[:, 1 + k, :]), ALU.is_equal))
                    st.then(V.tensor_tensor(cand[:, :, :], cand[:, :, :], rank[:, :, :], ALU.mult))
                    st.then(V.tensor_reduce(m[:, 3, :], cand[:, :, :], AX.X, ALU.max))
                    st.then(V.tensor_tensor(oh[:, k, :, :], cand[:, :, :], bc(m[:, 3, :]), ALU.is_equal))
                    if k == 0:
                        st.then(V.scalar_tensor_tensor(flat(pr), oh[:, k, :, :].rearrange("p t e -> p (t e)"), -2.0, flat(pr), ALU.mult, ALU.add))
                dve.sem_inc(listed, 1)
                st.then(V.tensor_tensor(m[:, 4, :], m[:, 1, :], m[:, 2, :], ALU.add))
                st.then(V.tensor_scalar(m[:, 4, :], m[:, 4, :], EPS_GATE, None, ALU.max))
                st.then(V.reciprocal(m[:, 4, :], m[:, 4, :]))
                dve.wait_ge(cums, 8)
                for k in range(TOPK):
                    for q in range(2):
                        V.tensor_copy(tot[:, k, :, :].rearrange("p e t -> p t e")[:, q * 64:(q + 1) * 64, :],
                                      banks[4 + 2 * k + q][:, :].rearrange("p (t e) -> p t e", e=E))
                        ins = V.tensor_scalar(pos[:, k, q * 64:(q + 1) * 64, :], banks[2 * k + q][:, :].rearrange("p (t e) -> p t e", e=E), -1.0, None, ALU.add)
                    st.then(ins)
                for k in range(TOPK):
                    fl = lambda t: t.rearrange("p e t -> p (e t)")
                    st.then(V.tensor_tensor_scan(fl(run[:, k, :, :]), fl(again[:, :, :]), fl(tot[:, k, :, :]), 0.0, ALU.mult, ALU.add))
                    st.then(V.tensor_tensor(tot[:, k, :, :], run[:, k, :, :], tot[:, k, :, :], ALU.subtract))
                    if k:
                        st.then(V.tensor_tensor(tot[:, k, :, :], tot[:, k, :, :], run[:, 0, :, TILES - 1:TILES].broadcast_to([P, E, TILES]), ALU.add))
                    pk = pos[:, k, :, :]
                    st.then(V.tensor_tensor(pk, pk, tot[:, k, :, :].rearrange("p e t -> p t e"), ALU.add))
                    st.then(V.tensor_tensor(cand[:, :, :], pk, oh[:, k, :, :], ALU.mult))
                    st.then(V.tensor_reduce(own[:, k, :], cand[:, :, :], AX.X, ALU.add))
                    st.then(V.tensor_tensor(cand[:, :, :], expert[:, :, :], oh[:, k, :, :], ALU.mult))
                    st.then(V.tensor_reduce(m[:, 5, :], cand[:, :, :], AX.X, ALU.add))
                    st.then(V.tensor_scalar(kept[:, k, :], own[:, k, :], float(CAP), None, ALU.is_lt))
                    st.then(V.scalar_tensor_tensor(own[:, k, :], m[:, 5, :], float(CAP), own[:, k, :], ALU.mult, ALU.add))
                    st.then(V.tensor_tensor(m[:, 6, :], own[:, k, :], kept[:, k, :], ALU.mult))
                    V.tensor_copy(slot[:, :, k], m[:, 6, :])
                    st.then(V.tensor_copy(ints[:, 0, k * TILES:(k + 1) * TILES], m[:, 6, :]))
                    st.then(V.tensor_tensor(m[:, 7, :], m[:, 1 + k, :], m[:, 4, :], ALU.mult))
                    st.then(V.tensor_tensor(wk[:, k, :], m[:, 7, :], kept[:, k, :], ALU.mult))
                V.tensor_scalar(ints[:, 1, :], ints[:, 0, :], P - 1, None, ALU.bitwise_and)
                st.then(V.tensor_scalar(ints[:, 2, :], ints[:, 0, :], P.bit_length() - 1, None, ALU.logical_shift_right))
                f2 = lambda t: t[:, :, :].rearrange("p k t -> p (k t)")
                V.tensor_copy(f2(row), ints[:, 1, :])
                V.tensor_scalar(f2(kept), f2(kept), -float(BLKS), float(BLKS), ALU.mult, ALU.add)
                st.then(V.tensor_copy(f2(tile_), ints[:, 2, :]))
                st.then(V.tensor_tensor(f2(tile_), f2(tile_), f2(kept), ALU.add))
                dve.sem_inc(used, UN * TOPK)
                with dve.Fori(0, TILES // UN) as i:
                    for t in range(UN):
                        for k in range(TOPK):
                            n = t * TOPK + k
                            col = bass.ds(i * UN + t, 1)
                            dve.wait_ge(used, i * (UN * TOPK) + n + 1)
                            V.tensor_scalar(ohr[:, n, :], cols_r[:, :], row[:, k, col], None, ALU.is_equal)
                            V.tensor_scalar(rb[:, n, :], cols_b[:, :], tile_[:, k, col], token[:, col], ALU.is_equal, ALU.mult).then_inc(lists, 1)
                dve.wait_ge(cums, 9)
                V.tensor_copy(idx[:, :], banks[0][:, 0:BLKS])
                st.per = st.k

            @block.tensor
            def _(pe):
                pe.wait_ge(consts, 2)
                pe.wait_ge(listed, 1)
                for k in range(TOPK):
                    for q in range(2):
                        rhs = oh[:, k, q * 64:(q + 1) * 64, :].rearrange("p t e -> p (t e)")
                        nc.tensor.matmul(banks[2 * k + q][:, :], tri[:, :], rhs, start=True, stop=True).then_inc(cums, 1)
                        nc.tensor.matmul(banks[4 + 2 * k + q][:, :], ones[:, :], rhs, start=True, stop=True).then_inc(cums, 1)
                pe.wait_ge(lists, 1)
                nc.tensor.matmul(banks[0][:, 0:BLKS], zero[:, 0:P], zero[:, :], start=True, stop=False)
                with pe.Fori(0, TILES // UN) as i:
                    for n in range(UN * TOPK):
                        pe.wait_ge(lists, i * (UN * TOPK) + n + 1)
                        nc.tensor.matmul(banks[0][:, 0:BLKS], ohr[:, n, :], rb[:, n, :], start=False, stop=False).then_inc(used, 1)
                nc.tensor.matmul(banks[0][:, 0:BLKS], zero[:, 0:P], zero[:, :], start=False, stop=True).then_inc(cums, 1)


def experts(nc, x1d, yd, w1, b1, w2, b2, idx, ident, banks):
    ctx = ExitStack()
    with ctx:
        def sb(name, *shape, dt=F32):
            return ctx.enter_context(nc.sbuf_tensor(name, list(shape), dt))

        def sem(name):
            return ctx.enter_context(nc.semaphore(name))
        MT = HID // P
        BPE = CAP // (P * SPB)
        W = SPB * P
        w1s, w2s = sb("w1s", P, 2, 2, HID), sb("w2s", P, 2, MT, D)
        b2s = sb("b2s", P, 2, D)
        b1e = sb("b1_expert", P, 2, MT)
        b1r, b1t = sb("b1_rows", E * MT, P), sb("b1_cols", P, E * MT)
        icur = sb("block_index", P, 2, SPB, dt=U32)
        xg = sb("gathered_rows", P, 2, SPB, D)
        xgT = sb("gathered_T", P, 2, 2, W)
        hT = sb("hidden_T", P, 2, MT, W)
        ysb = sb("result_rows", P, 2, SPB, D)
        w_loaded, b_loaded, expert_done = sem("w_loaded"), sem("b_loaded"), sem("expert_done")
        idx_ready, xg_used = sem("idx_ready"), sem("xg_used")
        gathered = [sem(f"gathered{i}") for i in range(2)]
        xgT_ready, hT_ready, y_ready = sem("xgT_ready"), sem("hT_ready"), sem("y_ready")
        y_stored = [sem(f"y_stored{i}") for i in range(2)]
        filled, b1_ready, b1_cur, passed = sem("filled"), sem("b1_ready"), sem("b1_cur"), sem("wait_passed2")
        freed = {w: sem(f"freed_by_{w}") for w in ("act", "dve")}
        order = []
        for j in range(2):
            order += [(("xT", j, k), "dve") for k in range(2)]
            order += [(("h", j, m), "act") for m in range(MT)]
            order += [(("y", j, t), "dve") for t in range(SPB // 2)]
        ring = Bank(order, banks, filled, freed)

        def loop(eng, body, begin=None, end=None):
            with eng.Fori(0, E // 2) as e2:
                for par in range(2):
                    e = e2 * 2 + par
                    if begin is not None:
                        begin(e, par)
                    with eng.Fori(0, BPE // 2) as j2:
                        for j in range(2):
                            pair = e * (BPE // 2) + j2
                            body(e, par, pair, pair * 2 + j, j)
                    if end is not None:
                        end(e)

        with nc.Block() as block:
            @block.sync
            def _(sp):
                sp.dma_start(b1r[:, :], b1.rearrange("e (m p) -> (e m) p", p=P)).then_inc(b_loaded, 16)

                def body(e, par, pair, n, j):
                    sp.wait_ge(y_ready, n * 2 + 2)
                    sp.dma_start(yd.rearrange("(n i p) d -> p n i d", i=SPB, p=P)[:, bass.ds(n, 1), :, :],
                                 ysb[:, j:j + 1, :, :]).then_inc(y_stored[j], 16)
                loop(sp, body)
                for j in range(2):
                    sp.wait_ge(y_stored[j], 16 * (E * BPE // 2 + 1))

            @block.gpsimd
            def _(pool):
                def begin(e, par):
                    pool.wait_ge(expert_done, e + 1)
                    pool.dma_start(w1s[:, par:par + 1, :, :], w1[bass.ds(e, 1), :, :].rearrange("e (k p) n -> p e k n", p=P)).then_inc(w_loaded, 16)
                    pool.dma_start(w2s[:, par:par + 1, :, :], w2[bass.ds(e, 1), :, :].rearrange("e (k p) n -> p e k n", p=P)).then_inc(w_loaded, 16)
                    pool.dma_start(b2s[:, par, :], b2[bass.ds(e, 1), :].broadcast_to([P, D])).then_inc(w_loaded, 16)

                def body(e, par, pair, n, j):
                    pool.wait_ge(idx_ready, n + 1)
                    pool.wait_ge(xg_used, n + 1)
                    pool.sem_inc(passed, 1)
                    for i in range(SPB):
                        nc.gpsimd.indirect_dma_start(out=xg[:, j, i, :], out_offset=None, in_=x1d[:, :],
                                                     in_offset=bass.IndirectOffsetOnAxis(ap=icur[:, j, i:i + 1], axis=0)).then_inc(gathered[j], 16)
                loop(pool, body, begin)

            @block.vector
            def _(dve):
                V = nc.vector
                dve.sem_inc(xg_used, 2)
                for j in range(2):
                    dve.sem_inc(y_stored[j], 16)
                dve.sem_inc(ring.freed["dve"], ring.count["dve"])

                def body(e, par, pair, n, j):
                    dve.wait_ge(w_loaded, e * 48 + 48)
                    V.tensor_copy(icur[:, j, :], idx[:, bass.ds(n * SPB, SPB)]).then_inc(idx_ready, 1)
                    for k in range(2):
                        dve.wait_ge(filled, ring.full(pair, ("xT", j, k)))
                        V.tensor_copy(xgT[:, j, k, :], ring["xT", j, k][:, :]).then_inc(xgT_ready, 1)
                        dve.wait_ge(xgT_ready, n * 2 + k + 1)
                        dve.sem_inc(ring.freed["dve"], 1)
                    dve.sem_inc(xg_used, 1)
                    dve.wait_ge(y_stored[j], pair * 16 + 16)
                    for t in range(SPB // 2):
                        dve.wait_ge(filled, ring.full(pair, ("y", j, t)))
                        V.tensor_tensor(ysb[:, j, 2 * t:2 * t + 2, :], ring["y", j, t][:, :].rearrange("p (i d) -> p i d", i=2),
                                        b2s[:, par:par + 1, :].broadcast_to([P, 2, D]), ALU.add).then_inc(y_ready, 1)
                        dve.wait_ge(y_ready, n * 2 + t + 1)
                        dve.sem_inc(ring.freed["dve"], 1)
                loop(dve, body)

            @block.scalar
            def _(act):
                act.sem_inc(ring.freed["act"], ring.count["act"])
                act.wait_ge(b1_ready, 1)
                nc.scalar.activation(b1t[:, :], banks[7][:, 0:E * MT], ACT.Copy).then_inc(b1_ready, 1)
                act.wait_ge(b1_ready, 2)

                def begin(e, par):
                    nc.scalar.activation(b1e[:, par, :], b1t[:, bass.ds(e * MT, MT)], ACT.Copy).then_inc(b1_cur, 1)

                def body(e, par, pair, n, j):
                    act.wait_ge(b1_cur, e + 1)
                    for m in range(MT):
                        act.wait_ge(filled, ring.full(pair, ("h", j, m)))
                        nc.scalar.activation(hT[:, j, m, :], ring["h", j, m][:, :], ACT.Gelu,
                                             bias=b1e[:, par, m:m + 1]).then_inc(hT_ready, 1)
                        act.wait_ge(hT_ready, n * MT + m + 1)
                        act.sem_inc(ring.freed["act"], 1)
                loop(act, body, begin)

            @block.tensor
            def _(pe):
                pe.sem_inc(expert_done, 2)
                pe.wait_ge(b_loaded, 16)
                nc.tensor.transpose(banks[7][:, 0:E * MT], b1r[:, :], ident[0:E * MT, 0:E * MT]).then_inc(b1_ready, 1)
                pe.wait_ge(b1_ready, 2)

                def body(e, par, pair, n, j):
                    pe.wait_ge(w_loaded, e * 48 + 48)
                    pe.wait_ge(gathered[j], pair * (16 * SPB) + 16 * SPB)
                    for k in range(2):
                        ps = ring.take(pe, pair, ("xT", j, k))
                        for i in range(SPB):
                            ins = nc.tensor.transpose(ps[:, i * P:(i + 1) * P], xg[:, j, i, k * P:(k + 1) * P], ident[:, :])
                        ins.then_inc(filled, 1)
                    pe.wait_ge(xgT_ready, n * 2 + 2)
                    for m in range(MT):
                        ps = ring.take(pe, pair, ("h", j, m))
                        for k in range(2):
                            ins = nc.tensor.matmul(ps[:, :], w1s[:, par, k, m * P:(m + 1) * P], xgT[:, j, k, :], start=k == 0, stop=k == 1)
                        ins.then_inc(filled, 1)
                    for t in range(SPB // 2):
                        ps = ring.take(pe, pair, ("y", j, t))
                        for i in range(2):
                            for m in range(MT):
                                if t == 0 and i == 0:
                                    pe.wait_ge(hT_ready, n * MT + m + 1)
                                s0 = (2 * t + i) * P
                                ins = nc.tensor.matmul(ps[:, i * D:(i + 1) * D], hT[:, j, m, s0:s0 + P], w2s[:, par, m, :], start=m == 0, stop=m == MT - 1)
                        ins.then_inc(filled, 1)

                def end(e):
                    pe.wait_ge(filled, e * (BPE // 2 * len(order)) + BPE // 2 * len(order))
                    pe.sem_inc(expert_done, 1)
                loop(pe, body, end=end)


def combine(nc, x1d, yd, slot, wk, out):
    ctx = ExitStack()
    with ctx:
        def sb(name, *shape, dt=F32):
            return ctx.enter_context(nc.sbuf_tensor(name, list(shape), dt))

        def sem(name):
            return ctx.enter_context(nc.semaphore(name))
        Q = 4
        NB = 2
        xs, ys = sb("x1_rows_sb", P, NB, Q, D), sb("y_rows_sb", P, NB, Q * TOPK, D)
        o = sb("out_rows", P, NB, Q, D)
        scur = sb("turn_slots", P, NB, Q * TOPK, dt=U32)
        stats, mv, rstd = sb("stats2", P, NB, Q, 6), sb("mv2", P, NB, Q, 2), sb("rstd2", P, NB, Q)
        eps = sb("eps2", P, 1)
        x_loaded = [sem(f"x1_loaded{i}") for i in range(NB)]
        y_loaded = [sem(f"y_loaded{i}") for i in range(NB)]
        scur_ready, used, var_ready, rstd_ready = sem("scur_ready"), sem("rows_used"), sem("var_ready2"), sem("rstd_ready2")
        passed = sem("wait_passed3")
        lns, out_ready, stored, steps = sem("ln_done"), sem("out_ready"), [sem(f"out_stored{i}") for i in range(NB)], sem("combine_steps")
        TURNS = TILES // Q
        STEPS = 1 + TOPK

        def loop(eng, body):
            with eng.Fori(0, TURNS // NB) as i:
                for j in range(NB):
                    body(i * NB + j, i, j)

        rows = lambda t: t.rearrange("(q i p) d -> p q i d", p=P, i=Q)
        with nc.Block() as block:
            @block.sync
            def _(sp):
                def load(n, i, j):
                    sp.wait_ge(used, n + 1)
                    sp.dma_start(xs[:, j:j + 1, :, :], rows(x1d)[:, bass.ds(n, 1), :, :]).then_inc(x_loaded[j], 16)
                loop(sp, load)

            @block.gpsimd
            def _(pool):
                def body(n, i, j):
                    pool.wait_ge(scur_ready, n + 1)
                    pool.wait_ge(used, n + 1)
                    pool.sem_inc(passed, 1)
                    for k in range(Q * TOPK):
                        nc.gpsimd.indirect_dma_start(out=ys[:, j, k, :], out_offset=None, in_=yd[:, :],
                                                     in_offset=bass.IndirectOffsetOnAxis(ap=scur[:, j, k:k + 1], axis=0)).then_inc(y_loaded[j], 16)
                loop(pool, body)

            @block.scalar
            def _(act):
                def body(n, i, j):
                    act.wait_ge(var_ready, n + 2)
                    nc.scalar.activation(rstd[:, j, :], mv[:, j, :, 1], ACT.Ln, bias=eps[:, 0:1]).then_inc(lns, 1)
                    act.wait_ge(lns, n + 1)
                    nc.scalar.activation(rstd[:, j, :], rstd[:, j, :], ACT.Exp, scale=-0.5).then_inc(rstd_ready, 1)
                    act.wait_ge(out_ready, n + 1)
                    act.dma_start(rows(out)[:, bass.ds(n, 1), :, :], o[:, j:j + 1, :, :]).then_inc(stored[j], 16)
                loop(act, body)
                for j in range(NB):
                    act.wait_ge(stored[j], 16 * (TURNS // NB + 1))

            @block.vector
            def _(dve):
                V = nc.vector
                V.memset(eps[:, :], EPS_LN).then_inc(var_ready, 1)
                dve.sem_inc(used, NB)
                for j in range(NB):
                    dve.sem_inc(stored[j], 16)
                dve.wait_ge(var_ready, 1)
                sl = slot[:, :, :].rearrange("p t k -> p (t k)")

                def body(n, i, j):
                    V.tensor_copy(scur[:, j, :], sl[:, bass.ds(n * (Q * TOPK), Q * TOPK)]).then_inc(scur_ready, 1)
                    dve.wait_ge(x_loaded[j], i * 16 + 16)
                    dve.wait_ge(y_loaded[j], i * (16 * Q * TOPK) + 16 * Q * TOPK)
                    dve.wait_ge(stored[j], i * 16 + 16)
                    for k in range(TOPK):
                        for q in range(Q):
                            ins = V.scalar_tensor_tensor(o[:, j, q, :], ys[:, j, q * TOPK + k, :], wk[:, k, bass.ds(n * Q + q, 1)],
                                                         xs[:, j, q, :] if k == 0 else o[:, j, q, :], ALU.mult, ALU.add)
                        ins.then_inc(steps, 1)
                        dve.wait_ge(steps, n * STEPS + k + 1)
                    dve.sem_inc(used, 1)
                    for q in range(Q):
                        ins = V.bn_stats(stats[:, j, q, :], o[:, j, q, :])
                    ins.then_inc(steps, 1)
                    dve.wait_ge(steps, n * STEPS + TOPK + 1)
                    dve.sem_inc(passed, 1)
                    for q in range(Q):
                        ins = V.bn_aggr(mv[:, j, q, :], stats[:, j, q, :])
                    ins.then_inc(var_ready, 1)
                    dve.wait_ge(rstd_ready, n + 1)
                    dve.wait_ge(var_ready, n + 2)
                    for q in range(Q):
                        ins = V.tensor_scalar(o[:, j, q, :], o[:, j, q, :], mv[:, j, q, 0:1], rstd[:, j, q:q + 1], ALU.subtract, ALU.mult)
                    ins.then_inc(out_ready, 1)
                loop(dve, body)


_INS = ["L0_attn_hidden", "L0_attn_p20_decay_log", "L0_attn_p20_theta", "L0_attn_ctrl_W", "L0_attn_ctrl_b",
        "L0_attn_p20c_W", "L0_attn_qconv_w", "L0_attn_kconv_w", "L0_attn_vconv_w", "L0_attn_mnorm_scale",
        "L0_attn_vnorm_scale", "L0_attn_ramp_logit", "L0_attn_out_W", "L0_attn_out_b", "L0_ffn_wg",
        "L0_ffn_w1", "L0_ffn_b1", "L0_ffn_w2", "L0_ffn_b2"]


def kernel(**inputs):
    import numpy as _np
    import concourse.bacc as _bacc
    from concourse import mybir as _mybir
    from concourse.bass_utils import run_bass_kernel_spmd as _run

    nc = _bacc.Bacc("TRN2", target_bir_lowering=False, num_devices=1)
    arrays, args = {}, []
    for name in _INS:
        a = _np.ascontiguousarray(inputs[name])
        arrays[name] = a
        args.append(nc.dram_tensor(name, a.shape, _mybir.dt.from_np(a.dtype), kind="ExternalInput").ap())
    out = nc.dram_tensor("out", (B, S, D), F32, kind="ExternalOutput").ap()
    build(nc, *args, out)
    r = _run(nc, [arrays], core_ids=[0])
    return r.results[0]["out"]
```

```python
import numpy as np
import concourse.bass as bass
from concourse import mybir
from contextlib import ExitStack

F32 = mybir.dt.float32
I32 = mybir.dt.int32
U32 = mybir.dt.uint32
ALU = mybir.AluOpType
ACT = mybir.ActivationFunctionType
AX = mybir.AxisListType

P = 128
B, S, D, H = 16, 1024, 256, 16
HD = D // H
TAPS = 4
CHUNK = 16
HPT = P // HD
E, TOPK, HID = 8, 2, 1024
N = B * S
CAP = -(-TOPK * N // E)
BPU = 4
GROUPS = B // BPU
SLABS = S // P
COLS = BPU * P
NCH = P // CHUNK
SETS = 2 * BPU
G = SETS * NCH
TILES = N // P
BLKS = E * CAP // P
SPB = 4
TILE = 32
PAIRS = [slice(r, r + TILE) for r in range(0, P, TILE)]
ACT_STEPS = dict(p=5, f=14, b=14)
DVE_STEPS = dict(p=10, f=52, b=25)
EPS_RMS, EPS_LN, EPS_GATE = 1e-6, 1e-5, 1e-9
TWO_PI = 2.0 * np.pi


class Bank:

    def __init__(self, order, banks, filled, freed):
        self.order, self.banks, self.filled, self.freed = order, banks, filled, freed
        self.at = {key: i for i, (key, _) in enumerate(order)}
        assert len(self.at) == len(order) and len(order) % len(banks) == 0
        self.count = {w: sum(o == w for _, o in order) for w in freed}
        self.nth, seen = [], {w: 0 for w in freed}
        for _, w in order:
            seen[w] += 1
            self.nth.append(seen[w])
        self.pads = sum(key[0] == "pad" for key, _ in order)
        self.said = 0

    def __getitem__(self, key):
        return self.banks[self.at[key] % len(self.banks)]

    def full(self, u, key):
        return u * len(self.order) + self.at[key] + 1

    def take(self, pe, u, key):
        i = self.at[key]
        assert i == self.said % len(self.order), (key, self.order[self.said % len(self.order)])
        self.said += 1
        if self.said == len(self.order) - self.pads:
            self.said = 0
        j = i - len(self.banks)
        who = self.order[j][1]
        value = u * self.count[who] + self.nth[j] + (self.count[who] if j >= 0 else 0)
        pe.wait_ge(self.freed[who], value)
        return self[key]


class Steps:

    def __init__(self, eng, sem, per):
        self.eng, self.sem, self.per, self.k = eng, sem, per, 0

    def start(self, u):
        self.u, self.k = u, 0

    def then(self, ins):
        self.k += 1
        ins.then_inc(self.sem, 1)
        self.eng.wait_ge(self.sem, self.u * self.per + self.k)

    def end(self):
        assert self.k == self.per, (self.k, self.per)


def build(nc, hidden, decay_log, theta, ctrl_W, ctrl_b, p20c_W, qconv, kconv, vconv, mnorm, vnorm,
          ramp, out_W, out_b, wg, w1, b1, w2, b2, out):
    ctx = ExitStack()
    with ctx:
        x1d = nc.dram_tensor("x1_rows", [N, D], F32, kind="Internal").ap()
        yd = nc.dram_tensor("expert_rows", [E * CAP, D], F32, kind="Internal").ap()
        keep = ctx.enter_context(nc.sbuf_tensor("router_scores", [P, B, SLABS, E], F32))
        ident = ctx.enter_context(nc.sbuf_tensor("ident", [P, P], F32))
        ones = ctx.enter_context(nc.sbuf_tensor("ones", [P, P], F32))
        banks = [ctx.enter_context(nc.psum_tensor(f"bank{i}", [P, 512], F32)) for i in range(8)]
        attention(nc, hidden, decay_log, theta, ctrl_W, ctrl_b, p20c_W, qconv, kconv, vconv, mnorm,
                  vnorm, ramp, out_W, out_b, wg, x1d, keep, ident, ones, banks)
        idx = ctx.enter_context(nc.sbuf_tensor("slot_token", [P, BLKS], U32))
        slot = ctx.enter_context(nc.sbuf_tensor("token_slot", [P, TILES, TOPK], U32))
        wk = ctx.enter_context(nc.sbuf_tensor("token_weight", [P, TOPK, TILES], F32))
        route(nc, keep, ident, ones, banks, idx, slot, wk)
        experts(nc, x1d, yd, w1, b1, w2, b2, idx, ident, banks)
        combine(nc, x1d, yd, slot, wk, out.rearrange("b t d -> (b t) d"))


def attention(nc, hidden, decay_log, theta, ctrl_W, ctrl_b, p20c_W, qconv, kconv, vconv, mnorm,
              vnorm, ramp, out_W, out_b, wg, x1d, keep, ident, ones, banks):
    units = GROUPS * SLABS
    ctx = ExitStack()
    with ctx:
        def sb(name, *shape, dt=F32):
            return ctx.enter_context(nc.sbuf_tensor(name, list(shape), dt))

        def sem(name):
            return ctx.enter_context(nc.semaphore(name))

        ctrlW = sb("ctrlW", P, 2, 3 * D + 2 * H + D)
        p20W = sb("p20W", P, 2, 3 * D)
        outW = sb("outW", P, 4, D)
        wgs = sb("wgs", P, 2, E)
        cb = sb("ctrl_bias", P, 6)
        BP = 32
        cdb = sb("ctrlW_gates", P, 2, BP + H)
        gb = sb("gate_bias", BP + H, 1)
        convw = sb("convw", P, 6, TAPS)
        mn = sb("mn", P, 1)
        vn = sb("vn", P, 2)
        outb = sb("outb_rows", P, D)
        gateb = sb("gateb_rows", P, D)
        blk = sb("head_blocks", P, P)
        hmask = sb("head_mask", P, HPT)
        pmask = sb("pair_mask", P, 2)
        diag = sb("diag16", P, CHUNK)
        upto = sb("upto16", P, CHUNK)
        below = sb("neg_below16", P, CHUNK)
        eps = sb("eps", P, 4)
        cosT = sb("cosT", P, P)
        sinT = sb("sinT", P, P)
        pw = sb("powers", P, 4, 2)
        rdec = sb("rdec", P, 4)
        decay0 = sb("decay_pattern", P, COLS)
        restart = sb("restart_pattern", H, COLS)
        carry = sb("scan_carry", P, GROUPS, 2, BPU)
        csm = sb("carry_small", P, 4, BPU)
        hist = sb("conv_history", P, GROUPS, 6, BPU, TAPS - 1)
        kept_state = sb("delta_state", P, GROUPS, SETS, HD)
        state = sb("delta_state_now", P, SETS, HD)
        W2 = 2 * COLS
        R = {k: sb(f"front{k}", P, W2) for k in (1, 2, 3, 4, 5, 8, 9, 11)}
        r10 = sb("front10", P, 2 * BPU * (P + TAPS - 1))
        inv = sb("inverse", P, CHUNK, HPT // 2, CHUNK)
        bd1 = sb("bd_first", P, 2, 8, TILE)
        vB = sb("values_by_group", P, HD * P)
        def pair(name, *shape):
            return [sb(f"{name}{k}", P, *shape) for k in range(2)]
        xin, xres = sb("x", P, BPU, D), sb("x_residual", P, BPU, D)
        gates, nps = pair("gate", BPU, D), pair("np", 2, COLS)
        kqis, gjs = pair("kqi", G, 3, CHUNK), pair("gj", 6, G)
        gqs, pTs, tTs, kcs, vbs = pair("gq", W2), pair("pT", W2), pair("tT", W2), pair("kc", W2), pair("vbeta", W2)
        bdk = sb("bd_k", P, 2, SETS, TILE)
        bdt = sb("bd_t", P, SETS, TILE)
        bdc = sb("bd_kc", P, SETS, TILE)
        bds = sb("bd_s", P, SETS, TILE)
        bde = sb("bd_e", P, SETS, TILE)
        ch = sb("chain_small", P, 4, SETS, HD)
        oTr = sb("oT", P, W2)
        osq, orr = sb("out_squares", P, W2), sb("out_scales", P, W2)
        x1T = oTr
        stats = sb("stats", P, BPU, 6)
        mv = sb("mv", P, BPU, 2)
        rstd = sb("rstd", P, BPU)

        def half(t, i):
            return t[:, i * COLS:(i + 1) * COLS]

        xT = R[1][:, :].rearrange("p (e n) -> p e n", e=2)
        prod_v, prod_p = R[2], R[3]
        zin, zout = R[4], R[5]
        vT = R[8]
        gi, bi, fdec = R[2], R[3], R[4]
        fP, fA, aT = R[1], R[5], R[2]
        aB = R[3]
        r11 = R[11]
        oT = oTr[:, :].rearrange("p (e n) -> p e n", e=2)
        y1 = orr[:, :].rearrange("p (b d) -> p b d", b=BPU)
        cin = r10[:, :].rearrange("p (a b t) -> p a b t", a=2, t=P + TAPS - 1)
        decx, logx = R[2][0:H, 0:COLS], R[2][0:H, COLS:]
        gcum, bet = R[5][0:H, 0:COLS], R[5][BP:BP + H, COLS:]
        g16 = lambda t: t[:, 0:G * CHUNK].rearrange("p (g i) -> p g i", i=CHUNK)
        by_chunk = lambda t: t[:, 0:G * CHUNK].rearrange("p (s c i) -> p s c i", s=SETS, c=NCH)
        conv_at = [half(R[9], 0), half(R[9], 1), half(R[5], 0), half(R[5], 1), half(vT, 0), half(vT, 1)]
        Xs, Dd, Ee, Ed = (ch[:, k, :, :] for k in range(4))

        passed = sem("wait_passed")
        s_load, s_const, s_x1 = sem("weights_loaded"), sem("constants"), sem("x1_stored")
        s_x, s_res = sem("x_loaded"), sem("residual_loaded")
        res_ready = sem("residual_with_bias")
        s_prep, s_ready = sem("prepared"), sem("setup_done")
        front_done, back_done = sem("front_done"), sem("back_done")
        xT_ready, rot_p, scanned = sem("xT_ready"), sem("rotated_by_pool"), sem("scanned")
        y_v, y_p, sq_ready, rs_ready = sem("y_even"), sem("y_odd"), sem("p20_squares"), sem("p20_rs")
        np_v, np_p = sem("np_even"), sem("np_odd")
        gate_added, gate_ready = sem("gate_added"), sem("gate_ready")
        dec_log, bet_ready, gcum_ready = sem("dec_log"), sem("bet_ready"), sem("gcum_ready")
        gi_ready, bi_ready = sem("gi_ready"), sem("bi_ready")
        cin_ready, conv_done, silu_done, raw_ready = sem("cin_ready"), sem("conv_done"), sem("silu_done"), sem("raw_ready")
        msq_ready, mrs_ready, kq_ready = sem("msq_ready"), sem("mrs_ready"), sem("kq_ready")
        diag_mul, gj_ready, diff_ready = sem("diag_mul"), sem("gj_ready"), sem("diff_ready")
        f_ready, e_ready, fp_ready, sm_ready = sem("f_ready"), sem("e_ready"), sem("fp_ready"), sem("sm_ready")
        bd1_ready, kc_ready = sem("bd1_ready"), sem("kc_ready")
        a_ready, ab_ready, inv_ready = sem("a_ready"), sem("ab_ready"), sem("inv_ready")
        vb_ready = sem("vb_ready")
        bdk_r, bdt_r, bdc_r, bds_r, bde_r = sem("bdk_r"), sem("bdt_r"), sem("bdc_r"), sem("bds_r"), sem("bde_r")
        d_ready, ed_ready, st_ready, ee_ready = sem("d_ready"), sem("ed_ready"), sem("st_ready"), sem("ee_ready")
        osq_ready, ors_ready, on_ready = sem("osq_ready"), sem("ors_ready"), sem("on_ready")
        var_ready, rstd_ready, x1_ready, x1T_ready = sem("var_ready"), sem("rstd_ready"), sem("x1_ready"), sem("x1T_ready")
        filled_f, filled_b = sem("front_filled"), sem("back_filled")
        freed = {(r, w): sem(f"{r}_freed_by_{w}") for r in "fb" for w in ("act", "dve")}
        setup_steps = sem("setup_steps")
        steps = {(r, w): sem(f"{r}_{w}_steps") for r in "pfb" for w in ("act", "dve", "pool")}

        MS = (2, 3, 0, 1, 4, 5)
        TURN = (0, 1, 4, 5, 2, 3)
        order = [(("xT", e), "act") for e in range(2)]
        order += [(("ctl", MS[i]), "act") for i in TURN[0:3]]
        order += [(("gate", b), "dve") for b in range(BPU // 2)]
        order += [(("dec",), "act"), (("ctl", MS[TURN[3]]), "act"), (("pss",), "act")]
        order += [(("ctl", MS[TURN[4]]), "act"), (("ctl", MS[TURN[5]]), "act")]
        for i, m in enumerate(MS):
            order += [(("p20", m), "dve")]
            if i >= 3:
                order += [(("nrm", MS[i - 3]), "act")]
        order += [(("nrm", MS[3]), "act")]
        order += [(("v1", t), "dve") for t in range(4)] + [(("v2", t), "dve") for t in range(2)]
        order += [(("mm1", t), "dve") for t in range(G // 8)]
        order += [(("aT", t), "act") for t in range(2)]
        order += [(("tT", t), "act") for t in range(2)]
        while len(order) % 4:
            order.append((("pad", len(order)), "act"))
        front = Bank(order, banks[0:4], filled_f, {w: freed["f", w] for w in ("act", "dve")})
        order = []
        for c in range(NCH):
            order += [(("X", c), "dve")] + [(("O", c - 1), "act")] * (c > 0) + [(("E", c), "act"), (("dS", c), "dve")]
        order.append((("O", NCH - 1), "act"))
        order += [(("on", hh), "act") for hh in range(2)]
        order += [(("proj", b), "dve") for b in range(BPU)]
        order += [(("x1T", b), "act") for b in range(BPU // 2)]
        order += [(("lg", 0), "act")]
        while len(order) % 4:
            order.append((("pad", len(order)), "act"))
        back = Bank(order, banks[4:8], filled_b, {w: freed["b", w] for w in ("act", "dve")})

        PRE, STAGES = 26, 30
        BACK_FIRST = [k for k in range(STAGES) if k < 6 or k >= 11]
        ROWS = [(1, 8), (8, 11), (11, 13), (13, 15), (15, 16)]

        def weave(fr, pre, bk, lead):
            def ahead():
                for _ in range(PRE):
                    yield fr
                for _ in range(PRE, STAGES):
                    yield pre
            front_ = ahead()

            def step(part):
                if part is not None:
                    next(part, None)
            if lead:
                step(next(front_))
            for k in range(STAGES):
                if lead or k in BACK_FIRST:
                    step(bk)
                    step(next(front_, None))
                else:
                    step(next(front_, None))
                    step(bk)
            for part in (fr, pre, bk):
                assert part is None or next(part, "end") == "end"

        def run(eng, pre, fr, bk, lead=False):
            def at(f, u, par):
                return f(u, par, u % GROUPS, u // GROUPS)
            weave(None, at(pre, 0, 0), None, lead)
            weave(at(fr, 0, 0), at(pre, 1, 1), None, lead)
            with eng.Fori(0, units // 2 - 1) as w:
                weave(at(fr, w * 2 + 1, 1), at(pre, w * 2 + 2, 0), at(bk, w * 2, 0), lead)
                weave(at(fr, w * 2 + 2, 0), at(pre, w * 2 + 3, 1), at(bk, w * 2 + 1, 1), lead)
            weave(at(fr, units - 1, 1), None, at(bk, units - 2, 0), lead)
            weave(None, None, at(bk, units - 1, 1), lead)

        NLOAD = 19 + HPT
        with nc.Block() as block:
            def bd(eng, out_, in_):
                n = in_.shape[1]
                return eng.tensor_tensor(out_.rearrange("p s (h i) -> p s h i", h=2),
                                         in_.unsqueeze(2).broadcast_to([P, n, 2, CHUNK]),
                                         pmask[:, :].unsqueeze(1).unsqueeze(3).broadcast_to([P, n, 2, CHUNK]),
                                         ALU.mult)

            @block.sync
            def _(sp):
                for dst, src in (
                    (ctrlW[:, :, :], ctrl_W.rearrange("(p e) n -> p e n", e=2)),
                    (p20W[:, :, :], p20c_W.rearrange("(p e) n -> p e n", e=2)),
                    (outW[:, 0:2, :], out_W[0:D, :].rearrange("(k p) n -> p k n", p=P)),
                    (outW[:, 2:4, :], out_W[D:2 * D, :].rearrange("(p e) n -> p e n", e=2)),
                    (wgs[:, :, :], wg.rearrange("(k p) n -> p k n", p=P)),
                    (cb[:, :], ctrl_b[0:3 * D].rearrange("(m p) -> p m", p=P)),
                    (cdb[:, :, 0:BP], ctrl_W[:, 3 * D:3 * D + BP].rearrange("(p e) n -> p e n", e=2)),
                    (cdb[:, :, BP:], ctrl_W[:, 3 * D + H:3 * D + 2 * H].rearrange("(p e) n -> p e n", e=2)),
                    (gb[0:H, :], ctrl_b[3 * D:3 * D + H].rearrange("(p o) -> p o", o=1)),
                    (gb[BP:, :], ctrl_b[3 * D + H:3 * D + 2 * H].rearrange("(p o) -> p o", o=1)),
                    (convw[:, 0:2, :], qconv.rearrange("(m p) t -> p m t", p=P)),
                    (convw[:, 2:4, :], kconv.rearrange("(m p) t -> p m t", p=P)),
                    (convw[:, 4:6, :], vconv.rearrange("(m p) t -> p m t", p=P)),
                    (vn[:, :], vnorm.rearrange("(p e) -> p e", e=2)),
                    (outb[:, :], out_b.partition_broadcast(P)),
                    (gateb[:, :], ctrl_b[3 * D + 2 * H:].partition_broadcast(P)),
                    (rdec[:, 0:1], decay_log.rearrange("(p o) -> p o", o=1)),
                    (rdec[:, 1:2], theta.rearrange("(p o) -> p o", o=1)),
                    (r11[:, 0:D], ramp.partition_broadcast(P)),
                ):
                    sp.dma_start(dst, src, allow_slow_non_contiguous=True).then_inc(s_load, 16)
                for h in range(HPT):
                    sp.dma_start(mn[h * HD:(h + 1) * HD, :], mnorm.rearrange("(p o) -> p o", o=1)).then_inc(s_load, 16)

                def rows(dst, u, grp, s, sig):
                    sp.dma_start(dst[:, :, :], hidden[bass.ds(grp * BPU, BPU), bass.ds(s * P, P), :]
                                 .rearrange("b t d -> t b d")).then_inc(sig, 16)

                def pre(u, par, grp, s):
                    sp.wait_ge(xT_ready, u * 2 + 2)
                    rows(xin, u, grp, s, s_x)
                    yield

                def heads(dst, src, sig):
                    for hh in range(2):
                        sp.dma_start(half(dst, hh), src[hh * HPT:(hh + 1) * HPT, :].unsqueeze(1)
                                     .broadcast_to([HPT, HD, COLS])).then_inc(sig, 16)

                def fr(u, par, grp, s):
                    yield
                    yield
                    sp.wait_ge(y_p, u + 1)
                    sp.wait_ge(bet_ready, u + 1)
                    heads(bi, bet, bi_ready)
                    sp.wait_ge(y_v, u + 1)
                    sp.wait_ge(gcum_ready, u + 1)
                    heads(gi, gcum, gi_ready)
                    yield

                def bk(u, par, grp, s):
                    sp.wait_ge(back_done, u + 2)
                    rows(xres, u, grp, s, s_res)
                    for _ in range(STAGES - 1):
                        yield
                    sp.wait_ge(x1_ready, u + 1)
                    sp.dma_start(x1d.rearrange("(b t) d -> t b d", b=B)[bass.ds(s * P, P), bass.ds(grp * BPU, BPU), :],
                                 y1).then_inc(s_x1, 16)
                    yield
                sp.wait_ge(s_ready, 1)
                run(sp, pre, fr, bk)
                sp.wait_ge(s_x1, units * 16 + 16)

            @block.gpsimd
            def _(pool):
                fp_, fc, bc_ = Steps(pool, steps["p", "pool"], 1), Steps(pool, steps["f", "pool"], 3), Steps(pool, steps["b", "pool"], 1)
                pool.memset(ident[:, :], 0.0).then_inc(s_const, 1)
                pool.memset(hmask[:, :], 1.0).then_inc(s_const, 1)
                pool.memset(ones[:, :], 1.0).then_inc(s_const, 1)
                pool.wait_ge(s_const, 3)
                pool.affine_select(out=ident[:, :], in_=ident[:, :], compare_op=ALU.not_equal, fill=1.0, base=0,
                                   pattern=[[-1, P]], channel_multiplier=1).then_inc(s_const, 1)
                pool.affine_select(out=hmask[:, :], in_=hmask[:, :], compare_op=ALU.is_ge, fill=0.0, base=0,
                                   pattern=[[-HD, HPT]], channel_multiplier=1).then_inc(s_const, 1)
                pool.wait_ge(s_const, 5)
                pool.affine_select(out=hmask[:, :], in_=hmask[:, :], compare_op=ALU.is_ge, fill=0.0, base=HD - 1,
                                   pattern=[[HD, HPT]], channel_multiplier=-1).then_inc(s_const, 1)
                pool.wait_ge(s_const, 6)
                pool.tensor_tensor(blk[:, :].rearrange("p (h j) -> p h j", j=HD),
                                   hmask[:, :].unsqueeze(2).broadcast_to([P, HPT, HD]),
                                   ones[:, :].rearrange("p (h j) -> p h j", j=HD), ALU.mult).then_inc(s_const, 1)
                pool.wait_ge(s_const, 7)
                pool.affine_select(out=osq[:, 0:P], in_=blk[:, :], compare_op=ALU.is_ge, fill=0.0, base=0,
                                   pattern=[[1, P]], channel_multiplier=-1).then_inc(s_const, 1)
                pool.wait_ge(s_ready, 1)
                tab = lambda t: t[:, :].unsqueeze(1).broadcast_to([P, BPU, P])
                v3 = lambda t, i: half(t, i).rearrange("p (b t) -> p b t", b=BPU)
                m16 = lambda t: t[:, :].unsqueeze(1).broadcast_to([P, G, CHUNK])

                def pre(u, par, grp, s):
                    fp_.start(u)
                    pool.wait_ge(front_done, u + 1)
                    yield
                    pool.wait_ge(xT_ready, u * 2 + 4)
                    pool.tensor_tensor(v3(prod_p, 0), xT[:, 1, :].rearrange("p (b t) -> p b t", b=BPU), tab(cosT), ALU.mult)
                    fp_.then(pool.tensor_tensor(v3(prod_p, 1), xT[:, 0, :].rearrange("p (b t) -> p b t", b=BPU), tab(sinT), ALU.mult))
                    pool.tensor_tensor(half(zin, 1), half(prod_p, 0), half(prod_p, 1), ALU.subtract).then_inc(rot_p, 1)
                    yield
                    fp_.end()

                def fr(u, par, grp, s):
                    npT, kqi = nps[par], kqis[par]
                    fc.start(u)
                    pool.wait_ge(back_done, u + 1)
                    pool.wait_ge(scanned, u * 2 + 2)
                    pool.wait_ge(rot_p, u + 1)
                    pool.tensor_tensor(v3(prod_p, 0), v3(zout, 1), tab(cosT), ALU.mult)
                    fc.then(pool.tensor_tensor(v3(prod_p, 1), v3(zout, 0), tab(sinT), ALU.mult))
                    pool.tensor_tensor(npT[:, 1, :], half(prod_p, 0), half(prod_p, 1), ALU.add).then_inc(y_p, 1)
                    for _ in range(3):
                        yield
                    pool.wait_ge(rs_ready, u + 1)
                    pool.wait_ge(y_p, u + 1)
                    pool.tensor_tensor(npT[:, 1, :], npT[:, 1, :], half(R[4], 0), ALU.mult).then_inc(np_p, 1)
                    yield
                    pool.wait_ge(gi_ready, u * 32 + 32)
                    pool.wait_ge(np_v, u + 1)
                    pool.wait_ge(np_p, u + 1)
                    pool.tensor_tensor(g16(R[4]), g16(gi), m16(diag), ALU.mult).then_inc(diag_mul, 1)
                    yield
                    pool.wait_ge(bi_ready, u * 32 + 32)
                    pool.wait_ge(gj_ready, u * 2 + 1)
                    pool.tensor_tensor(g16(R[4]), g16(bi), m16(diag), ALU.mult).then_inc(diag_mul, 1)
                    for _ in range(5, 13):
                        yield
                    pool.wait_ge(f_ready, u + 1)
                    pool.wait_ge(kq_ready, u * 4 + 4)
                    first(u, kqi, 0)
                    first(u, kqi, 1)
                    fc.then(pool.tensor_tensor(g16(fP), g16(fdec), m16(upto), ALU.mult))
                    fc.then(pool.tensor_tensor(g16(fdec), g16(fdec), m16(below), ALU.mult))
                    pool.tensor_tensor(g16(fA), g16(fdec), g16(bi), ALU.mult).then_inc(fp_ready, 1)
                    yield
                    for t in range(2, 8):
                        first(u, kqi, t)
                        if t % 2:
                            yield
                    pool.wait_ge(e_ready, u + 1)
                    pool.tensor_tensor(g16(gqs[par]), kqi[:, :, 1, :], g16(r11), ALU.mult).then_inc(fp_ready, 1)
                    yield
                    fc.end()

                def first(u, kqi, t):
                    if t >= 2:
                        pool.wait_ge(front.filled, front.full(u, ("mm1", t - 2)))
                    bd(pool, bd1[:, t % 2, :, :], kqi[:, 8 * t:8 * t + 8, 0, :]).then_inc(bd1_ready, 1)

                def bk(u, par, grp, s):
                    kqi, kc = kqis[par], kcs[par]
                    kview = kqi[:, :, 0, :].rearrange("p (s c) i -> p s c i", c=NCH)
                    pool.wait_ge(back_done, u + 2)
                    pool.wait_ge(front_done, u + 2)
                    bd(pool, bdk[:, 0, :, :], kview[:, :, 0, :]).then_inc(bdk_r, 1)
                    for c in range(NCH):
                        if c:
                            pool.wait_ge(back.filled, back.full(u, ("dS", c - 1)))
                        bd(pool, bdc[:, :, :], by_chunk(kc)[:, :, c, :]).then_inc(bdc_r, 1)
                        yield
                        if c + 1 < NCH:
                            if c:
                                pool.wait_ge(back.filled, back.full(u, ("X", c - 1)))
                            bd(pool, bdk[:, (c + 1) % 2, :, :], kview[:, :, c + 1, :]).then_inc(bdk_r, 1)
                        yield
                        if c == 2:
                            pool.wait_ge(s_res, u * 16 + 16)
                            pool.wait_ge(gate_ready, u + 1)
                            bc_.start(u)
                            bc_.then(pool.tensor_tensor(osq[:, :].rearrange("p (b d) -> p b d", d=D), gates[par][:, :, :],
                                                        outb[:, :].unsqueeze(1).broadcast_to([P, BPU, D]), ALU.mult))
                            pool.tensor_tensor(xres[:, :, :].rearrange("p b d -> p (b d)"), osq[:, :],
                                               xres[:, :, :].rearrange("p b d -> p (b d)"), ALU.add).then_inc(res_ready, 1)
                        yield
                run(pool, pre, fr, bk)

            @block.scalar
            def _(act):
                A = nc.scalar.activation
                act.wait_ge(s_load, NLOAD * 16)
                act.wait_ge(s_prep, 1)
                A(rdec[:, 0:1], rdec[:, 0:1], ACT.Exp).then_inc(s_prep, 1)
                act.wait_ge(s_prep, 2)
                A(rdec[:, 0:1], rdec[:, 0:1], ACT.Exp, scale=-1.0).then_inc(s_prep, 1)
                A(pw[:, 0, 1:2], rdec[:, 1:2], ACT.Sin).then_inc(s_prep, 1)
                A(pw[:, 0, 0:1], rdec[:, 2:3], ACT.Sin).then_inc(s_prep, 1)
                A(r11[:, 0:D], r11[:, 0:D], ACT.Sigmoid).then_inc(s_prep, 1)
                act.wait_ge(s_ready, 1)
                act.sem_inc(front_done, 1)
                act.sem_inc(back_done, 2)
                act.sem_inc(front.freed["act"], front.count["act"])
                act.sem_inc(back.freed["act"], back.count["act"])
                fp_, fc, bc_ = (Steps(act, steps[h, "act"], ACT_STEPS[h]) for h in "pfb")

                def copy(st, bank, u, key, out_, in_, func=ACT.Copy, sig=None, **kw):
                    act.wait_ge(bank.filled, bank.full(u, key))
                    st.then(A(out_, in_, func, **kw))
                    act.sem_inc(bank.freed["act"], 1)
                    if sig is not None:
                        act.sem_inc(sig, 1)

                def rs(st, bank, u, key, out_, scale, e, sig):
                    act.wait_ge(bank.filled, bank.full(u, key))
                    st.then(A(out_, bank[key][:, :], ACT.Ln, scale=scale, bias=eps[:, e:e + 1]))
                    act.sem_inc(bank.freed["act"], 1)
                    A(out_, out_, ACT.Exp, scale=-0.5).then_inc(sig, 1)

                def conv_in(st, u, grp, i):
                    m = MS[TURN[i]]
                    if i >= 2:
                        act.wait_ge(conv_done, u * 6 + i - 1)
                    act.sem_inc(passed, 1)
                    A(cin[:, i % 2, :, 0:TAPS - 1], hist[:, bass.ds(grp, 1), m, :, :].rearrange("p o b t -> p (o b) t"), ACT.Copy)
                    act.wait_ge(front.filled, front.full(u, ("ctl", m)))
                    st.then(A(cin[:, i % 2, :, TAPS - 1:], front["ctl", m][:, :].rearrange("p (b t) -> p b t", b=BPU),
                              ACT.Identity, bias=cb[:, m:m + 1]))
                    act.sem_inc(front.freed["act"], 1)
                    act.sem_inc(cin_ready, 1)
                    A(hist[:, bass.ds(grp, 1), m, :, :].rearrange("p o b t -> p (o b) t"), cin[:, i % 2, :, P:], ACT.Copy).then_inc(cin_ready, 1)

                def silu(u, i):
                    act.wait_ge(conv_done, u * 6 + i + 1)
                    A(conv_at[TURN[i]], conv_at[TURN[i]], ACT.Silu).then_inc(silu_done, 1)

                def square(u, i):
                    if i >= 2:
                        act.wait_ge(front.filled, front.full(u, ("nrm", MS[i - 2])))
                    else:
                        act.wait_ge(cin_ready, u * 12 + 12)
                    act.wait_ge(raw_ready, u * 6 + i + 1)
                    act.sem_inc(passed, 1)
                    A(half(r10, i % 2), conv_at[i], ACT.Square).then_inc(msq_ready, 1)

                def scales(u, i):
                    if i >= 2:
                        act.wait_ge(kq_ready, u * 4 + i - 1)
                    m = MS[i]
                    rs(fc, front, u, ("nrm", m), half(r11, i % 2), float(HD) if m < 2 else 1.0, 1 if m < 2 else 0, mrs_ready)

                def pre(u, par, grp, s):
                    fp_.start(u)
                    act.wait_ge(front_done, u + 1)
                    for e in range(2):
                        copy(fp_, front, u, ("xT", e), xT[:, e, :], front["xT", e][:, :], sig=xT_ready)
                    yield
                    conv_in(fp_, u, grp, 0)
                    yield
                    conv_in(fp_, u, grp, 1)
                    yield
                    conv_in(fp_, u, grp, 2)
                    yield
                    fp_.end()

                def fr(u, par, grp, s):
                    npT, gj = nps[par], gjs[par]
                    GJ, BJ, EC, ECJ, NBG = (gj[:, k, :] for k in range(5))
                    fc.start(u)
                    act.wait_ge(back_done, u + 1)
                    act.wait_ge(y_v, u + 1)
                    act.wait_ge(y_p, u + 1)
                    A(half(R[4], 0), npT[:, 0, :], ACT.Square).then_inc(sq_ready, 1)
                    A(half(R[4], 1), npT[:, 1, :], ACT.Square).then_inc(sq_ready, 1)
                    yield
                    act.wait_ge(gate_added, u * 2 + 2)
                    A(gates[par][:, :, :], gates[par][:, :, :], ACT.Sigmoid).then_inc(gate_ready, 1)
                    act.wait_ge(front.filled, front.full(u, ("dec",)))
                    A(decx, front["dec",][0:H, :], ACT.Identity, bias=gb[0:H, :])
                    A(bet, front["dec",][BP:BP + H, :], ACT.Sigmoid, bias=gb[BP:, :]).then_inc(bet_ready, 1)
                    act.wait_ge(bet_ready, u + 1)
                    act.sem_inc(front.freed["act"], 1)
                    conv_in(fc, u, grp, 3)
                    yield
                    nc.scalar.preload_act_table_set("natural_log_exp_and_others")
                    fc.then(A(logx, decx, ACT.Abs))
                    fc.then(A(logx, logx, ACT.Exp, scale=-1.0))
                    A(logx, logx, ACT.Ln, bias=1.0).then_inc(dec_log, 1)
                    yield
                    rs(fc, front, u, ("pss",), half(R[4], 0), 1.0 / D, 0, rs_ready)
                    yield
                    conv_in(fc, u, grp, 4)
                    yield
                    conv_in(fc, u, grp, 5)
                    yield
                    yield
                    for i in range(6):
                        silu(u, i)
                    nc.scalar.preload_act_table_set("natural_log_exp_and_others")
                    square(u, 0)
                    yield
                    square(u, 1)
                    yield
                    for i in range(4):
                        scales(u, i)
                        if i < 2:
                            square(u, i + 2)
                            yield
                    act.wait_ge(diff_ready, u + 1)
                    A(g16(fdec), g16(fdec), ACT.Exp).then_inc(f_ready, 1)
                    A(EC, g16(gi)[:, :, CHUNK - 1], ACT.Exp)
                    A(ECJ, ECJ, ACT.Exp)
                    A(NBG, GJ, ACT.Exp).then_inc(sm_ready, 1)
                    yield
                    act.wait_ge(kq_ready, u * 4 + 4)
                    A(r11[:, :], gi[:, :], ACT.Exp).then_inc(e_ready, 1)
                    for _ in range(12, 15):
                        yield
                    for t in range(8):
                        key = ("mm1", t)
                        act.wait_ge(front.filled, front.full(u, key))
                        A(g16(kcs[par])[:, 8 * t:8 * t + 8, :],
                          front[key][:, 0:384].rearrange("p (g k i) -> p g k i", k=3, i=CHUNK)[:, :, 2, :], ACT.Copy).then_inc(kc_ready, 1)
                        if t % 2:
                            yield
                    for t in range(2):
                        copy(fc, front, u, ("aT", t), aB[:, t * 512:(t + 1) * 512], front["aT", t][:, :], sig=ab_ready)
                    for _ in range(19, 24):
                        yield
                    for t in range(2):
                        act.wait_ge(front.filled, front.full(u, ("tT", t)))
                        fc.then(A(g16(tTs[par]).rearrange("p g i -> p i g")[:, 8 * t:8 * t + 8, :],
                                  front["tT", t][:, :].rearrange("p (i g) -> p i g", i=8), ACT.Copy))
                        act.sem_inc(front.freed["act"], 1 + (front.pads if t else 0))
                    act.sem_inc(front_done, 1)
                    yield
                    fc.end()

                def o_copy(u, c):
                    copy(bc_, back, u, ("O", c), oTr[:, :].rearrange("p (s c i) -> p s c i", s=SETS, c=NCH)[:, :, c, :],
                         back["O", c][:, 0:SETS * CHUNK].rearrange("p (s i) -> p s i", i=CHUNK))

                def bk(u, par, grp, s):
                    bc_.start(u)
                    act.wait_ge(back_done, u + 2)
                    act.wait_ge(s_x1, u * 16 + 16)
                    for c in range(NCH):
                        yield
                        if c:
                            o_copy(u, c - 1)
                        act.wait_ge(back.filled, back.full(u, ("E", c)))
                        act.wait_ge(ed_ready, u * NCH + c + 1)
                        act.sem_inc(passed, 1)
                        A(Ee, back["E", c][:, 0:SETS * HD].rearrange("p (s v) -> p s v", v=HD), ACT.Copy).then_inc(ee_ready, 1)
                        act.wait_ge(ee_ready, u * NCH + c + 1)
                        act.sem_inc(back.freed["act"], 1)
                        yield
                        yield
                    o_copy(u, NCH - 1)
                    act.wait_ge(res_ready, u + 1)
                    A(osq[:, :], oTr[:, :], ACT.Square).then_inc(osq_ready, 1)
                    yield
                    for hh in range(2):
                        act.wait_ge(back.filled, back.full(u, ("on", hh)))
                        bc_.then(A(half(orr, hh), back["on", hh][:, :], ACT.Ln, scale=1.0 / HD, bias=eps[:, 0:1]))
                        act.sem_inc(back.freed["act"], 1)
                    A(orr[:, :], orr[:, :], ACT.Exp, scale=-0.5).then_inc(ors_ready, 1)
                    yield
                    yield
                    act.wait_ge(var_ready, u + 1)
                    bc_.then(A(rstd[:, :], mv[:, :, 1], ACT.Ln, bias=eps[:, 2:3]))
                    A(rstd[:, :], rstd[:, :], ACT.Exp, scale=-0.5).then_inc(rstd_ready, 1)
                    yield
                    for b in range(BPU // 2):
                        copy(bc_, back, u, ("x1T", b), x1T[:, b * 512:(b + 1) * 512], back["x1T", b][:, :], sig=x1T_ready)
                    yield
                    act.wait_ge(back.filled, back.full(u, ("lg", 0)))
                    act.sem_inc(passed, 1)
                    bc_.then(A(keep[:, bass.ds(grp * BPU, BPU), bass.ds(s, 1), :],
                               back["lg", 0][:, 0:BPU * E].rearrange("p (b o e) -> p b o e", o=1, e=E), ACT.Copy))
                    act.sem_inc(back.freed["act"], 1 + back.pads)
                    act.sem_inc(back_done, 1)
                    yield
                    bc_.end()

                run(act, pre, fr, bk)

            @block.vector
            def _(dve):
                V = nc.vector
                setup = [0]

                def link(ins):
                    setup[0] += 1
                    ins.then_inc(setup_steps, 1)
                    dve.wait_ge(setup_steps, setup[0])
                dve.wait_ge(s_load, NLOAD * 16)
                dve.wait_ge(s_const, 8)
                link(V.tensor_scalar(rdec[:, 2:3], rdec[:, 1:2], 1.0 / TWO_PI, 12582912.0, ALU.mult, ALU.add))
                link(V.tensor_scalar(rdec[:, 2:3], rdec[:, 2:3], -12582912.0, None, ALU.add))
                link(V.scalar_tensor_tensor(rdec[:, 1:2], rdec[:, 2:3], -6.28125, rdec[:, 1:2], ALU.mult, ALU.add))
                link(V.scalar_tensor_tensor(rdec[:, 1:2], rdec[:, 2:3], -(TWO_PI - 6.28125), rdec[:, 1:2], ALU.mult, ALU.add))
                link(V.tensor_scalar(rdec[:, 1:2], rdec[:, 1:2], float(np.float32(3.1415925)), float(np.float32(-3.1415925)), ALU.min, ALU.max))
                link(V.tensor_scalar(rdec[:, 2:3], rdec[:, 1:2], -1.0, None, ALU.mult))
                link(V.tensor_tensor(rdec[:, 2:3], rdec[:, 1:2], rdec[:, 2:3], ALU.max))
                link(V.tensor_scalar(rdec[:, 2:3], rdec[:, 2:3], -1.0, float(np.pi / 2), ALU.mult, ALU.add))
                V.memset(eps[:, 0:1], EPS_RMS)
                V.memset(eps[:, 1:2], HD * EPS_RMS)
                V.memset(carry[:, :, :, :], 0.0)
                V.memset(hist[:, :, :, :, :], 0.0)
                V.memset(kept_state[:, :, :, :], 0.0)
                link(V.memset(eps[:, 2:3], EPS_LN))
                dve.sem_inc(s_prep, 1)
                link(V.tensor_reduce(diag[:, :], ident[:, :].rearrange("p (h i) -> p i h", h=HPT), AX.X, ALU.add))
                link(V.tensor_reduce(upto[:, :], osq[:, 0:P].rearrange("p (h i) -> p i h", h=HPT), AX.X, ALU.add))
                link(V.tensor_reduce(pmask[:, :], hmask[:, :].rearrange("p (q a) -> p a q", a=2), AX.X, ALU.add))
                link(V.tensor_tensor(below[:, :], diag[:, :], upto[:, :], ALU.subtract))
                for kqi in kqis:
                    V.tensor_copy(kqi[:, :, 2, :], diag[:, :].unsqueeze(1).broadcast_to([P, G, CHUNK]))
                V.memset(inv[:, :, :, :], 0.0)
                V.memset(restart[:, :], 1.0)
                V.memset(cosT[:, 0:1], 1.0)
                link(V.memset(sinT[:, 0:1], 0.0))
                for i in range(CHUNK):
                    V.memset(inv[:, i, :, i:i + 1], 1.0)
                link(V.memset(restart[:, :].rearrange("p (g i) -> p g i", i=CHUNK)[:, :, 0:1], 0.0))
                for e in range(2):
                    V.tensor_scalar(p20W[:, e, :], p20W[:, e, :], vn[:, e:e + 1], None, ALU.mult)
                    V.tensor_scalar(outW[:, 2 + e, :], outW[:, 2 + e, :], vn[:, e:e + 1], None, ALU.mult)
                    link(V.tensor_scalar(outW[:, e, :], outW[:, e, :], mn[:, 0:1], None, ALU.mult))
                dve.wait_ge(s_prep, 6)
                for e in range(2):
                    link(V.tensor_tensor(p20W[:, e, :].rearrange("p (k n) -> p k n", k=3), p20W[:, e, :].rearrange("p (k n) -> p k n", k=3),
                                         r11[:, 0:D].unsqueeze(1).broadcast_to([P, 3, D]), ALU.mult))
                link(V.memset(decay0[:, :], 1.0))
                link(V.tensor_scalar(decay0[:, :], decay0[:, :], rdec[:, 0:1], None, ALU.mult))
                link(V.memset(decay0[:, :].rearrange("p (b t) -> p b t", b=BPU)[:, :, 0:1], 0.0))
                n = 1
                while n < P:
                    link(V.tensor_scalar(pw[:, 2, :], pw[:, 0, :], pw[:, 0, 1:2], None, ALU.mult))
                    c0, s0 = pw[:, 0, 0:1], pw[:, 0, 1:2]
                    link(V.tensor_scalar(cosT[:, n:2 * n], sinT[:, 0:n], s0, -1.0, ALU.mult, ALU.mult))
                    link(V.scalar_tensor_tensor(cosT[:, n:2 * n], cosT[:, 0:n], c0, cosT[:, n:2 * n], ALU.mult, ALU.add))
                    link(V.tensor_scalar(sinT[:, n:2 * n], cosT[:, 0:n], s0, None, ALU.mult))
                    link(V.scalar_tensor_tensor(sinT[:, n:2 * n], sinT[:, 0:n], c0, sinT[:, n:2 * n], ALU.mult, ALU.add))
                    link(V.scalar_tensor_tensor(pw[:, 1, 0:1], c0, c0, pw[:, 2, 1:2], ALU.mult, ALU.subtract))
                    link(V.tensor_scalar(pw[:, 1, 1:2], pw[:, 2, 0:1], 2.0, None, ALU.mult))
                    link(V.tensor_copy(pw[:, 0, :], pw[:, 1, :]))
                    n *= 2
                dve.sem_inc(front.freed["dve"], front.count["dve"])
                dve.sem_inc(back.freed["dve"], back.count["dve"])
                dve.sem_inc(s_x1, 16)
                dve.sem_inc(xT_ready, 2)
                dve.sem_inc(s_ready, 1)
                fp_, fc, bc_ = (Steps(dve, steps[h, "dve"], DVE_STEPS[h]) for h in "pfb")
                tab = lambda t: t[:, :].unsqueeze(1).broadcast_to([P, BPU, P])
                v3 = lambda t, i: half(t, i).rearrange("p (b t) -> p b t", b=BPU)
                xb = lambda e: xT[:, e, :].rearrange("p (b t) -> p b t", b=BPU)

                def freed_(bank, n=1):
                    dve.sem_inc(bank.freed["dve"], n)

                def conv(fc, u, i):
                    m = MS[TURN[i]]
                    dve.wait_ge(cin_ready, u * 12 + 2 * i + 1)
                    o = conv_at[TURN[i]].rearrange("p (b t) -> p b t", b=BPU)
                    for k in range(TAPS):
                        src = cin[:, i % 2, :, TAPS - 1 - k:TAPS - 1 - k + P]
                        w = convw[:, m, TAPS - 1 - k:TAPS - k]
                        if k == 0:
                            fc.then(V.tensor_scalar(o, src, w, None, ALU.mult))
                        elif k < TAPS - 1:
                            fc.then(V.scalar_tensor_tensor(o, src, w, o, ALU.mult, ALU.add))
                        else:
                            V.scalar_tensor_tensor(o, src, w, o, ALU.mult, ALU.add).then_inc(conv_done, 1)

                def raw(u, i):
                    key = ("p20", MS[i])
                    dve.wait_ge(silu_done, u * 6 + TURN.index(i) + 1)
                    dve.wait_ge(front.filled, front.full(u, key))
                    V.tensor_tensor(conv_at[i], conv_at[i], front[key][:, :], ALU.add).then_inc(raw_ready, 1)
                    dve.wait_ge(raw_ready, u * 6 + i + 1)
                    freed_(front)

                def kq(u, i, kqi):
                    m = MS[i]
                    dve.wait_ge(mrs_ready, u * 4 + i + 1)
                    V.tensor_tensor(kqi[:, (m % 2) * (G // 2):(m % 2 + 1) * (G // 2), 0 if m >= 2 else 1, :],
                                    conv_at[i].rearrange("p (g i) -> p g i", i=CHUNK),
                                    half(r11, i % 2).rearrange("p (g i) -> p g i", i=CHUNK), ALU.mult).then_inc(kq_ready, 1)

                def now(grp):
                    return carry[:, bass.ds(grp, 1), :, :].rearrange("p o e b -> p (o e) b")

                def pre(u, par, grp, s):
                    fp_.start(u)
                    dve.wait_ge(front_done, u + 1)
                    yield
                    dve.wait_ge(xT_ready, u * 2 + 4)
                    V.tensor_tensor(v3(prod_v, 0), xb(0), tab(cosT), ALU.mult)
                    fp_.then(V.tensor_tensor(v3(prod_v, 1), xb(1), tab(sinT), ALU.mult))
                    fp_.then(V.tensor_tensor(half(zin, 0), half(prod_v, 0), half(prod_v, 1), ALU.add))
                    yield
                    dve.wait_ge(rot_p, u + 1)
                    cr = now(grp)
                    for e in range(2):
                        fp_.then(V.scalar_tensor_tensor(v3(zin, e)[:, :, 0], cr[:, e, :], rdec[:, 0:1], v3(zin, e)[:, :, 0], ALU.mult, ALU.add))
                    for e in range(2):
                        V.tensor_tensor_scan(half(zout, e), decay0[:, :], half(zin, e), 0.0, ALU.mult, ALU.add).then_inc(scanned, 1)
                    conv(fp_, u, 0)
                    yield
                    conv(fp_, u, 1)
                    yield
                    fp_.end()

                def fr(u, par, grp, s):
                    npT, kqi, gate, pT = nps[par], kqis[par], gates[par], pTs[par]
                    GJ, BJ, EC, ECJ, NBG = (gjs[par][:, k, :] for k in range(5))
                    cr = now(grp)
                    fc.start(u)
                    dve.wait_ge(back_done, u + 1)
                    dve.wait_ge(scanned, u * 2 + 2)
                    V.tensor_tensor(v3(prod_v, 0), v3(zout, 0), tab(cosT), ALU.mult)
                    fc.then(V.tensor_tensor(v3(prod_v, 1), v3(zout, 1), tab(sinT), ALU.mult))
                    zr, zi = v3(zout, 0)[:, :, P - 1], v3(zout, 1)[:, :, P - 1]
                    V.tensor_scalar(csm[:, 0, :], zi, pw[:, 0, 1:2], None, ALU.mult)
                    fc.then(V.tensor_scalar(csm[:, 1, :], zr, pw[:, 0, 1:2], None, ALU.mult))
                    V.scalar_tensor_tensor(cr[:, 0, :], zr, pw[:, 0, 0:1], csm[:, 0, :], ALU.mult, ALU.subtract)
                    V.scalar_tensor_tensor(cr[:, 1, :], zi, pw[:, 0, 0:1], csm[:, 1, :], ALU.mult, ALU.add)
                    V.tensor_tensor(npT[:, 0, :], half(prod_v, 0), half(prod_v, 1), ALU.subtract).then_inc(y_v, 1)
                    for b in range(BPU // 2):
                        dve.wait_ge(front.filled, front.full(u, ("gate", b)))
                        V.tensor_tensor(gate[:, 2 * b:2 * b + 2, :], front["gate", b][:, :].rearrange("p (b d) -> p b d", b=2),
                                        gateb[:, :].unsqueeze(1).broadcast_to([P, 2, D]), ALU.add).then_inc(gate_added, 1)
                        dve.wait_ge(gate_added, u * 2 + b + 1)
                        freed_(front)
                    yield
                    conv(fc, u, 2)
                    yield
                    conv(fc, u, 3)
                    dve.wait_ge(dec_log, u + 1)
                    fc.then(V.scalar_tensor_tensor(logx, decx, 0.0, logx, ALU.min, ALU.subtract))
                    V.tensor_tensor_scan(gcum, restart[:, :], logx, 0.0, ALU.mult, ALU.add).then_inc(gcum_ready, 1)
                    yield
                    dve.wait_ge(rs_ready, u + 1)
                    dve.wait_ge(y_v, u + 1)
                    V.tensor_tensor(npT[:, 0, :], npT[:, 0, :], half(R[4], 0), ALU.mult).then_inc(np_v, 1)
                    yield
                    yield
                    dve.wait_ge(diag_mul, u * 2 + 1)
                    V.tensor_reduce(GJ, g16(R[4]), AX.X, ALU.add).then_inc(gj_ready, 1)
                    dve.wait_ge(bi_ready, u * 32 + 32)
                    conv(fc, u, 4)
                    yield
                    conv(fc, u, 5)
                    raw(u, 0)
                    yield
                    dve.wait_ge(diag_mul, u * 2 + 2)
                    V.tensor_reduce(BJ, g16(R[4]), AX.X, ALU.add).then_inc(gj_ready, 1)
                    dve.wait_ge(gj_ready, u * 2 + 2)
                    fc.then(V.tensor_tensor(g16(fdec), g16(gi), GJ.unsqueeze(2).broadcast_to([P, G, CHUNK]), ALU.subtract))
                    V.tensor_scalar(g16(fdec), g16(fdec), 0.0, None, ALU.min)
                    V.tensor_tensor(ECJ, g16(gi)[:, :, CHUNK - 1], GJ, ALU.subtract).then_inc(diff_ready, 1)
                    raw(u, 1)
                    yield
                    raw(u, 2)
                    yield
                    raw(u, 3)
                    kq(u, 0, kqi)
                    yield
                    raw(u, 4)
                    kq(u, 1, kqi)
                    yield
                    raw(u, 5)
                    kq(u, 2, kqi)
                    kq(u, 3, kqi)
                    yield
                    dve.wait_ge(sm_ready, u + 1)
                    V.scalar_tensor_tensor(NBG, BJ, -1.0, NBG, ALU.mult, ALU.mult)
                    for t in range(4):
                        dve.wait_ge(front.filled, front.full(u, ("v1", t)))
                        fc.then(V.tensor_copy(vB[0:G, :].rearrange("p (v h j) -> p j h v", v=HD, h=HPT)[:, 4 * t:4 * t + 4, :, :],
                                              front["v1", t][0:G, :].rearrange("p (j h v) -> p j h v", j=4, h=HPT)))
                        freed_(front)
                        dve.sem_inc(vb_ready, 1)
                        if t == 1:
                            yield
                    yield
                    for t in range(2):
                        dve.wait_ge(front.filled, front.full(u, ("v2", t)))
                        fc.then(V.tensor_tensor(g16(vbs[par]).rearrange("p g v -> p v g")[:, 8 * t:8 * t + 8, :],
                                                front["v2", t][:, :].rearrange("p (v g) -> p v g", v=8),
                                                BJ.unsqueeze(1).broadcast_to([P, 8, G]), ALU.mult))
                        freed_(front)
                    yield
                    dve.wait_ge(fp_ready, u * 2 + 1)
                    for t in range(G // 8):
                        key = ("mm1", t)
                        dve.wait_ge(front.filled, front.full(u, key))
                        dve.wait_ge(kc_ready, u * 8 + t + 1)
                        ps = front[key][:, 0:384].rearrange("p (g k i) -> p g k i", k=3, i=CHUNK)
                        gs = slice(8 * t, 8 * t + 8)
                        if t == 0:
                            dve.wait_ge(e_ready, u + 1)
                        V.tensor_tensor(aT[:, :].rearrange("p (i g) -> p g i", i=CHUNK)[:, gs, :], ps[:, :, 0, :], g16(fA)[:, gs, :], ALU.mult)
                        V.tensor_tensor(g16(pT)[:, gs, :], ps[:, :, 1, :], g16(fP)[:, gs, :], ALU.mult).then_inc(a_ready, 1)
                        dve.wait_ge(a_ready, u * 8 + t + 1)
                        freed_(front)
                        if t % 2:
                            yield
                    yield
                    dve.wait_ge(ab_ready, u * 2 + 2)
                    aBv = aB[:, :].rearrange("p (i h j) -> p i h j", i=CHUNK, h=HPT // 2)
                    for k, (i0, i1) in enumerate(ROWS):
                        for i in range(i0, i1):
                            pr = R[5][:, 0:HPT // 2 * i * i].rearrange("p (h c j) -> p h c j", h=HPT // 2, c=i)
                            fc.then(V.tensor_tensor(pr, aBv[:, i, :, 0:i].unsqueeze(2).broadcast_to([P, HPT // 2, i, i]),
                                                    inv[:, 0:i, :, 0:i].rearrange("p j h c -> p h c j"), ALU.mult))
                            fc.then(V.tensor_reduce(inv[:, i, :, 0:i], pr, AX.X, ALU.add))
                        if k + 1 == len(ROWS):
                            dve.sem_inc(inv_ready, 1)
                        yield
                    fc.end()

                def bk(u, par, grp, s):
                    tT, vbeta, gate, x = tTs[par], vbs[par], gates[par], xres
                    GJ, BJ, EC, ECJ, NBG = (gjs[par][:, k, :] for k in range(5))
                    colv = lambda t, c: t.rearrange("p (s c) -> p s c", c=NCH)[:, :, c].unsqueeze(2).broadcast_to([P, SETS, HD])
                    bps = lambda key: back[key][:, 0:SETS * HD].rearrange("p (s v) -> p s v", v=HD)
                    here = kept_state[:, bass.ds(grp, 1), :, :].rearrange("p o s v -> p (o s) v")
                    bc_.start(u)
                    dve.wait_ge(back_done, u + 2)
                    dve.wait_ge(front_done, u + 2)
                    dve.wait_ge(s_x1, u * 16 + 16)
                    dve.sem_inc(passed, 1)
                    V.tensor_copy(state[:, :, :], here).then_inc(st_ready, 1)
                    bd(V, bdt[:, :, :], by_chunk(tT)[:, :, 0, :]).then_inc(bdt_r, 1)
                    dve.wait_ge(st_ready, u * (NCH + 1) + 1)
                    for c in range(NCH):
                        dve.wait_ge(back.filled, back.full(u, ("X", c)))
                        bc_.then(V.tensor_tensor(Xs, bps(("X", c)), colv(NBG, c), ALU.mult))
                        freed_(back)
                        V.tensor_tensor(Dd, Xs, by_chunk(vbeta)[:, :, c, :], ALU.add).then_inc(d_ready, 1)
                        yield
                        dve.wait_ge(back.filled, back.full(u, ("E", c)))
                        V.tensor_tensor(Ed, bps(("E", c)), colv(ECJ, c), ALU.mult).then_inc(ed_ready, 1)
                        if c:
                            dve.wait_ge(back.filled, back.full(u, ("O", c - 1)))
                        bd(V, bds[:, :, :], state[:, :, :]).then_inc(bds_r, 1)
                        yield
                        dve.wait_ge(bds_r, u * NCH + c + 1)
                        bc_.then(V.tensor_tensor(state[:, :, :], state[:, :, :], colv(EC, c), ALU.mult))
                        dve.wait_ge(back.filled, back.full(u, ("dS", c)))
                        V.tensor_tensor(state[:, :, :], state[:, :, :], bps(("dS", c)), ALU.add).then_inc(st_ready, 1)
                        if c + 1 < NCH:
                            bd(V, bdt[:, :, :], by_chunk(tT)[:, :, c + 1, :]).then_inc(bdt_r, 1)
                        dve.wait_ge(ee_ready, u * NCH + c + 1)
                        bd(V, bde[:, :, :], Ee).then_inc(bde_r, 1)
                        dve.wait_ge(st_ready, u * (NCH + 1) + c + 2)
                        freed_(back)
                        yield
                    dve.sem_inc(passed, 1)
                    V.tensor_copy(here, state[:, :, :])
                    yield
                    dve.wait_ge(ors_ready, u + 1)
                    V.tensor_tensor(oTr[:, :], oTr[:, :], orr[:, :], ALU.mult).then_inc(on_ready, 1)
                    yield
                    dve.wait_ge(on_ready, u + 1)
                    dve.wait_ge(res_ready, u + 1)
                    for b in range(BPU):
                        dve.wait_ge(back.filled, back.full(u, ("proj", b)))
                        bc_.then(V.tensor_tensor(y1[:, b, :], back["proj", b][:, 0:D], gate[:, b, :], ALU.mult))
                        freed_(back)
                        bc_.then(V.tensor_tensor(y1[:, b, :], y1[:, b, :], xres[:, b, :], ALU.add))
                        ins = V.bn_stats(stats[:, b, :], y1[:, b, :])
                    yield
                    bc_.then(ins)
                    dve.sem_inc(passed, 1)
                    for b in range(BPU):
                        ins = V.bn_aggr(mv[:, b, :], stats[:, b, :])
                    ins.then_inc(var_ready, 1)
                    yield
                    dve.wait_ge(rstd_ready, u + 1)
                    dve.wait_ge(var_ready, u + 1)
                    for b in range(BPU):
                        ins = V.tensor_scalar(y1[:, b, :], y1[:, b, :], mv[:, b, 0:1], rstd[:, b:b + 1], ALU.subtract, ALU.mult)
                    ins.then_inc(x1_ready, 1)
                    yield
                    bc_.end()

                run(dve, pre, fr, bk)

            @block.tensor
            def _(pe):
                T = nc.tensor

                def mm(u, key, mrows, parts):
                    ps = front.take(pe, u, key)
                    for k, (l, r) in enumerate(parts):
                        ins = T.matmul(ps[0:mrows, :], l, r, start=k == 0, stop=k == len(parts) - 1)
                    ins.then_inc(front.filled, 1)

                def ctl(u, i):
                    m = MS[TURN[i]]
                    mm(u, ("ctl", m), P, [(ctrlW[:, e, m * P:(m + 1) * P], xT[:, e, :]) for e in range(2)])

                def pre(u, par, grp, s):
                    pe.wait_ge(front_done, u + 1)
                    pe.wait_ge(s_x, u * 16 + 16)
                    for e in range(2):
                        ps = front.take(pe, u, ("xT", e))
                        for j in range(4):
                            ins = T.transpose(ps[:, j * P:(j + 1) * P], xin[:, j, :].rearrange("p (c e) -> p e c", e=2)[:, e, :], ident[:, :])
                        ins.then_inc(front.filled, 1)
                    yield
                    pe.wait_ge(xT_ready, u * 2 + 4)
                    ctl(u, 0)
                    yield
                    ctl(u, 1)
                    yield
                    ctl(u, 2)
                    yield

                def fr(u, par, grp, s):
                    npT, kqi = nps[par], kqis[par]

                    def p20(i):
                        mm(u, ("p20", MS[i]), P, [(p20W[:, e, MS[i] * P:(MS[i] + 1) * P], npT[:, e, :]) for e in range(2)])

                    def nrm(i):
                        pe.wait_ge(msq_ready, u * 4 + i + 1)
                        mm(u, ("nrm", MS[i]), P, [(blk[:, :], half(r10, i % 2))])

                    for b2 in range(BPU // 2):
                        ps = front.take(pe, u, ("gate", b2))
                        for j in range(2):
                            b = 2 * b2 + j
                            for e in range(2):
                                ins = T.matmul(ps[:, j * D:(j + 1) * D], xT[:, e, b * P:(b + 1) * P], ctrlW[:, e, 3 * D + 2 * H:], start=e == 0, stop=e == 1)
                        ins.then_inc(front.filled, 1)
                    yield
                    mm(u, ("dec",), BP + H, [(cdb[:, e, :], xT[:, e, :]) for e in range(2)])
                    ctl(u, 3)
                    yield
                    yield
                    pe.wait_ge(sq_ready, u * 2 + 2)
                    mm(u, ("pss",), P, [(ones[:, :], half(R[4], e)) for e in range(2)])
                    yield
                    ctl(u, 4)
                    yield
                    ctl(u, 5)
                    yield
                    pe.wait_ge(np_v, u + 1)
                    pe.wait_ge(np_p, u + 1)
                    for i in range(6):
                        p20(i)
                        if i >= 3:
                            nrm(i - 3)
                        yield
                    nrm(3)
                    yield
                    pe.wait_ge(raw_ready, u * 6 + 6)
                    for t in range(4):
                        ps = front.take(pe, u, ("v1", t))
                        pe.sem_inc(passed, 1)
                        for j in range(4):
                            ins = T.transpose(ps[0:G, j * P:(j + 1) * P], g16(vT)[:, :, 4 * t + j], ident[:, :])
                        ins.then_inc(front.filled, 1)
                    yield
                    yield
                    pe.wait_ge(vb_ready, u * 4 + 4)
                    for t in range(2):
                        ps = front.take(pe, u, ("v2", t))
                        pe.sem_inc(passed, 1)
                        for j in range(8):
                            v = 8 * t + j
                            ins = T.transpose(ps[:, j * G:(j + 1) * G], vB[0:G, v * P:(v + 1) * P], ident[0:G, 0:G])
                        ins.then_inc(front.filled, 1)
                    for t in range(G // 8):
                        pe.wait_ge(bd1_ready, u * 8 + t + 1)
                        ps = front.take(pe, u, ("mm1", t))
                        pe.sem_inc(passed, 1)
                        for j in range(8):
                            for r in PAIRS:
                                ins = T.matmul(ps[r, j * 48:(j + 1) * 48], bd1[r, t % 2, j, :],
                                               kqi[r, 8 * t + j, :, :].rearrange("p k i -> p (k i)"), start=True, stop=True)
                        ins.then_inc(front.filled, 1)
                        if t % 2:
                            yield
                    yield
                    HF = P // 2
                    pe.wait_ge(a_ready, u * 8 + 8)
                    for t in range(2):
                        ps = front.take(pe, u, ("aT", t))
                        pe.sem_inc(passed, 1)
                        for j in range(8):
                            i = 8 * t + j
                            for q in range(2):
                                r = slice(q * HF, (q + 1) * HF)
                                ins = T.matmul(ps[r, j * HF:(j + 1) * HF], aT[r, i * G:(i + 1) * G], ident[r, r], start=True, stop=True)
                        ins.then_inc(front.filled, 1)
                    for _ in range(20, 25):
                        yield
                    pe.wait_ge(inv_ready, u + 1)
                    for t in range(2):
                        ps = front.take(pe, u, ("tT", t))
                        pe.sem_inc(passed, 1)
                        for j in range(8):
                            i = 8 * t + j
                            for q in range(2):
                                r = slice(q * HF, (q + 1) * HF)
                                ins = T.matmul(ps[r, j * G:(j + 1) * G], inv[r, i, :, :].rearrange("p h c -> p (h c)"), ident[r, r], start=True, stop=True)
                        ins.then_inc(front.filled, 1 + (front.pads if t else 0))
                    yield

                def bk(u, par, grp, s):
                    gq, pT, npT = gqs[par], pTs[par], nps[par]

                    def each(key, lhs, rhs):
                        ps = back.take(pe, u, key)
                        pe.sem_inc(passed, 1)
                        for k in range(SETS):
                            for r in PAIRS:
                                ins = T.matmul(ps[r, k * HD:(k + 1) * HD], lhs[r, k, :], rhs[r, k, :], start=True, stop=True)
                        ins.then_inc(back.filled, 1)

                    def outputs(c, part):
                        if part == 0:
                            back.take(pe, u, ("O", c))
                            pe.wait_ge(bds_r, u * NCH + c + 1)
                            pe.wait_ge(bde_r, u * NCH + c + 1)
                            pe.sem_inc(passed, 1)
                        ps = back["O", c]
                        for k in range(part * SETS // 2, (part + 1) * SETS // 2):
                            for r in PAIRS:
                                T.matmul(ps[r, k * HD:(k + 1) * HD], bds[r, k, :], by_chunk(gq)[r, k, c, :], start=True, stop=False)
                            for r in PAIRS:
                                ins = T.matmul(ps[r, k * HD:(k + 1) * HD], bde[r, k, :], by_chunk(pT)[r, k, c, :], start=False, stop=True)
                        if part == 1:
                            ins.then_inc(back.filled, 1)

                    pe.wait_ge(fp_ready, u * 2 + 2)
                    for c in range(NCH):
                        pe.wait_ge(bdk_r, u * NCH + c + 1)
                        pe.wait_ge(st_ready, u * (NCH + 1) + c + 1)
                        each(("X", c), bdk[:, c % 2, :, :], state)
                        if c:
                            outputs(c - 1, 0)
                        yield
                        if c:
                            outputs(c - 1, 1)
                        pe.wait_ge(bdt_r, u * NCH + c + 1)
                        pe.wait_ge(d_ready, u * NCH + c + 1)
                        each(("E", c), bdt, Dd)
                        yield
                        pe.wait_ge(bdc_r, u * NCH + c + 1)
                        pe.wait_ge(ed_ready, u * NCH + c + 1)
                        each(("dS", c), bdc, Ed)
                        yield
                    outputs(NCH - 1, 0)
                    outputs(NCH - 1, 1)
                    yield
                    pe.wait_ge(osq_ready, u + 1)
                    for hh in range(2):
                        ps = back.take(pe, u, ("on", hh))
                        T.matmul(ps[:, :], blk[:, :], osq[:, hh * COLS:(hh + 1) * COLS], start=True, stop=True).then_inc(back.filled, 1)
                    for b in range(BPU):
                        ps = back.take(pe, u, ("proj", b))
                        for k in (2, 3):
                            T.matmul(ps[:, 0:D], npT[:, k % 2, b * P:(b + 1) * P], outW[:, k, :], start=k == 2, stop=False)
                    yield
                    pe.wait_ge(on_ready, u + 1)
                    for b in range(BPU):
                        for k in range(2):
                            ins = T.matmul(back["proj", b][:, 0:D], oT[:, k, b * P:(b + 1) * P], outW[:, k, :], start=False, stop=k == 1)
                        ins.then_inc(back.filled, 1)
                    yield
                    yield
                    pe.wait_ge(x1_ready, u + 1)
                    for b2 in range(BPU // 2):
                        ps = back.take(pe, u, ("x1T", b2))
                        for j in range(4):
                            ins = T.transpose(ps[:, j * P:(j + 1) * P], y1[:, 2 * b2 + j // 2, (j % 2) * P:(j % 2 + 1) * P], ident[:, :])
                        ins.then_inc(back.filled, 1)
                    yield
                    pe.wait_ge(x1T_ready, u * 2 + 2)
                    ps = back.take(pe, u, ("lg", 0))
                    for b in range(BPU):
                        for k in range(2):
                            ins = T.matmul(ps[:, b * E:(b + 1) * E], x1T[:, (2 * b + k) * P:(2 * b + k + 1) * P], wgs[:, k, :], start=k == 0, stop=k == 1)
                    ins.then_inc(back.filled, 1 + back.pads)
                    yield
                pe.wait_ge(s_ready, 1)
                run(pe, pre, fr, bk, lead=True)


def route(nc, keep, ident, ones, banks, idx, slot, wk):
    ctx = ExitStack()
    with ctx:
        def sb(name, *shape, dt=F32):
            return ctx.enter_context(nc.sbuf_tensor(name, list(shape), dt))

        def sem(name):
            return ctx.enter_context(nc.semaphore(name))
        TE = TILES * E
        tri = sb("tri", P, P)
        pr = sb("probs", P, TILES, E)
        cand = sb("cand", P, TILES, E)
        rank = sb("rank", P, TILES, E)
        expert = sb("expert_id", P, TILES, E)
        oh = sb("one_hot", P, TOPK, TILES, E)
        tot = sb("totals", P, TOPK, E, TILES)
        run = sb("running", P, TOPK, E, TILES)
        again = sb("restart_at_tile0", P, E, TILES)
        pos = sb("positions", P, TOPK, TILES, E)
        m = sb("per_token", P, 8, TILES)
        own = sb("own_position", P, TOPK, TILES)
        kept = sb("kept", P, TOPK, TILES)
        row = sb("row_in_tile", P, TOPK, TILES)
        tile_ = sb("slot_tile", P, TOPK, TILES)
        ints = sb("ints", P, 3, TOPK * TILES, dt=I32)
        ramp_i = sb("ramp_int", P, TILES * E, dt=I32)
        token = sb("token_id", P, TILES)
        cols_r = sb("cols128", P, P)
        cols_b = sb("cols_blocks", P, BLKS)
        UN = 4
        ohr = sb("row_one_hot", P, UN * TOPK, P)
        rb = sb("tile_one_hot", P, UN * TOPK, BLKS)
        zero = sb("zeros", P, BLKS)
        steps, consts = sem("route_steps"), sem("route_consts")
        exped, cums, lists, used, listed = sem("exped"), sem("cums"), sem("list_operands"), sem("list_used"), sem("listed")
        ramp_used = sem("ramp_used")
        score = keep[:, :, :, :].rearrange("p b s e -> p (b s) e")
        with nc.Block() as block:
            @block.gpsimd
            def _(pool):
                pool.memset(tri[:, :], 1.0).then_inc(consts, 1)
                pool.wait_ge(consts, 1)
                pool.affine_select(out=tri[:, :], in_=tri[:, :], compare_op=ALU.is_ge, fill=0.0, base=0,
                                   pattern=[[1, P]], channel_multiplier=-1).then_inc(consts, 1)
                for k, (pattern, base, mult, width) in enumerate((
                        ([[0, TILES], [-1, E]], E, 0, TE), ([[0, TILES], [1, E]], 0, 0, TE),
                        ([[P, TILES]], 0, 1, TILES), ([[1, P]], 0, 0, P), ([[1, BLKS]], 0, 0, BLKS))):
                    if k:
                        pool.wait_ge(ramp_used, k)
                    pool.iota(ramp_i[:, 0:width], pattern=pattern, base=base, channel_multiplier=mult).then_inc(consts, 1)

            @block.scalar
            def _(act):
                act.wait_ge(steps, 2)
                nc.scalar.activation(pr[:, :, :], pr[:, :, :], ACT.Exp).then_inc(exped, 1)

            @block.vector
            def _(dve):
                V = nc.vector
                st = Steps(dve, steps, 0)
                st.start(0)
                bc = lambda t: t.unsqueeze(2).broadcast_to([P, TILES, E])
                flat = lambda t: t[:, :, :].rearrange("p t e -> p (t e)")
                st.then(V.tensor_reduce(m[:, 0, :], score, AX.X, ALU.max))
                st.then(V.tensor_tensor(pr[:, :, :], score, bc(m[:, 0, :]), ALU.subtract))
                for k, (dst, width) in enumerate(((flat(rank), TE), (flat(expert), TE), (token[:, :], TILES), (cols_r[:, :], P), (cols_b[:, :], BLKS))):
                    dve.wait_ge(consts, 3 + k)
                    V.tensor_copy(dst, ramp_i[:, 0:width]).then_inc(ramp_used, 1)
                V.memset(again[:, :, :], 1.0)
                V.memset(zero[:, :], 0.0)
                dve.wait_ge(ramp_used, 5)
                dve.wait_ge(exped, 1)
                st.then(V.tensor_reduce(m[:, 0, :], pr[:, :, :], AX.X, ALU.add))
                st.then(V.reciprocal(m[:, 0, :], m[:, 0, :]))
                V.memset(again[:, :, 0:1], 0.0)
                st.then(V.tensor_tensor(pr[:, :, :], pr[:, :, :], bc(m[:, 0, :]), ALU.mult))
                for k in range(TOPK):
                    st.then(V.tensor_reduce(m[:, 1 + k, :], pr[:, :, :], AX.X, ALU.max))
                    st.then(V.tensor_tensor(cand[:, :, :], pr[:, :, :], bc(m[:, 1 + k, :]), ALU.is_equal))
                    st.then(V.tensor_tensor(cand[:, :, :], cand[:, :, :], rank[:, :, :], ALU.mult))
                    st.then(V.tensor_reduce(m[:, 3, :], cand[:, :, :], AX.X, ALU.max))
                    st.then(V.tensor_tensor(oh[:, k, :, :], cand[:, :, :], bc(m[:, 3, :]), ALU.is_equal))
                    if k == 0:
                        st.then(V.scalar_tensor_tensor(flat(pr), oh[:, k, :, :].rearrange("p t e -> p (t e)"), -2.0, flat(pr), ALU.mult, ALU.add))
                dve.sem_inc(listed, 1)
                st.then(V.tensor_tensor(m[:, 4, :], m[:, 1, :], m[:, 2, :], ALU.add))
                st.then(V.tensor_scalar(m[:, 4, :], m[:, 4, :], EPS_GATE, None, ALU.max))
                st.then(V.reciprocal(m[:, 4, :], m[:, 4, :]))
                dve.wait_ge(cums, 8)
                for k in range(TOPK):
                    for q in range(2):
                        V.tensor_copy(tot[:, k, :, :].rearrange("p e t -> p t e")[:, q * 64:(q + 1) * 64, :],
                                      banks[4 + 2 * k + q][:, :].rearrange("p (t e) -> p t e", e=E))
                        ins = V.tensor_scalar(pos[:, k, q * 64:(q + 1) * 64, :], banks[2 * k + q][:, :].rearrange("p (t e) -> p t e", e=E), -1.0, None, ALU.add)
                    st.then(ins)
                for k in range(TOPK):
                    fl = lambda t: t.rearrange("p e t -> p (e t)")
                    st.then(V.tensor_tensor_scan(fl(run[:, k, :, :]), fl(again[:, :, :]), fl(tot[:, k, :, :]), 0.0, ALU.mult, ALU.add))
                    st.then(V.tensor_tensor(tot[:, k, :, :], run[:, k, :, :], tot[:, k, :, :], ALU.subtract))
                    if k:
                        st.then(V.tensor_tensor(tot[:, k, :, :], tot[:, k, :, :], run[:, 0, :, TILES - 1:TILES].broadcast_to([P, E, TILES]), ALU.add))
                    pk = pos[:, k, :, :]
                    st.then(V.tensor_tensor(pk, pk, tot[:, k, :, :].rearrange("p e t -> p t e"), ALU.add))
                    st.then(V.tensor_tensor(cand[:, :, :], pk, oh[:, k, :, :], ALU.mult))
                    st.then(V.tensor_reduce(own[:, k, :], cand[:, :, :], AX.X, ALU.add))
                    st.then(V.tensor_tensor(cand[:, :, :], expert[:, :, :], oh[:, k, :, :], ALU.mult))
                    st.then(V.tensor_reduce(m[:, 5, :], cand[:, :, :], AX.X, ALU.add))
                    st.then(V.tensor_scalar(kept[:, k, :], own[:, k, :], float(CAP), None, ALU.is_lt))
                    st.then(V.scalar_tensor_tensor(own[:, k, :], m[:, 5, :], float(CAP), own[:, k, :], ALU.mult, ALU.add))
                    st.then(V.tensor_tensor(m[:, 6, :], own[:, k, :], kept[:, k, :], ALU.mult))
                    V.tensor_copy(slot[:, :, k], m[:, 6, :])
                    st.then(V.tensor_copy(ints[:, 0, k * TILES:(k + 1) * TILES], m[:, 6, :]))
                    st.then(V.tensor_tensor(m[:, 7, :], m[:, 1 + k, :], m[:, 4, :], ALU.mult))
                    st.then(V.tensor_tensor(wk[:, k, :], m[:, 7, :], kept[:, k, :], ALU.mult))
                V.tensor_scalar(ints[:, 1, :], ints[:, 0, :], P - 1, None, ALU.bitwise_and)
                st.then(V.tensor_scalar(ints[:, 2, :], ints[:, 0, :], P.bit_length() - 1, None, ALU.logical_shift_right))
                f2 = lambda t: t[:, :, :].rearrange("p k t -> p (k t)")
                V.tensor_copy(f2(row), ints[:, 1, :])
                V.tensor_scalar(f2(kept), f2(kept), -float(BLKS), float(BLKS), ALU.mult, ALU.add)
                st.then(V.tensor_copy(f2(tile_), ints[:, 2, :]))
                st.then(V.tensor_tensor(f2(tile_), f2(tile_), f2(kept), ALU.add))
                dve.sem_inc(used, UN * TOPK)
                with dve.Fori(0, TILES // UN) as i:
                    for t in range(UN):
                        for k in range(TOPK):
                            n = t * TOPK + k
                            col = bass.ds(i * UN + t, 1)
                            dve.wait_ge(used, i * (UN * TOPK) + n + 1)
                            V.tensor_scalar(ohr[:, n, :], cols_r[:, :], row[:, k, col], None, ALU.is_equal)
                            V.tensor_scalar(rb[:, n, :], cols_b[:, :], tile_[:, k, col], token[:, col], ALU.is_equal, ALU.mult).then_inc(lists, 1)
                dve.wait_ge(cums, 9)
                V.tensor_copy(idx[:, :], banks[0][:, 0:BLKS])
                st.per = st.k

            @block.tensor
            def _(pe):
                pe.wait_ge(consts, 2)
                pe.wait_ge(listed, 1)
                for k in range(TOPK):
                    for q in range(2):
                        rhs = oh[:, k, q * 64:(q + 1) * 64, :].rearrange("p t e -> p (t e)")
                        nc.tensor.matmul(banks[2 * k + q][:, :], tri[:, :], rhs, start=True, stop=True).then_inc(cums, 1)
                        nc.tensor.matmul(banks[4 + 2 * k + q][:, :], ones[:, :], rhs, start=True, stop=True).then_inc(cums, 1)
                pe.wait_ge(lists, 1)
                nc.tensor.matmul(banks[0][:, 0:BLKS], zero[:, 0:P], zero[:, :], start=True, stop=False)
                with pe.Fori(0, TILES // UN) as i:
                    for n in range(UN * TOPK):
                        pe.wait_ge(lists, i * (UN * TOPK) + n + 1)
                        nc.tensor.matmul(banks[0][:, 0:BLKS], ohr[:, n, :], rb[:, n, :], start=False, stop=False).then_inc(used, 1)
                nc.tensor.matmul(banks[0][:, 0:BLKS], zero[:, 0:P], zero[:, :], start=False, stop=True).then_inc(cums, 1)


def experts(nc, x1d, yd, w1, b1, w2, b2, idx, ident, banks):
    ctx = ExitStack()
    with ctx:
        def sb(name, *shape, dt=F32):
            return ctx.enter_context(nc.sbuf_tensor(name, list(shape), dt))

        def sem(name):
            return ctx.enter_context(nc.semaphore(name))
        MT = HID // P
        BPE = CAP // (P * SPB)
        W = SPB * P
        w1s, w2s = sb("w1s", P, 2, 2, HID), sb("w2s", P, 2, MT, D)
        b2s = sb("b2s", P, 2, D)
        b1e = sb("b1_expert", P, 2, MT)
        b1r, b1t = sb("b1_rows", E * MT, P), sb("b1_cols", P, E * MT)
        icur = sb("block_index", P, 2, SPB, dt=U32)
        xg = sb("gathered_rows", P, 2, SPB, D)
        xgT = sb("gathered_T", P, 2, 2, W)
        hT = sb("hidden_T", P, 2, MT, W)
        ysb = sb("result_rows", P, 2, SPB, D)
        w_loaded, b_loaded, expert_done = sem("w_loaded"), sem("b_loaded"), sem("expert_done")
        idx_ready, xg_used = sem("idx_ready"), sem("xg_used")
        gathered = [sem(f"gathered{i}") for i in range(2)]
        xgT_ready, hT_ready, y_ready = sem("xgT_ready"), sem("hT_ready"), sem("y_ready")
        y_stored = [sem(f"y_stored{i}") for i in range(2)]
        filled, b1_ready, b1_cur, passed = sem("filled"), sem("b1_ready"), sem("b1_cur"), sem("wait_passed2")
        freed = {w: sem(f"freed_by_{w}") for w in ("act", "dve")}
        order = []
        order += [(("xT", 0, k), "dve") for k in range(2)]
        order += [(("h", 0, m), "act") for m in range(MT)]
        order += [(("xT", 1, k), "dve") for k in range(2)]
        order += [(("y", 0, t), "dve") for t in range(SPB // 2)]
        order += [(("h", 1, m), "act") for m in range(MT)]
        order += [(("y", 1, t), "dve") for t in range(SPB // 2)]
        ring = Bank(order, banks, filled, freed)

        def loop(eng, body, begin=None, end=None):
            with eng.Fori(0, E // 2) as e2:
                for par in range(2):
                    e = e2 * 2 + par
                    if begin is not None:
                        begin(e, par)
                    with eng.Fori(0, BPE // 2) as j2:
                        for j in range(2):
                            pair = e * (BPE // 2) + j2
                            body(e, par, pair, pair * 2 + j, j)
                    if end is not None:
                        end(e)

        with nc.Block() as block:
            @block.sync
            def _(sp):
                sp.dma_start(b1r[:, :], b1.rearrange("e (m p) -> (e m) p", p=P)).then_inc(b_loaded, 16)

                def body(e, par, pair, n, j):
                    sp.wait_ge(y_ready, n * 2 + 2)
                    sp.dma_start(yd.rearrange("(n i p) d -> p n i d", i=SPB, p=P)[:, bass.ds(n, 1), :, :],
                                 ysb[:, j:j + 1, :, :]).then_inc(y_stored[j], 16)
                loop(sp, body)
                for j in range(2):
                    sp.wait_ge(y_stored[j], 16 * (E * BPE // 2 + 1))

            @block.gpsimd
            def _(pool):
                def begin(e, par):
                    pool.wait_ge(expert_done, e + 1)
                    pool.dma_start(w1s[:, par:par + 1, :, :], w1[bass.ds(e, 1), :, :].rearrange("e (k p) n -> p e k n", p=P)).then_inc(w_loaded, 16)
                    pool.dma_start(w2s[:, par:par + 1, :, :], w2[bass.ds(e, 1), :, :].rearrange("e (k p) n -> p e k n", p=P)).then_inc(w_loaded, 16)
                    pool.dma_start(b2s[:, par, :], b2[bass.ds(e, 1), :].broadcast_to([P, D])).then_inc(w_loaded, 16)

                def body(e, par, pair, n, j):
                    pool.wait_ge(xg_used, n + 1)
                    pool.sem_inc(passed, 1)
                    pool.tensor_copy(icur[:, j, :], idx[:, bass.ds(n * SPB, SPB)]).then_inc(idx_ready, 1)
                    pool.wait_ge(idx_ready, n + 1)
                    pool.sem_inc(passed, 1)
                    for i in range(SPB):
                        nc.gpsimd.indirect_dma_start(out=xg[:, j, i, :], out_offset=None, in_=x1d[:, :],
                                                     in_offset=bass.IndirectOffsetOnAxis(ap=icur[:, j, i:i + 1], axis=0)).then_inc(gathered[j], 16)
                loop(pool, body, begin)

            @block.vector
            def _(dve):
                V = nc.vector
                dve.sem_inc(xg_used, 2)
                for j in range(2):
                    dve.sem_inc(y_stored[j], 16)
                dve.sem_inc(ring.freed["dve"], ring.count["dve"])

                def body(e, par, pair, n, j):
                    dve.wait_ge(w_loaded, e * 48 + 48)
                    if j == 0:
                        for q in range(2):
                            for k in range(2):
                                dve.wait_ge(filled, ring.full(pair, ("xT", q, k)))
                                V.tensor_copy(xgT[:, q, k, :], ring["xT", q, k][:, :]).then_inc(xgT_ready, 1)
                                dve.wait_ge(xgT_ready, pair * 4 + 2 * q + k + 1)
                                dve.sem_inc(ring.freed["dve"], 1)
                            dve.sem_inc(xg_used, 1)
                    dve.wait_ge(y_stored[j], pair * 16 + 16)
                    for t in range(SPB // 2):
                        dve.wait_ge(filled, ring.full(pair, ("y", j, t)))
                        V.tensor_tensor(ysb[:, j, 2 * t:2 * t + 2, :], ring["y", j, t][:, :].rearrange("p (i d) -> p i d", i=2),
                                        b2s[:, par:par + 1, :].broadcast_to([P, 2, D]), ALU.add).then_inc(y_ready, 1)
                        dve.wait_ge(y_ready, n * 2 + t + 1)
                        dve.sem_inc(ring.freed["dve"], 1)
                loop(dve, body)

            @block.scalar
            def _(act):
                act.sem_inc(ring.freed["act"], ring.count["act"])
                act.wait_ge(b1_ready, 1)
                nc.scalar.activation(b1t[:, :], banks[7][:, 0:E * MT], ACT.Copy).then_inc(b1_ready, 1)
                act.wait_ge(b1_ready, 2)

                def begin(e, par):
                    nc.scalar.activation(b1e[:, par, :], b1t[:, bass.ds(e * MT, MT)], ACT.Copy).then_inc(b1_cur, 1)

                def body(e, par, pair, n, j):
                    act.wait_ge(b1_cur, e + 1)
                    for m in range(MT):
                        act.wait_ge(filled, ring.full(pair, ("h", j, m)))
                        nc.scalar.activation(hT[:, j, m, :], ring["h", j, m][:, :], ACT.Gelu,
                                             bias=b1e[:, par, m:m + 1]).then_inc(hT_ready, 1)
                        act.wait_ge(hT_ready, n * MT + m + 1)
                        act.sem_inc(ring.freed["act"], 1)
                loop(act, body, begin)

            @block.tensor
            def _(pe):
                pe.sem_inc(expert_done, 2)
                pe.wait_ge(b_loaded, 16)
                nc.tensor.transpose(banks[7][:, 0:E * MT], b1r[:, :], ident[0:E * MT, 0:E * MT]).then_inc(b1_ready, 1)
                pe.wait_ge(b1_ready, 2)

                def turn(pair, j):
                    pe.wait_ge(gathered[j], pair * (16 * SPB) + 16 * SPB)
                    for k in range(2):
                        ps = ring.take(pe, pair, ("xT", j, k))
                        for i in range(SPB):
                            ins = nc.tensor.transpose(ps[:, i * P:(i + 1) * P], xg[:, j, i, k * P:(k + 1) * P], ident[:, :])
                        ins.then_inc(filled, 1)

                def body(e, par, pair, n, j):
                    pe.wait_ge(w_loaded, e * 48 + 48)
                    if j == 0:
                        turn(pair, 0)
                    pe.wait_ge(xgT_ready, n * 2 + 2)
                    for m in range(MT):
                        ps = ring.take(pe, pair, ("h", j, m))
                        for k in range(2):
                            ins = nc.tensor.matmul(ps[:, :], w1s[:, par, k, m * P:(m + 1) * P], xgT[:, j, k, :], start=k == 0, stop=k == 1)
                        ins.then_inc(filled, 1)
                    if j == 0:
                        turn(pair, 1)
                    for t in range(SPB // 2):
                        ps = ring.take(pe, pair, ("y", j, t))
                        for i in range(2):
                            for m in range(MT):
                                if t == 0 and i == 0:
                                    pe.wait_ge(hT_ready, n * MT + m + 1)
                                s0 = (2 * t + i) * P
                                ins = nc.tensor.matmul(ps[:, i * D:(i + 1) * D], hT[:, j, m, s0:s0 + P], w2s[:, par, m, :], start=m == 0, stop=m == MT - 1)
                        ins.then_inc(filled, 1)

                def end(e):
                    pe.wait_ge(filled, e * (BPE // 2 * len(order)) + BPE // 2 * len(order))
                    pe.sem_inc(expert_done, 1)
                loop(pe, body, end=end)


def combine(nc, x1d, yd, slot, wk, out):
    ctx = ExitStack()
    with ctx:
        def sb(name, *shape, dt=F32):
            return ctx.enter_context(nc.sbuf_tensor(name, list(shape), dt))

        def sem(name):
            return ctx.enter_context(nc.semaphore(name))
        Q = 4
        NB = 2
        xs, ys = sb("x1_rows_sb", P, NB, Q, D), sb("y_rows_sb", P, NB, Q * TOPK, D)
        o = sb("out_rows", P, NB, Q, D)
        scur = sb("turn_slots", P, NB, Q * TOPK, dt=U32)
        stats, mv, rstd = sb("stats2", P, NB, Q, 6), sb("mv2", P, NB, Q, 2), sb("rstd2", P, NB, Q)
        eps = sb("eps2", P, 1)
        x_loaded = [sem(f"x1_loaded{i}") for i in range(NB)]
        y_loaded = [sem(f"y_loaded{i}") for i in range(NB)]
        scur_ready, used, var_ready, rstd_ready = sem("scur_ready"), sem("rows_used"), sem("var_ready2"), sem("rstd_ready2")
        passed = sem("wait_passed3")
        lns, out_ready, stored, steps = sem("ln_done"), sem("out_ready"), [sem(f"out_stored{i}") for i in range(NB)], sem("combine_steps")
        TURNS = TILES // Q
        STEPS = 1 + TOPK

        def loop(eng, body):
            with eng.Fori(0, TURNS // NB) as i:
                for j in range(NB):
                    body(i * NB + j, i, j)

        rows = lambda t: t.rearrange("(q i p) d -> p q i d", p=P, i=Q)
        sl = slot[:, :, :].rearrange("p t k -> p (t k)")
        with nc.Block() as block:
            @block.sync
            def _(sp):
                def load(n, i, j):
                    sp.wait_ge(used, n + 1)
                    sp.dma_start(xs[:, j:j + 1, :, :], rows(x1d)[:, bass.ds(n, 1), :, :]).then_inc(x_loaded[j], 16)
                loop(sp, load)

            @block.gpsimd
            def _(pool):
                def body(n, i, j):
                    pool.wait_ge(used, n + 1)
                    pool.sem_inc(passed, 1)
                    pool.tensor_copy(scur[:, j, :], sl[:, bass.ds(n * (Q * TOPK), Q * TOPK)]).then_inc(scur_ready, 1)
                    pool.wait_ge(scur_ready, n + 1)
                    pool.sem_inc(passed, 1)
                    for k in range(Q * TOPK):
                        nc.gpsimd.indirect_dma_start(out=ys[:, j, k, :], out_offset=None, in_=yd[:, :],
                                                     in_offset=bass.IndirectOffsetOnAxis(ap=scur[:, j, k:k + 1], axis=0)).then_inc(y_loaded[j], 16)
                loop(pool, body)

            @block.scalar
            def _(act):
                def body(n, i, j):
                    act.wait_ge(var_ready, n + 2)
                    nc.scalar.activation(rstd[:, j, :], mv[:, j, :, 1], ACT.Ln, bias=eps[:, 0:1]).then_inc(lns, 1)
                    act.wait_ge(lns, n + 1)
                    nc.scalar.activation(rstd[:, j, :], rstd[:, j, :], ACT.Exp, scale=-0.5).then_inc(rstd_ready, 1)
                    act.wait_ge(out_ready, n + 1)
                    act.dma_start(rows(out)[:, bass.ds(n, 1), :, :], o[:, j:j + 1, :, :]).then_inc(stored[j], 16)
                loop(act, body)
                for j in range(NB):
                    act.wait_ge(stored[j], 16 * (TURNS // NB + 1))

            @block.vector
            def _(dve):
                V = nc.vector
                V.memset(eps[:, :], EPS_LN).then_inc(var_ready, 1)
                dve.sem_inc(used, NB)
                for j in range(NB):
                    dve.sem_inc(stored[j], 16)
                dve.wait_ge(var_ready, 1)

                def body(n, i, j):
                    dve.wait_ge(x_loaded[j], i * 16 + 16)
                    dve.wait_ge(y_loaded[j], i * (16 * Q * TOPK) + 16 * Q * TOPK)
                    dve.wait_ge(stored[j], i * 16 + 16)
                    for k in range(TOPK):
                        for q in range(Q):
                            ins = V.scalar_tensor_tensor(o[:, j, q, :], ys[:, j, q * TOPK + k, :], wk[:, k, bass.ds(n * Q + q, 1)],
                                                         xs[:, j, q, :] if k == 0 else o[:, j, q, :], ALU.mult, ALU.add)
                        ins.then_inc(steps, 1)
                        dve.wait_ge(steps, n * STEPS + k + 1)
                    dve.sem_inc(used, 1)
                    for q in range(Q):
                        ins = V.bn_stats(stats[:, j, q, :], o[:, j, q, :])
                    ins.then_inc(steps, 1)
                    dve.wait_ge(steps, n * STEPS + TOPK + 1)
                    dve.sem_inc(passed, 1)
                    for q in range(Q):
                        ins = V.bn_aggr(mv[:, j, q, :], stats[:, j, q, :])
                    ins.then_inc(var_ready, 1)
                    dve.wait_ge(rstd_ready, n + 1)
                    dve.wait_ge(var_ready, n + 2)
                    for q in range(Q):
                        ins = V.tensor_scalar(o[:, j, q, :], o[:, j, q, :], mv[:, j, q, 0:1], rstd[:, j, q:q + 1], ALU.subtract, ALU.mult)
                    ins.then_inc(out_ready, 1)
                loop(dve, body)


_INS = ["L0_attn_hidden", "L0_attn_p20_decay_log", "L0_attn_p20_theta", "L0_attn_ctrl_W", "L0_attn_ctrl_b",
        "L0_attn_p20c_W", "L0_attn_qconv_w", "L0_attn_kconv_w", "L0_attn_vconv_w", "L0_attn_mnorm_scale",
        "L0_attn_vnorm_scale", "L0_attn_ramp_logit", "L0_attn_out_W", "L0_attn_out_b", "L0_ffn_wg",
        "L0_ffn_w1", "L0_ffn_b1", "L0_ffn_w2", "L0_ffn_b2"]


def kernel(**inputs):
    import numpy as _np
    import concourse.bacc as _bacc
    from concourse import mybir as _mybir
    from concourse.bass_utils import run_bass_kernel_spmd as _run

    nc = _bacc.Bacc("TRN2", target_bir_lowering=False, num_devices=1)
    arrays, args = {}, []
    for name in _INS:
        a = _np.ascontiguousarray(inputs[name])
        arrays[name] = a
        args.append(nc.dram_tensor(name, a.shape, _mybir.dt.from_np(a.dtype), kind="ExternalInput").ap())
    out = nc.dram_tensor("out", (B, S, D), F32, kind="ExternalOutput").ap()
    build(nc, *args, out)
    r = _run(nc, [arrays], core_ids=[0])
    return r.results[0]["out"]
```
